# Optimizing a Trainium2 kernel written in Bass

```python
import numpy as np
import jax
import jax.numpy as jnp

def _softmax(x, axis=-1):
    return jax.nn.softmax(x, axis=axis)

def _gelu(x):
    return jax.nn.gelu(x, approximate=True)

def _silu(x):
    return jax.nn.silu(x)

def _sigmoid(x):
    return jax.nn.sigmoid(x)

def _layernorm(x, axis=-1, eps=1e-05):
    m = jnp.mean(x, axis=axis, keepdims=True)
    v = jnp.var(x, axis=axis, keepdims=True)
    return (x - m) / jnp.sqrt(v + eps)

def _scatter_add(tgt, idx, src, axis=0):
    return tgt.at[idx].add(src)

def _segment_sum(src, seg, n):
    return jax.ops.segment_sum(src, seg, n)
kernel_name = 'mk_macaron_d2_jaxref_r8_a08d59'

def setup_inputs(seed: int=0):
    np.random.seed(seed)
    _w = jnp.asarray

    def _L0_attn_setup():
        import jax, jax.numpy as jnp
        from jax import lax
        import numpy as np
        EPS = 1e-05

        def _rms(v, w):
            return v * lax.rsqrt(jnp.mean(v * v, axis=-1, keepdims=True) + EPS) * w

        def _selective_scan(u, delta, A, Bm, Cm, D, gate):
            Bsz, I, L = u.shape
            N = A.shape[1]

            def step(s, inp):
                u_t, d_t, B_t, C_t = inp
                dA = jnp.exp(d_t[..., None] * A)
                dBu = d_t[..., None] * B_t[:, None, :] * u_t[..., None]
                s = dA * s + dBu
                y = jnp.einsum('bin,bn->bi', s, C_t)
                return (s, y)
            xs = (u.transpose(2, 0, 1), delta.transpose(2, 0, 1), Bm.transpose(1, 0, 2), Cm.transpose(1, 0, 2))
            s0 = jnp.zeros((Bsz, I, N), u.dtype)
            _, ys = lax.scan(step, s0, xs)
            y = ys.transpose(1, 2, 0) + D[:, None] * u
            return y * jax.nn.silu(gate)
        key = jax.random.key(seed)
        ks = jax.random.split(key, 13)
        H, I, N, K, R = (256, 512, 16, 4, 128)
        B, L = (2, 256)
        sc = lambda d: 1.0 / np.sqrt(d)
        return {'x': jax.random.normal(ks[0], (B, L, H), jnp.float32), 'W_in': jax.random.normal(ks[1], (2 * I, H), jnp.float32) * sc(H), 'conv_w': jax.random.normal(ks[2], (I, K), jnp.float32) * sc(K), 'conv_b': jax.random.normal(ks[3], (I,), jnp.float32) * 0.01, 'Wx': jax.random.normal(ks[4], (R + 2 * N, I), jnp.float32) * sc(I), 'dt_ln_w': jnp.ones((R,), jnp.float32), 'b_ln_w': jnp.ones((N,), jnp.float32), 'c_ln_w': jnp.ones((N,), jnp.float32), 'Wdt': jax.random.normal(ks[5], (I, R), jnp.float32) * sc(R), 'dt_bias': jax.random.normal(ks[6], (I,), jnp.float32) * 0.1 - 4.0, 'A': -jax.random.uniform(ks[7], (I, N), jnp.float32, 0.5, 16.0), 'D': jnp.ones((I,), jnp.float32), 'Wout': jax.random.normal(ks[8], (H, I), jnp.float32) * sc(I)}
    _L0_attn_in = _L0_attn_setup()

    def _L0_ffn_setup():
        import jax, jax.numpy as jnp
        import numpy as np
        from jax import lax
        H = 256
        I = 176
        E = 16
        TOP_K = 6
        IS = 2 * I

        def _swiglu(x, w13_, w2_):
            gu = x @ w13_.T
            g, u = jnp.split(gu, 2, axis=-1)
            return jax.nn.silu(g) * u @ w2_.T
        key = jax.random.key(seed)
        ks = jax.random.split(key, 6)
        return {'hidden_states': jax.random.normal(ks[0], (1, 256, H), jnp.float32), 'gate_w': jax.random.normal(ks[1], (E, H), jnp.float32) * 0.02, 'w13': jax.random.normal(ks[2], (E, 2 * I, H), jnp.float32) * 0.02, 'w2': jax.random.normal(ks[3], (E, H, I), jnp.float32) * 0.02, 'sw13': jax.random.normal(ks[4], (2 * IS, H), jnp.float32) * 0.02, 'sw2': jax.random.normal(ks[5], (H, IS), jnp.float32) * 0.02}
    _L0_ffn_in = _L0_ffn_setup()

    def _L1_attn_setup():
        import math
        import jax, jax.numpy as jnp
        import numpy as np
        NUM_HEAD = 16
        EMB = 256
        HEAD_DIM = EMB // NUM_HEAD
        B, T = (2, 256)

        def get_slopes(n):
            start = 2 ** (-2 ** (-(math.log2(n) - 3)))
            return np.array([start * start ** i for i in range(n)], dtype=np.float32)
        key = jax.random.key(seed)
        ks = jax.random.split(key, 5)
        x = jax.random.normal(ks[0], (B, T, EMB), jnp.float32)

        def w(k, scale=0.02):
            return jax.random.normal(k, (EMB, EMB), jnp.float32) * scale
        return {'x': x, 'Wq': w(ks[1]), 'bq': jnp.zeros((EMB,), jnp.float32), 'Wk': w(ks[2]), 'bk': jnp.zeros((EMB,), jnp.float32), 'Wv': w(ks[3]), 'bv': jnp.zeros((EMB,), jnp.float32), 'Wo': w(ks[4], scale=0.02 / math.sqrt(24)), 'bo': jnp.zeros((EMB,), jnp.float32)}
    _L1_attn_in = _L1_attn_setup()

    def _L1_ffn_setup():
        import jax, jax.numpy as jnp
        import numpy as np
        HIDDEN = 256
        INTER = 1024
        SCALE = 64.0

        def fwht(x):
            orig_shape = x.shape
            n = orig_shape[-1]
            x = x.reshape(-1, n)
            h = 1
            while h < n:
                x = x.reshape(-1, n // (2 * h), 2, h)
                a, b = (x[:, :, 0, :], x[:, :, 1, :])
                x = jnp.stack([a + b, a - b], axis=2).reshape(-1, n)
                h *= 2
            return (x / jnp.sqrt(jnp.asarray(n, x.dtype))).reshape(orig_shape)
        key = jax.random.key(seed)
        ks = jax.random.split(key, 8)
        inp = jax.random.normal(ks[0], (4, 256, HIDDEN), dtype=jnp.float32)
        SU_ug = jnp.where(jax.random.bernoulli(ks[1], 0.5, (HIDDEN,)), 1.0, -1.0).astype(jnp.float32)
        SU_dp = jnp.where(jax.random.bernoulli(ks[2], 0.5, (INTER,)), 1.0, -1.0).astype(jnp.float32)
        Wscale_ug = jax.random.uniform(ks[3], (2 * INTER,), jnp.float32, 0.5, 1.5)
        Wscale_dp = jax.random.uniform(ks[4], (HIDDEN,), jnp.float32, 0.5, 1.5)
        W_up = jax.random.normal(ks[5], (INTER, HIDDEN), dtype=jnp.float32) * 0.02
        W_gate = jax.random.normal(ks[6], (INTER, HIDDEN), dtype=jnp.float32) * 0.02
        W_down = jax.random.normal(ks[7], (HIDDEN, INTER), dtype=jnp.float32) * 0.02
        return {'input': inp, 'SU_ug': SU_ug, 'SU_dp': SU_dp, 'Wscale_ug': Wscale_ug, 'Wscale_dp': Wscale_dp, 'W_up': W_up, 'W_gate': W_gate, 'W_down': W_down}
    _L1_ffn_in = _L1_ffn_setup()
    _d = {'L0_attn_x': _L0_attn_in['x'], 'L0_attn_W_in': _L0_attn_in['W_in'], 'L0_attn_conv_w': _L0_attn_in['conv_w'], 'L0_attn_conv_b': _L0_attn_in['conv_b'], 'L0_attn_Wx': _L0_attn_in['Wx'], 'L0_attn_dt_ln_w': _L0_attn_in['dt_ln_w'], 'L0_attn_b_ln_w': _L0_attn_in['b_ln_w'], 'L0_attn_c_ln_w': _L0_attn_in['c_ln_w'], 'L0_attn_Wdt': _L0_attn_in['Wdt'], 'L0_attn_dt_bias': _L0_attn_in['dt_bias'], 'L0_attn_A': _L0_attn_in['A'], 'L0_attn_D': _L0_attn_in['D'], 'L0_attn_Wout': _L0_attn_in['Wout'], 'L0_ffn_gate_w': _L0_ffn_in['gate_w'], 'L0_ffn_w13': _L0_ffn_in['w13'], 'L0_ffn_w2': _L0_ffn_in['w2'], 'L0_ffn_sw13': _L0_ffn_in['sw13'], 'L0_ffn_sw2': _L0_ffn_in['sw2'], 'L1_attn_Wq': _L1_attn_in['Wq'], 'L1_attn_bq': _L1_attn_in['bq'], 'L1_attn_Wk': _L1_attn_in['Wk'], 'L1_attn_bk': _L1_attn_in['bk'], 'L1_attn_Wv': _L1_attn_in['Wv'], 'L1_attn_bv': _L1_attn_in['bv'], 'L1_attn_Wo': _L1_attn_in['Wo'], 'L1_attn_bo': _L1_attn_in['bo'], 'L1_ffn_SU_ug': _L1_ffn_in['SU_ug'], 'L1_ffn_SU_dp': _L1_ffn_in['SU_dp'], 'L1_ffn_Wscale_ug': _L1_ffn_in['Wscale_ug'], 'L1_ffn_Wscale_dp': _L1_ffn_in['Wscale_dp'], 'L1_ffn_W_up': _L1_ffn_in['W_up'], 'L1_ffn_W_gate': _L1_ffn_in['W_gate'], 'L1_ffn_W_down': _L1_ffn_in['W_down']}
    _x0 = _d['L0_attn_x']
    _d['L0_attn_x'] = jax.random.normal(jax.random.fold_in(jax.random.key(seed), 1), (8, 256, 256), dtype=_x0.dtype)
    del _x0
    return _d

def reference(L0_attn_x, L0_attn_W_in, L0_attn_conv_w, L0_attn_conv_b, L0_attn_Wx, L0_attn_dt_ln_w, L0_attn_b_ln_w, L0_attn_c_ln_w, L0_attn_Wdt, L0_attn_dt_bias, L0_attn_A, L0_attn_D, L0_attn_Wout, L0_ffn_gate_w, L0_ffn_w13, L0_ffn_w2, L0_ffn_sw13, L0_ffn_sw2, L1_attn_Wq, L1_attn_bq, L1_attn_Wk, L1_attn_bk, L1_attn_Wv, L1_attn_bv, L1_attn_Wo, L1_attn_bo, L1_ffn_SU_ug, L1_ffn_SU_dp, L1_ffn_Wscale_ug, L1_ffn_Wscale_dp, L1_ffn_W_up, L1_ffn_W_gate, L1_ffn_W_down):

    def _L0_attn_ref(x, W_in, conv_w, conv_b, Wx, dt_ln_w, b_ln_w, c_ln_w, Wdt, dt_bias, A, D, Wout):
        import jax, jax.numpy as jnp
        from jax import lax
        import numpy as np
        EPS = 1e-05

        def _rms(v, w):
            return v * lax.rsqrt(jnp.mean(v * v, axis=-1, keepdims=True) + EPS) * w

        def _selective_scan(u, delta, A, Bm, Cm, D, gate):
            Bsz, I, L = u.shape
            N = A.shape[1]

            def step(s, inp):
                u_t, d_t, B_t, C_t = inp
                dA = jnp.exp(d_t[..., None] * A)
                dBu = d_t[..., None] * B_t[:, None, :] * u_t[..., None]
                s = dA * s + dBu
                y = jnp.einsum('bin,bn->bi', s, C_t)
                return (s, y)
            xs = (u.transpose(2, 0, 1), delta.transpose(2, 0, 1), Bm.transpose(1, 0, 2), Cm.transpose(1, 0, 2))
            s0 = jnp.zeros((Bsz, I, N), u.dtype)
            _, ys = lax.scan(step, s0, xs)
            y = ys.transpose(1, 2, 0) + D[:, None] * u
            return y * jax.nn.silu(gate)
        proj = jnp.einsum('blh,oh->bol', x, W_in)
        h, gate = jnp.split(proj, 2, axis=1)
        I = h.shape[1]
        K = conv_w.shape[1]
        conv = lax.conv_general_dilated(h, conv_w[:, None, :], window_strides=(1,), padding=[(K - 1, 0)], dimension_numbers=('NCH', 'OIH', 'NCH'), feature_group_count=I)
        h = jax.nn.silu(conv + conv_b[None, :, None])
        ssm_p = jnp.einsum('bil,oi->blo', h, Wx)
        R = Wdt.shape[1]
        N = A.shape[1]
        ts, Bm, Cm = jnp.split(ssm_p, [R, R + N], axis=-1)
        ts = _rms(ts, dt_ln_w)
        Bm = _rms(Bm, b_ln_w)
        Cm = _rms(Cm, c_ln_w)
        dt = jnp.einsum('blr,ir->bil', ts, Wdt)
        delta = jax.nn.softplus(dt + dt_bias[None, :, None])
        y = _selective_scan(h, delta, A, Bm, Cm, D, gate)
        return jnp.einsum('bil,hi->blh', y, Wout)

    def _L0_ffn_ref(hidden_states, gate_w, w13, w2, sw13, sw2):
        import jax, jax.numpy as jnp
        import numpy as np
        from jax import lax
        H = 256
        I = 176
        E = 16
        TOP_K = 6
        IS = 2 * I

        def _swiglu(x, w13_, w2_):
            gu = x @ w13_.T
            g, u = jnp.split(gu, 2, axis=-1)
            return jax.nn.silu(g) * u @ w2_.T
        B, S, Hd = hidden_states.shape
        x = hidden_states.reshape(-1, Hd)
        T = x.shape[0]
        scores = jax.nn.softmax(x @ gate_w.T, axis=-1)
        topk_w, topk_ids = lax.top_k(scores, TOP_K)
        topk_w = topk_w / (topk_w.sum(-1, keepdims=True) + 1e-20)
        combine = jnp.einsum('tk,tke->te', topk_w, jax.nn.one_hot(topk_ids, E, dtype=topk_w.dtype))

        def body(acc, ew):
            w13_e, w2_e, c_e = ew
            y = _swiglu(x, w13_e, w2_e)
            return (acc + c_e[:, None] * y, None)
        out, _ = lax.scan(body, jnp.zeros_like(x), (w13, w2, combine.T))
        out = out + _swiglu(x, sw13, sw2)
        return out.reshape(B, S, Hd)

    def _L1_attn_ref(x, Wq, bq, Wk, bk, Wv, bv, Wo, bo):
        import math
        import jax, jax.numpy as jnp
        import numpy as np
        NUM_HEAD = 16
        EMB = 256
        HEAD_DIM = EMB // NUM_HEAD
        B, T = (2, 256)

        def get_slopes(n):
            start = 2 ** (-2 ** (-(math.log2(n) - 3)))
            return np.array([start * start ** i for i in range(n)], dtype=np.float32)
        Bx, Tx, C = x.shape
        slopes = jnp.asarray(get_slopes(NUM_HEAD))

        def split_heads(y):
            return y.reshape(Bx, Tx, NUM_HEAD, HEAD_DIM).transpose(0, 2, 1, 3)
        q = split_heads(x @ Wq + bq)
        k = split_heads(x @ Wk + bk)
        v = split_heads(x @ Wv + bv)
        attn = jnp.einsum('bhqd,bhkd->bhqk', q, k) / jnp.sqrt(jnp.float32(HEAD_DIM))
        alibi = -slopes[:, None, None] * (Tx - 1 - jnp.arange(Tx, dtype=jnp.float32))[None, None, :]
        attn = attn + alibi
        causal = jnp.tril(jnp.ones((Tx, Tx), dtype=bool))[None, None]
        attn = jnp.where(causal, attn, jnp.finfo(jnp.float32).min)
        p = jax.nn.softmax(attn, axis=-1)
        out = jnp.einsum('bhqk,bhkd->bhqd', p, v).transpose(0, 2, 1, 3).reshape(Bx, Tx, C)
        return out @ Wo + bo

    def _L1_ffn_ref(input, SU_ug, SU_dp, Wscale_ug, Wscale_dp, W_up, W_gate, W_down):
        import jax, jax.numpy as jnp
        import numpy as np
        HIDDEN = 256
        INTER = 1024
        SCALE = 64.0

        def fwht(x):
            orig_shape = x.shape
            n = orig_shape[-1]
            x = x.reshape(-1, n)
            h = 1
            while h < n:
                x = x.reshape(-1, n // (2 * h), 2, h)
                a, b = (x[:, :, 0, :], x[:, :, 1, :])
                x = jnp.stack([a + b, a - b], axis=2).reshape(-1, n)
                h *= 2
            return (x / jnp.sqrt(jnp.asarray(n, x.dtype))).reshape(orig_shape)
        n = SU_ug.shape[0]
        x = input.reshape(-1, n)
        x = fwht(x * SU_ug) / SCALE
        x_up = x @ W_up.T * (Wscale_ug[:INTER] * SCALE)
        x_gate = x @ W_gate.T * (Wscale_ug[INTER:] * SCALE)
        x = jax.nn.silu(x_gate) * x_up
        x = fwht(x * SU_dp) / SCALE
        x = x @ W_down.T * (Wscale_dp * SCALE)
        return x.reshape(input.shape)
    x = L0_attn_x
    x = x + 0.5 * _L0_ffn_ref(_layernorm(x, axis=-1), L0_ffn_gate_w, L0_ffn_w13, L0_ffn_w2, L0_ffn_sw13, L0_ffn_sw2)
    x = x + _L0_attn_ref(_layernorm(x, axis=-1), L0_attn_W_in, L0_attn_conv_w, L0_attn_conv_b, L0_attn_Wx, L0_attn_dt_ln_w, L0_attn_b_ln_w, L0_attn_c_ln_w, L0_attn_Wdt, L0_attn_dt_bias, L0_attn_A, L0_attn_D, L0_attn_Wout)
    x = x + 0.5 * _L0_ffn_ref(_layernorm(x, axis=-1), L0_ffn_gate_w, L0_ffn_w13, L0_ffn_w2, L0_ffn_sw13, L0_ffn_sw2)
    x = x + 0.5 * _L1_ffn_ref(_layernorm(x, axis=-1), L1_ffn_SU_ug, L1_ffn_SU_dp, L1_ffn_Wscale_ug, L1_ffn_Wscale_dp, L1_ffn_W_up, L1_ffn_W_gate, L1_ffn_W_down)
    x = x + _L1_attn_ref(_layernorm(x, axis=-1), L1_attn_Wq, L1_attn_bq, L1_attn_Wk, L1_attn_bk, L1_attn_Wv, L1_attn_bv, L1_attn_Wo, L1_attn_bo)
    x = x + 0.5 * _L1_ffn_ref(_layernorm(x, axis=-1), L1_ffn_SU_ug, L1_ffn_SU_dp, L1_ffn_Wscale_ug, L1_ffn_Wscale_dp, L1_ffn_W_up, L1_ffn_W_gate, L1_ffn_W_down)
    return x

_drawn_inputs = setup_inputs


def setup_inputs(seed=0):
    import zlib

    import numpy as np

    out = dict(_drawn_inputs(seed))
    spreads = {'L0_attn_dt_ln_w': (1.0, 0.6),
     'L0_attn_b_ln_w': (1.0, 0.6),
     'L0_attn_c_ln_w': (1.0, 0.6),
     'L0_attn_D': (1.0, 0.2),
     'L1_attn_bq': (0.0, 0.8),
     'L1_attn_bk': (0.0, 2.0),
     'L1_attn_bv': (0.0, 0.8),
     'L1_attn_bo': (0.0, 0.468)}
    factors = {'L0_attn_conv_b': 8.0,
     'L0_attn_dt_bias': 38.328,
     'L0_ffn_gate_w': 8.0,
     'L0_ffn_w13': 8.0,
     'L0_ffn_w2': 8.0,
     'L0_ffn_sw13': 3.095,
     'L0_ffn_sw2': 3.094,
     'L1_attn_Wq': 8.0,
     'L1_attn_Wk': 8.0,
     'L1_attn_Wv': 8.0,
     'L1_attn_Wo': 6.83,
     'L1_ffn_Wscale_ug': 4.45,
     'L1_ffn_Wscale_dp': 6.184,
     'L0_attn_Wx': 8.0,
     'L0_attn_Wdt': 8.0,
     'L0_attn_A': 8.0}
    for name, (base, spread) in spreads.items():
        noise = np.random.default_rng([zlib.crc32(name.encode()), seed]).standard_normal(out[name].shape)
        drawn = base * np.exp(spread * noise) if base else spread * noise
        out[name] = jnp.asarray(drawn.astype(out[name].dtype))
    for name, factor in factors.items():
        out[name] = (out[name] * factor).astype(out[name].dtype)
    return out
```

```python
from contextlib import ExitStack

import numpy as np

import concourse.bass as bass
from concourse import mybir

F32 = mybir.dt.float32
F32R = mybir.dt.float32r
ALU = mybir.AluOpType
ACT = mybir.ActivationFunctionType
AX_X = mybir.AxisListType.X

P = 128
BATCH, SEQ, HID = 8, 256, 256
TOK = BATCH * SEQ
TILES = TOK // P
CHUNK = 512
NCH = TOK // CHUNK
KB = HID // P
EPS = 1e-5

NEXP, TOPK, EINT = 16, 6, 176
FEAT = NEXP * EINT + 2 * EINT
MOE_TILES = -(-FEAT // P)
MOE_G = 5
ONES_ROW = NEXP
INTER = 1024
FFN_TILES = INTER // P
IN, NST, KCONV, RANK = 512, 16, 4, 128
IB = IN // P
XP = RANK + 2 * NST
HEADS, HD = 16, 16
HSLOT = 32
HGRP = P // HSLOT
NGRP = HEADS // HGRP
MASKED = -1e30


class Sem:

    def __init__(self, k, name, per=0, credit=0, passes=0, total=0):
        self.per, key = per, k.kind + name
        if key in k.used:
            self.sem, self.base = k.used[key]
        else:
            self.sem, self.base = k.ctx.enter_context(k.nc.semaphore(key)), credit
            if credit:
                k.credits.append(self)
        k.used[key] = self.sem, self.base + (total or passes * per)

    def wait(self, eng, count, it=0):
        v = it * self.per + (count + self.base)
        if isinstance(v, int) and v <= 0:
            return
        eng.wait_ge(self.sem, v)

    def __rmatmul__(self, ins):
        ins.then_inc(self.sem, 1)
        return ins


class Kern:

    def __init__(self, nc, ctx):
        self.nc, self.ctx, self.kind, self.credits, self.used = nc, ctx, "", [], {}
        self.base = 20480
        self.psum = ctx.enter_context(nc.psum_tensor("psum", [P, 8, 512], F32))
        self.X = self.keep("X", [P, TILES, HID])
        self.xH = self.keep("xnT_hi", [P, KB, TOK], F32R)
        self.xL = self.keep("xnT_lo", [P, KB, TOK], F32R)
        self.acc_at = self.base
        self.accT = self.keep("accT", [P, KB, TOK])
        self.gate = self.keep("gate_table", [64, TOK], F32R)
        self.ident = self.keep("ident", [P, P])
        self.xst = self.keep("x_stage", [P, 2, HID])
        self.st6 = self.keep("bn6", [P, 2, 6])
        self.mv = self.keep("mean_var", [P, 2, 2])
        self.rs = self.keep("rstd", [P, 2])
        self.half = self.keep("minus_half", [P, 16])
        self.gw = self.keep("gate_w_raw", [P, KB, NEXP])
        self.gwH = self.keep("gate_w_hi", [P, KB, NEXP], F32R)
        self.gwL = self.keep("gate_w_lo", [P, KB, NEXP], F32R)
        self.lgT = self.keep("logitsT", [NEXP, CHUNK])
        self.lg = self.keep("logits", [P, 4, NEXP])
        self.ex = self.keep("exps", [P, 4, NEXP])
        self.mx = self.keep("top8", [P, 4, 8])
        self.rest = self.keep("not_chosen", [P, 4, NEXP])
        self.red = self.keep("row_stats", [P, 4])
        self.red2 = self.keep("row_stats2", [P, 4])
        self.s_const = Sem(self, "const")
        self.s_init = Sem(self, "init")
        self.s_half = Sem(self, "half")
        self.s_own = Sem(self, "own")
        self.arena = self.base

    def own(self, e):
        e.sem_inc(self.s_own.sem, 1)

    def at(self, name, shape, dt, off):
        return self.nc.alloc_sbuf_tensor_at(name, list(shape), dt, offset=off)

    def keep(self, name, shape, dt=F32):
        t = self.at(name, shape, dt, self.base)
        self.base += -(-4 * int(np.prod(shape[1:])) // 32) * 32
        return t


class Arena:

    def __init__(self, k, tag):
        self.k, self.tag, self.off = k, tag, k.arena

    def new(self, name, shape, dt=F32, over=None):
        off = self.off if over is None else over
        t = self.k.at(self.tag + name, shape, dt, off)
        end = off + -(-4 * int(np.prod(shape[1:])) // 32) * 32
        if over is None:
            self.off = end
        return t


def three(e, out, wH, wL, xH, xL, start, stop):
    e.matmul(out, wH, xH, start=start, stop=False)
    e.matmul(out, wH, xL, start=False, stop=False)
    return e.matmul(out, wL, xH, start=False, stop=stop)


class Tail:

    def __init__(self, k, tag, entry=False, last=False, route=False):
        self.k, self.entry, self.last, self.route = k, entry, last, route
        k.kind = "tail_"
        self.src_ready = None
        self.src = None
        if not entry:
            self.s_back = Sem(k, "back", 2, passes=NCH)
            self.s_add = Sem(k, "add", 2, credit=1, passes=NCH)
        if last:
            self.s_store = Sem(k, "store")
            return
        self.s_st = Sem(k, "bnst", 4, passes=NCH)
        self.s_ag = Sem(k, "bnag", 4, passes=NCH)
        self.s_ve = Sem(k, "vareps", 2, passes=NCH)
        self.s_rs = Sem(k, "rstd", 2, passes=NCH)
        self.s_xs = Sem(k, "xs", 2, passes=NCH)
        self.s_fw = Sem(k, "fw", 2, passes=NCH)
        self.s_xH = Sem(k, "xH", 2, credit=1, passes=NCH)
        self.s_xL = Sem(k, "xL", 2, credit=1, passes=NCH)
        if entry:
            self.s_in = [Sem(k, f"in{c}") for c in range(NCH)]
        if route:
            self.r_lgT = Sem(k, "r_lgT", 1, passes=NCH)
            self.r_lgTs = Sem(k, "r_lgTs", 1, passes=NCH)
            self.r_lg = Sem(k, "r_lg", 1, passes=NCH)
            self.r_v = Sem(k, "r_v", 16, passes=NCH)
            self.r_ex = Sem(k, "r_ex", 1, passes=NCH)
            self.r_cT = Sem(k, "r_cT", 1, passes=NCH)
            self.r_cH = Sem(k, "r_cH", 1, credit=1, passes=NCH)
            self.r_cL = Sem(k, "r_cL", 1, credit=1, passes=NCH)

    def bank(self):
        return self.k.psum[:, 7, :]

    def ready(self, e, c):
        self.s_xH.wait(e, 2, c)
        self.s_xL.wait(e, 2, c)
        if self.route:
            self.r_cH.wait(e, 1, c)
            self.r_cL.wait(e, 1, c)

    def idle(self, e, c):
        if self.last:
            return self.s_add.wait(e, 0, c)
        self.s_xH.wait(e, 0, c)
        self.s_xL.wait(e, 0, c)
        if self.route:
            self.r_cH.wait(e, 0, c)
            self.r_cL.wait(e, 0, c)

    def pe(self, e, c, slot):
        k, ptr, p = self.k, self.bank(), slot // 2
        if slot in (0, 2) and not self.entry:
            if slot == 0:
                self.src_ready.wait(e, 1, c)
            elif not self.last:
                self.s_xL.wait(e, 1, c)
            else:
                self.s_add.wait(e, 1, c)
            src = self.src(c)
            for j in range(2):
                for kb in range(KB):
                    m = e.transpose(ptr[:, j * 256 + kb * P:j * 256 + kb * P + P],
                                    src[:, kb, (2 * p + j) * P:(2 * p + j + 1) * P], k.ident[:])
            m @ self.s_back
        if slot in (1, 3) and not self.last:
            self.s_xs.wait(e, p + 1, c)
            for j in range(2):
                for kb in range(KB):
                    m = e.transpose(ptr[:, kb * 256 + j * P:kb * 256 + j * P + P],
                                    k.xst[:, j, kb * P:(kb + 1) * P], k.ident[:])
            m @ self.s_fw
        if slot == 4:
            self.s_xH.wait(e, 2, c)
            self.s_xL.wait(e, 2, c)
            k.own(e)
            n = 0
            for kb in range(KB):
                for w in (k.gwH, k.gwL):
                    for x in (k.xH, k.xL):
                        n += 1
                        m = e.matmul(ptr[0:NEXP, :], w[:, kb, :], x[:, kb, bass.ds(c * CHUNK, CHUNK)],
                                     start=(n == 1), stop=(n == 4 * KB))
            m @ self.r_lgT
        if slot == 5:
            self.r_lgTs.wait(e, 1, c)
            k.own(e)
            for j in range(4):
                m = e.transpose(ptr[:, j * NEXP:(j + 1) * NEXP], k.lgT[:, j * P:(j + 1) * P],
                                k.ident[0:NEXP, 0:NEXP])
            m @ self.r_lg
        if slot == 6:
            self.r_v.wait(e, 16, c)
            for j in range(4):
                m = e.transpose(ptr[0:NEXP, j * P:(j + 1) * P], k.lg[:, j, :], k.ident[:])
            m @ self.r_cT

    def act(self, e, c, slot):
        k, ptr, p = self.k, self.bank(), slot // 2
        if slot in (1, 3) and not self.last:
            self.s_fw.wait(e, p + 1, c)
            e.activation(k.xH[:, :, bass.ds(c * CHUNK + p * 256, 256)],
                         ptr.rearrange("p (k t) -> p k t", k=KB), ACT.Copy) @ self.s_xH
        if slot == 4:
            self.r_lgT.wait(e, 1, c)
            e.activation(k.lgT[:], ptr[0:NEXP, :], ACT.Copy) @ self.r_lgTs
        if slot == 5:
            self.r_v.wait(e, 2, c)
            e.activation(k.ex[:], k.lg[:], ACT.Exp) @ self.r_ex
        if slot == 6:
            self.r_cT.wait(e, 1, c)
            e.activation(k.gate[0:NEXP, bass.ds(c * CHUNK, CHUNK)], ptr[0:NEXP, :], ACT.Copy) @ self.r_cH

    def sync(self, e):
        for c in range(NCH):
            self.s_add.wait(e, 2, c)
            e.dma_start(self.out[c * CHUNK:(c + 1) * CHUNK, :].rearrange("(n p) f -> p n f", p=P),
                        self.k.X[:, 4 * c:4 * c + 4, :]).then_inc(self.s_store.sem, 16)
        e.wait_ge(self.s_store.sem, 16 * NCH)

    def pool(self, e, c, slot):
        if slot in (0, 2) and not self.last:
            k, p = self.k, slot // 2
            self.s_ag.wait(e, 2 * p + 2, c)
            k.own(e)
            e.tensor_scalar(k.rs[:], k.mv[:, :, 1], EPS, None, ALU.add) @ self.s_ve
            self.s_ve.wait(e, p + 1, c)
            e.tensor_tensor(k.rs[:], k.rs[:], k.half[:, 0:2], ALU.pow) @ self.s_rs

    def dve(self, e, c, slot):
        k, ptr, p = self.k, self.bank(), slot // 2
        if slot in (0, 2):
            rows = k.X[:, bass.ds(c * 4 + 2 * p, 2), :]
            if self.entry:
                self.s_in[c].wait(e, 16)
            else:
                self.s_back.wait(e, p + 1, c)
                e.tensor_tensor(rows, rows, ptr.rearrange("p (j f) -> p j f", j=2), ALU.add) @ self.s_add
                self.s_add.wait(e, p + 1, c)
            if self.last:
                return
            for j in range(2):
                if j == 0:
                    k.own(e)
                e.bn_stats(k.st6[:, j, :], k.X[:, c * 4 + 2 * p + j, :]) @ self.s_st
            for j in range(2):
                self.s_st.wait(e, 2 * p + j + 1, c)
                k.own(e)
                e.bn_aggr(k.mv[:, j, :], k.st6[:, j, :]) @ self.s_ag
            self.s_rs.wait(e, p + 1, c)
            for j in range(2):
                m = e.tensor_scalar(k.xst[:, j, :], k.X[:, c * 4 + 2 * p + j, :], k.mv[:, j, 0:1],
                                    k.rs[:, j:j + 1], ALU.subtract, ALU.mult)
            m @ self.s_xs
        if slot in (1, 3) and not self.last:
            self.s_xH.wait(e, p + 1, c)
            cols = bass.ds(c * CHUNK + p * 256, 256)
            e.tensor_tensor(k.xL[:, :, cols], ptr.rearrange("p (k t) -> p k t", k=KB),
                            k.xH[:, :, cols].bitcast(F32), ALU.subtract) @ self.s_xL
        if slot == 5:
            n = [0]

            def step(ins):
                ins @ self.r_v
                n[0] += 1
                self.r_v.wait(e, n[0], c)

            def over(x):
                return x[:].unsqueeze(2).broadcast_to([P, 4, NEXP])

            self.r_lg.wait(e, 1, c)
            logits = ptr[:, 0:4 * NEXP].rearrange("p (j x) -> p j x", j=4)
            step(e.tensor_reduce(k.red[:], logits, AX_X, ALU.max))
            step(e.tensor_tensor(k.lg[:], logits, over(k.red), ALU.subtract))
            self.r_ex.wait(e, 1, c)
            for j in range(4):
                k.own(e)
                step(e.max(k.mx[:, j, :], k.ex[:, j, :]))
            step(e.memset(k.mx[:, :, TOPK:8], -1.0))
            for j in range(4):
                k.own(e)
                e.match_replace(k.rest[:, j, :], k.mx[:, j, :], k.ex[:, j, :], 0.0) @ self.r_v
            n[0] = 11
            self.r_v.wait(e, 11, c)
            step(e.tensor_tensor(k.lg[:], k.ex[:], k.rest[:], ALU.subtract))
            step(e.tensor_reduce(k.red[:], k.lg[:], AX_X, ALU.add))
            step(e.tensor_scalar(k.red2[:], k.red[:], 1e-20, None, ALU.add))
            step(e.reciprocal(k.red[:], k.red2[:]))
            step(e.tensor_tensor(k.lg[:], k.lg[:], over(k.red), ALU.mult))
        if slot == 6:
            self.r_cH.wait(e, 1, c)
            cols = bass.ds(c * CHUNK, CHUNK)
            e.tensor_tensor(k.gate[32:32 + NEXP, cols], ptr[0:NEXP, :],
                            k.gate[0:NEXP, cols].bitcast(F32), ALU.subtract) @ self.r_cL


class SwiGLU:

    WCOLS = 2 * KB * P + HID

    def __init__(self, k, tag, groups, G, pack, rows, before, tail):
        self.k, self.NG, self.G, self.pack, self.rows = k, groups, G, pack, rows
        self.before, self.tail = before, tail
        k.kind = "glu_"
        S = NCH * G
        self.S = S
        self.s_raw = [Sem(k, f"raw{i}", 32 if rows is not None else 16, passes=groups) for i in range(G)]
        self.s_wH = Sem(k, "wH", G, passes=groups)
        self.s_wL = Sem(k, "wL", G, passes=groups)
        self.s_gu = Sem(k, "gu", S, passes=groups)
        self.s_cb = Sem(k, "cb", S, passes=groups)
        self.s_dn = Sem(k, "dn", S, credit=G, passes=groups)
        self.s_silu = Sem(k, "silu", S, passes=groups)
        self.s_hH = Sem(k, "hH", S, passes=groups)
        self.s_t = Sem(k, "t", S, credit=2, passes=groups)
        self.s_h = Sem(k, "h", S, passes=groups) if rows is not None else None
        self.s_hL = Sem(k, "hL", S, credit=2, passes=groups)
        self.s_acc = Sem(k, "acc", 4, credit=1, passes=groups)
        self.s_zero = Sem(k, "zero", total=1)
        tail.src_ready, tail.src = _Shifted(self.s_acc, 4 * (groups - 1)), \
            lambda c: k.accT[:, :, c * CHUNK:(c + 1) * CHUNK]
        a = Arena(k, tag)
        self.raw = a.new("w_raw", [P, G, self.WCOLS])
        self.raws = a.new("rows_raw", [64, G, P])
        self.wH = a.new("w_hi", [P, G, self.WCOLS], F32R)
        self.wL = a.new("w_lo", [P, G, self.WCOLS], F32R)
        self.rw = a.new("rows", [64, G, P], F32R)
        self.hb = a.new("hidden", [P, 2, CHUNK])
        self.hH = a.new("hidden_hi", [P, 2, CHUNK], F32R)
        self.hL = a.new("hidden_lo", [P, 2, CHUNK], F32R)

    def over_groups(self, e, step):
        if self.NG > 1:
            with e.Fori(0, self.NG - 1) as g:
                for s in range(self.S):
                    step(g, s, False)
        for s in range(self.S):
            step(self.NG - 1, s, True)

    def tails(self, fn, e, s):
        c, kk = divmod(s, self.G)
        if c and kk < 4:
            fn(e, c - 1, kk)

    def after(self, fn, e):
        for slot in range(4):
            fn(e, NCH - 1, slot)
        if self.tail.route:
            for c in range(NCH):
                for slot in (4, 5, 6):
                    fn(e, c, slot)

    def sync(self, e):
        self.before.ready(e, NCH - 1)
        for t in range(self.G):
            e.dma_start(self.raw[:, t, :], self.pack[t]).then_inc(self.s_raw[t].sem, 16)
            if self.rows is not None:
                e.dma_start(self.raws[:, t, :], self.rows[t]).then_inc(self.s_raw[t].sem, 16)
        if self.NG > 1:
            with e.Fori(0, self.NG - 1) as g:
                for t in range(self.G):
                    self.s_wH.wait(e, t + 1, g)
                    self.s_wL.wait(e, t + 1, g)
                    nxt = g * self.G + (self.G + t)
                    e.dma_start(self.raw[:, t, :], self.pack[bass.ds(nxt, 1), :, :].rearrange("o p n -> (o p) n")).then_inc(self.s_raw[t].sem, 16)
                    if self.rows is not None:
                        e.dma_start(self.raws[:, t, :], self.rows[bass.ds(nxt, 1), :, :].rearrange("o p n -> (o p) n")).then_inc(self.s_raw[t].sem, 16)
        if self.tail.last:
            self.tail.sync(e)

    def pool(self, e):
        self.before.ready(e, NCH - 1)
        e.memset(self.k.accT[:], 0.0) @ self.s_zero
        for c in range(NCH):
            for slot in (0, 2):
                self.tail.pool(e, c, slot)

    def gu(self, e, g, s):
        c, t = divmod(s, self.G)
        k, b = self.k, 2 * (s % 2)
        if c == 0:
            self.s_wH.wait(e, t + 1, g)
            self.s_wL.wait(e, t + 1, g)
        self.s_t.wait(e, s - 1, g)
        cols = slice(c * CHUNK, (c + 1) * CHUNK)
        for half in range(2):
            for kb in range(KB):
                w = slice((half * KB + kb) * P, (half * KB + kb + 1) * P)
                m = three(e, k.psum[:, b + half, :], self.wH[:, t, w], self.wL[:, t, w],
                          k.xH[:, kb, cols], k.xL[:, kb, cols], kb == 0, kb == KB - 1)
        m @ self.s_gu

    def cb(self, e, g, s):
        if self.rows is None:
            return
        c, t = divmod(s, self.G)
        e.matmul(self.k.psum[:, 4, :], self.rw[:, t, :], self.k.gate[:, c * CHUNK:(c + 1) * CHUNK],
                 start=True, stop=True) @ self.s_cb

    def down(self, e, g, s):
        c, t = divmod(s, self.G)
        if t == 0:
            self.s_acc.wait(e, c, g)
        self.s_hH.wait(e, s + 1, g)
        self.s_hL.wait(e, s + 1, g)
        for ob in range(KB):
            w = slice(2 * KB * P + ob * P, 2 * KB * P + (ob + 1) * P)
            m = three(e, self.k.psum[:, 5 + ob, :], self.wH[:, t, w], self.wL[:, t, w],
                      self.hH[:, s % 2, :], self.hL[:, s % 2, :], t == 0, t == self.G - 1)
        m @ self.s_dn

    def tensor(self, e):
        for c in range(NCH):
            self.before.ready(e, c)
            if c == 0:
                self.gu(e, 0, 0)
                self.cb(e, 0, 0)

        def step(g, s, last):
            if s + 1 < self.S:
                self.gu(e, g, s + 1)
            elif not last:
                self.gu(e, g + 1, 0)
            self.down(e, g, s)
            if s + 1 < self.S:
                self.cb(e, g, s + 1)
            elif not last:
                self.cb(e, g + 1, 0)
            if last:
                self.tails(self.tail.pe, e, s)

        self.over_groups(e, step)
        self.after(self.tail.pe, e)

    def split_hi(self, e, g, t):
        self.s_raw[t].wait(e, self.s_raw[t].per, g)
        self.s_dn.wait(e, t + 1 - self.G, g)
        e.activation(self.wH[:, t, :], self.raw[:, t, :], ACT.Copy) @ self.s_wH
        if self.rows is not None:
            pass

    def split_lo(self, e, g, t):
        if self.rows is not None:
            self.s_raw[t].wait(e, self.s_raw[t].per, g)
            self.s_dn.wait(e, t + 1 - self.G, g)
            e.tensor_copy(self.rw[:, t, :], self.raws[:, t, :])
        self.s_wH.wait(e, t + 1, g)
        e.tensor_tensor(self.wL[:, t, :], self.raw[:, t, :], self.wH[:, t, :].bitcast(F32),
                        ALU.subtract) @ self.s_wL

    def splits(self, fn, e, g, s, last):
        if s < self.G - 1:
            fn(e, g, s + 1)
        elif s == self.S - 1 and not last:
            fn(e, g + 1, 0)

    def scalar(self, e):
        self.before.ready(e, NCH - 1)
        self.split_hi(e, 0, 0)

        def step(g, s, last):
            b = s % 2
            self.splits(self.split_hi, e, g, s, last)
            self.s_gu.wait(e, s + 1, g)
            self.s_hL.wait(e, s - 1, g)
            e.activation(self.hb[:, b, :], self.k.psum[:, 2 * b, :], ACT.Silu) @ self.s_silu
            (self.s_h or self.s_t).wait(e, s + 1, g)
            self.s_dn.wait(e, s - 1, g)
            e.activation(self.hH[:, b, :], self.hb[:, b, :], ACT.Copy) @ self.s_hH
            if last:
                self.tails(self.tail.act, e, s)

        self.over_groups(e, step)
        self.after(self.tail.act, e)

    def vector(self, e):
        k = self.k
        self.before.ready(e, NCH - 1)
        self.split_lo(e, 0, 0)
        self.s_zero.wait(e, 1)

        def step(g, s, last):
            b, (c, t) = s % 2, divmod(s, self.G)
            self.splits(self.split_lo, e, g, s, last)
            self.s_silu.wait(e, s + 1, g)
            e.tensor_tensor(self.hb[:, b, :], self.hb[:, b, :], k.psum[:, 2 * b + 1, :],
                            ALU.mult) @ self.s_t
            if self.s_h:
                self.s_cb.wait(e, s + 1, g)
                self.s_t.wait(e, s + 1, g)
                e.tensor_tensor(self.hb[:, b, :], self.hb[:, b, :], k.psum[:, 4, :],
                                ALU.mult) @ self.s_h
            self.s_hH.wait(e, s + 1, g)
            self.s_dn.wait(e, s - 1, g)
            e.tensor_tensor(self.hL[:, b, :], self.hb[:, b, :], self.hH[:, b, :].bitcast(F32),
                            ALU.subtract) @ self.s_hL
            if t == self.G - 1:
                self.s_dn.wait(e, s + 1, g)
                cols = slice(c * CHUNK, (c + 1) * CHUNK)
                e.scalar_tensor_tensor(k.accT[:, :, cols], k.psum[:, 5:5 + KB, :], 0.5,
                                       k.accT[:, :, cols], ALU.mult, ALU.add) @ self.s_acc
            if last:
                self.tails(self.tail.dve, e, s)

        self.over_groups(e, step)
        self.after(self.tail.dve, e)


class _Shifted:

    def __init__(self, sem, shift):
        self.sem, self.shift = sem, shift

    def wait(self, eng, count, c):
        self.sem.wait(eng, self.shift + c + count)


class Entry:

    def __init__(self, k, x, tail):
        self.k, self.x, self.tail = k, x, tail

    def sync(self, e):
        for c in range(NCH):
            e.dma_start(self.k.X[:, 4 * c:4 * c + 4, :],
                        self.x[c * CHUNK:(c + 1) * CHUNK, :].rearrange("(n p) f -> p n f", p=P)
                        ).then_inc(self.tail.s_in[c].sem, 16)

    def run(self, e, fn):
        for c in range(NCH):
            for slot in range(7):
                fn(e, c, slot)

    def tensor(self, e):
        self.run(e, self.tail.pe)

    def scalar(self, e):
        self.run(e, self.tail.act)

    def vector(self, e):
        self.run(e, self.tail.dve)

    def pool(self, e):
        self.run(e, self.tail.pool)


class Scan:

    def __init__(self, k, tag, ins, before, tail):
        self.k, self.ins, self.before, self.tail = k, ins, before, tail
        k.kind = tag
        self.s_in = Sem(k, "in", 8)
        self.s_hp = Sem(k, "hp", 4)
        self.s_cv = Sem(k, "cv", 4)
        self.s_sg = Sem(k, "sg", 4)
        self.s_pad = Sem(k, "pad", 1)
        self.s_conv = Sem(k, "conv", 4)
        self.s_u = Sem(k, "u", 4)
        self.s_ul = Sem(k, "ul", 1)
        self.s_xp = Sem(k, "xp", 4)
        self.s_sq = Sem(k, "sq", 4)
        self.s_ms = Sem(k, "ms", 2)
        self.s_rr = Sem(k, "rr", 1)
        self.s_tsn = Sem(k, "tsn", 12)
        self.s_tst = Sem(k, "tst", 2)
        self.s_tsw = Sem(k, "tsw", 2)
        self.s_tsl = Sem(k, "tsl", 1)
        self.s_bc = Sem(k, "bc", 1)
        self.s_dt = Sem(k, "dt", 4)
        self.s_abs = Sem(k, "abs", 4)
        self.s_relu = Sem(k, "relu", 4)
        self.s_e = Sem(k, "e", 1)
        self.s_l = Sem(k, "l", 1)
        self.s_delta = Sem(k, "delta", 1)
        self.s_dtu = Sem(k, "dtu", 1)
        self.s_dz = Sem(k, "dz", 1)
        self.s_bcast = Sem(k, "bcast", NST)
        self.s_bs = Sem(k, "bs", NST)
        self.s_dA = Sem(k, "dA", IB * NST)
        self.s_m1 = Sem(k, "m1", NST)
        self.s_scan = Sem(k, "scan", NST)
        self.s_z = Sem(k, "z", NST)
        self.s_y = Sem(k, "y", NST)
        self.s_yl = Sem(k, "yl", 1)
        self.s_o = Sem(k, "o", 1)
        self.s_fin = Sem(k, "fin", 1)
        self.s_v = Sem(k, "v", 22)
        self.s_load = Sem(k, "load")
        self.s_wh, self.s_wl = Sem(k, "wh"), Sem(k, "wl")
        tail.src_ready, tail.src = self.s_fin, lambda c: self.fin
        a = Arena(k, tag)
        new = a.new
        self.wcols = [KB * 2 * IN, IB * XP, IN, IB * HID]
        total = sum(self.wcols)
        self.wH, self.wL = new("w_hi", [P, total], F32R), new("w_lo", [P, total], F32R)
        self.u = new("u", [P, IB, CHUNK])
        self.sg = new("silu_gate", [P, IB, CHUNK])
        at = a.off
        self.delta = new("delta", [P, IB, CHUNK])
        self.dtu = new("delta_u", [P, IB, CHUNK])
        self.hpad = new("conv_in", [P, IB, 2, SEQ + KCONV - 1], over=at)
        at = a.off
        self.dA = new("decay", [P, 2, IB, CHUNK])
        small = Arena(k, tag)
        small.off = at
        self.sq = small.new("squares", [P, 4, XP])
        self.tsn = small.new("ts_norm", [P, 4, RANK])
        self.bcn = small.new("bc_norm", [P, 4, 2 * NST])
        self.tsw = small.new("ts_weighted", [P, CHUNK])
        self.bcw = small.new("bc_weighted", [2 * NST, CHUNK])
        self.tsH = small.new("ts_hi", [P, CHUNK], F32R)
        self.tsL = small.new("ts_lo", [P, CHUNK], F32R)
        assert small.off <= a.off
        at = a.off
        self.st = [new(f"state{i}", [P, IB, CHUNK]) for i in range(3)]
        self.raw = new("w_raw", [P, total], over=at)
        self.Bs = new("B_all", [P, 2, CHUNK])
        self.bc = new("BC", [64, CHUNK], F32R)
        self.ms, self.rr = new("mean_sq", [P, 12]), new("rms_inv", [P, 12])
        self.fin = new("out", [P, KB, CHUNK])
        self.cw, self.cb = new("conv_w", [P, IB, KCONV]), new("conv_b", [P, IB])
        self.dtw, self.bcwt = new("dt_ln", [P, 1]), new("bc_ln", [2 * NST, 1])
        self.dtb, self.A, self.D = new("dt_bias", [P, IB]), new("A", [P, IB, NST]), new("D", [P, IB])
        self.eye = new("state_pick_raw", [64, 2 * NST])
        self.pick = new("state_pick", [64, 2 * NST], F32R)
        assert a.off <= k.nc.sbuf_usable_end, a.off
        acc = Arena(k, tag)
        acc.off = k.acc_at
        self.uH, self.uL = acc.new("u_hi", [P, IB, CHUNK], F32R), acc.new("u_lo", [P, IB, CHUNK], F32R)

    def weight(self, n, cols):
        at = sum(self.wcols[:n])
        s = slice(at + cols.start, at + cols.stop)
        return self.wH[:, s], self.wL[:, s]

    def sync(self, e):
        self.before.ready(e, NCH - 1)
        i = self.ins
        at = 0
        for w, n in zip(("W_in", "Wx", "Wdt", "Wout"), self.wcols):
            e.dma_start(self.raw[:, at:at + n], i[w]).then_inc(self.s_load.sem, 16)
            at += n
        for dst, name in ((self.cw, "conv_w"), (self.cb, "conv_b"), (self.dtw, "dt_ln"),
                          (self.bcwt, "bc_ln"), (self.dtb, "dt_bias"), (self.A, "A"), (self.D, "D"),
                          (self.eye, "state_pick")):
            e.dma_start(dst[:], i[name]).then_inc(self.s_load.sem, 16)
        if self.tail.last:
            self.tail.sync(e)

    def loop(self, e, body):
        with e.Fori(0, NCH) as c:
            self.tail.idle(e, c)
            body(c)

    def tails(self, fn, e, c):
        for slot in range(7 if self.tail.route else 4):
            fn(e, c, slot)

    def pool(self, e):
        self.before.ready(e, NCH - 1)

        def body(c):
            self.k.own(e)
            e.memset(self.hpad[:, :, :, 0:KCONV - 1], 0.0) @ self.s_pad
            self.s_ms.wait(e, 2, c)
            e.tensor_tensor(self.rr[:], self.ms[:], self.k.half[:, 0:12], ALU.pow) @ self.s_rr
            self.s_dt.wait(e, 4, c)
            self.s_bc.wait(e, 1, c)
            self.k.own(e)
            e.memset(self.dA[:].rearrange("p a b (s t) -> p (a b s) t", t=SEQ)[:, :, 0], 0.0) @ self.s_dz
            self.s_dtu.wait(e, 1, c)
            for n in range(NST):
                self.s_bs.wait(e, n + 1, c)
                if n >= 3:
                    self.s_y.wait(e, n - 2, c)
                e.tensor_tensor(self.st[n % 3][:], self.dtu[:],
                                self.Bs[:, n % 2, :].unsqueeze(1).broadcast_to([P, IB, CHUNK]),
                                ALU.mult) @ self.s_m1
            self.tails(self.tail.pool, e, c)

        self.loop(e, body)

    def tensor(self, e):
        k = self.k
        self.before.ready(e, NCH - 1)
        self.s_wl.wait(e, 1)

        def bcast(c, n):
            if n >= 2:
                self.s_bs.wait(e, n - 1, c)
                self.s_z.wait(e, n - 1, c)
            for part in range(2):
                col = part * NST + n
                m = e.matmul(k.psum[:, 4 + 2 * (n % 2) + part, :],
                             self.pick[:, col:col + 1].broadcast_to([64, P]), self.bc[:],
                             start=True, stop=True)
            m @ self.s_bcast

        def body(c):
            cols = bass.ds(c * CHUNK, CHUNK)
            for m in range(2 * IB):
                for kb in range(KB):
                    w = self.weight(0, slice(kb * 2 * IN + m * P, kb * 2 * IN + (m + 1) * P))
                    x = three(e, k.psum[:, m, :], *w, k.xH[:, kb, cols], k.xL[:, kb, cols],
                              kb == 0, kb == KB - 1)
                x @ self.s_in
            self.s_ul.wait(e, 1, c)
            for j in range(4):
                t = slice(j * P, (j + 1) * P)
                for ib in range(IB):
                    w = self.weight(1, slice(ib * XP, (ib + 1) * XP))
                    x = three(e, k.psum[:, j, 0:XP], self.uH[:, ib, t], self.uL[:, ib, t], *w,
                              ib == 0, ib == IB - 1)
                x @ self.s_xp
            self.s_tsn.wait(e, 12, c)
            self.s_sg.wait(e, 4, c)
            for j in range(4):
                x = e.transpose(k.psum[:, 4, j * P:(j + 1) * P], self.tsn[:, j, :], k.ident[:])
            x @ self.s_tst
            for j in range(4):
                x = e.transpose(k.psum[0:2 * NST, 5, j * P:(j + 1) * P], self.bcn[:, j, :], k.ident[:])
            x @ self.s_tst
            self.s_tsl.wait(e, 1, c)
            for m in range(IB):
                w = self.weight(2, slice(m * P, (m + 1) * P))
                three(e, k.psum[:, m, :], *w, self.tsH[:], self.tsL[:], True, True) @ self.s_dt
            self.s_bc.wait(e, 1, c)
            self.s_tsw.wait(e, 2, c)
            bcast(c, 0)
            bcast(c, 1)
            for n in range(NST):
                if n + 2 < NST:
                    bcast(c, n + 2)
                self.s_z.wait(e, n + 1, c)
                for m in range(IB):
                    x = e.matmul(k.psum[:, m, :], k.ident[:], self.st[n % 3][:, m, :],
                                 start=(n == 0), stop=(n == NST - 1))
                x @ self.s_y
            self.s_yl.wait(e, 1, c)
            for ob in range(KB):
                for ib in range(IB):
                    w = self.weight(3, slice(ib * HID + ob * P, ib * HID + (ob + 1) * P))
                    x = three(e, k.psum[:, 4 + ob, :], *w, self.uH[:, ib, :], self.uL[:, ib, :],
                              ib == 0, ib == IB - 1)
            x @ self.s_o
            self.tails(self.tail.pe, e, c)

        self.loop(e, body)

    def scalar(self, e):
        k, ps = self.k, self.k.psum
        self.before.ready(e, NCH - 1)
        e.wait_ge(self.s_load.sem, 16 * 12)
        e.activation(self.wH[:], self.raw[:], ACT.Copy) @ self.s_wh

        def body(c):
            self.s_pad.wait(e, 1, c)
            for m in range(IB):
                self.s_in.wait(e, m + 1, c)
                e.activation(self.hpad[:, m, :, KCONV - 1:], ps[:, m, :].rearrange("p (s t) -> p s t", s=2),
                             ACT.Copy) @ self.s_hp
                e.activation(self.u[:, m, :], ps[:, m, :], ACT.Identity, bias=self.cb[:, m:m + 1],
                             scale=self.cw[:, m, KCONV - 1:KCONV]) @ self.s_cv
            for m in range(IB):
                self.s_in.wait(e, IB + m + 1, c)
                e.activation(self.sg[:, m, :], ps[:, IB + m, :], ACT.Silu) @ self.s_sg
            for m in range(IB):
                self.s_conv.wait(e, m + 1, c)
                e.activation(self.u[:, m, :], self.u[:, m, :], ACT.Silu) @ self.s_u
            for j in range(4):
                self.s_xp.wait(e, j + 1, c)
                e.activation(self.sq[:, j, :], ps[:, j, 0:XP], ACT.Square) @ self.s_sq
            self.s_tst.wait(e, 1, c)
            e.activation(self.tsw[:], ps[:, 4, :], ACT.Copy, scale=self.dtw[:]) @ self.s_tsw
            self.s_tst.wait(e, 2, c)
            e.activation(self.bcw[:], ps[0:2 * NST, 5, :], ACT.Copy, scale=self.bcwt[:]) @ self.s_tsw
            ax, ln = self.st[0], self.st[1]
            for m in range(IB):
                self.s_dt.wait(e, m + 1, c)
                e.activation(ax[:, m, :], ps[:, m, :], ACT.Abs, bias=self.dtb[:, m:m + 1]) @ self.s_abs
            for m in range(IB):
                e.activation(self.delta[:, m, :], ps[:, m, :], ACT.Relu, bias=self.dtb[:, m:m + 1]) @ self.s_relu
            self.s_abs.wait(e, 4, c)
            e.activation(ax[:], ax[:], ACT.Exp, scale=-1.0) @ self.s_e
            self.s_e.wait(e, 1, c)
            e.activation(ln[:], ax[:], ACT.Ln, bias=1.0) @ self.s_l
            self.s_delta.wait(e, 1, c)
            for n in range(NST):
                self.s_bcast.wait(e, n + 1, c)
                if n >= 2:
                    self.s_m1.wait(e, n - 1, c)
                e.activation(self.Bs[:, n % 2, :], ps[:, 4 + 2 * (n % 2), :], ACT.Copy) @ self.s_bs
                if n >= 2:
                    self.s_scan.wait(e, n - 1, c)
                for m in range(IB):
                    e.activation(
                        self.dA[:, n % 2, m, :].rearrange("p (s t) -> p s t", s=2)[:, :, 1:],
                        self.delta[:, m, :].rearrange("p (s t) -> p s t", s=2)[:, :, 1:],
                        ACT.Exp, scale=self.A[:, m, n:n + 1]) @ self.s_dA
            self.s_o.wait(e, 1, c)
            e.activation(self.fin[:], ps[:, 4:6, :], ACT.Copy) @ self.s_fin
            self.tails(self.tail.act, e, c)

        self.loop(e, body)

    def vector(self, e):
        k, ps = self.k, self.k.psum
        self.before.ready(e, NCH - 1)
        e.wait_ge(self.s_load.sem, 16 * 12)
        e.tensor_copy(self.pick[:], self.eye[:])
        self.s_wh.wait(e, 1)
        e.tensor_tensor(self.wL[:], self.raw[:], self.wH[:].bitcast(F32), ALU.subtract) @ self.s_wl
        self.s_wl.wait(e, 1)

        def body(c):
            count = [0]

            def v(ins, wait=True):
                ins @ self.s_v
                count[0] += 1
                if wait:
                    self.s_v.wait(e, count[0], c)

            for tap in range(KCONV - 1):
                for m in range(IB):
                    if tap == 0:
                        self.s_cv.wait(e, m + 1, c)
                        self.s_hp.wait(e, m + 1, c)
                    else:
                        self.s_v.wait(e, (tap - 1) * IB + m + 1, c)
                    um = self.u[:, m, :].rearrange("p (s t) -> p s t", s=2)
                    x = e.scalar_tensor_tensor(um, self.hpad[:, m, :, tap:tap + SEQ],
                                               self.cw[:, m, tap:tap + 1], um, ALU.mult, ALU.add)
                    if tap < KCONV - 2:
                        v(x, wait=False)
                    else:
                        x @ self.s_conv
            self.s_u.wait(e, 4, c)
            v(e.tensor_copy(self.uH[:], self.u[:]))
            e.tensor_tensor(self.uL[:], self.u[:], self.uH[:].bitcast(F32), ALU.subtract) @ self.s_ul
            self.s_sq.wait(e, 4, c)
            v(e.tensor_reduce(self.ms[:, 0:4], self.sq[:, :, 0:RANK], AX_X, ALU.add), wait=False)
            v(e.tensor_reduce(self.ms[:, 4:12].rearrange("p (j s) -> p j s", s=2),
                              self.sq[:, :, RANK:XP].rearrange("p j (s n) -> p j s n", s=2),
                              AX_X, ALU.add))
            e.tensor_scalar(self.ms[:, 0:4], self.ms[:, 0:4], 1.0 / RANK, EPS, ALU.mult, ALU.add) @ self.s_ms
            e.tensor_scalar(self.ms[:, 4:12], self.ms[:, 4:12], 1.0 / NST, EPS, ALU.mult, ALU.add) @ self.s_ms
            self.s_rr.wait(e, 1, c)
            for j in range(4):
                for dst, a, b, r in ((self.tsn[:, j, :], 0, RANK, j),
                                     (self.bcn[:, j, 0:NST], RANK, RANK + NST, 4 + 2 * j),
                                     (self.bcn[:, j, NST:], RANK + NST, XP, 5 + 2 * j)):
                    e.tensor_scalar(dst, ps[:, j, a:b], self.rr[:, r:r + 1], None, ALU.mult) @ self.s_tsn
            self.s_tsw.wait(e, 1, c)
            v(e.tensor_copy(self.tsH[:], self.tsw[:]))
            e.tensor_tensor(self.tsL[:], self.tsw[:], self.tsH[:].bitcast(F32), ALU.subtract) @ self.s_tsl
            self.s_tsw.wait(e, 2, c)
            v(e.tensor_copy(self.bc[0:2 * NST, :], self.bcw[:]))
            e.tensor_tensor(self.bc[32:32 + 2 * NST, :], self.bcw[:], self.bc[0:2 * NST, :].bitcast(F32),
                            ALU.subtract) @ self.s_bc
            self.s_relu.wait(e, 4, c)
            ax, ln, t = self.st
            self.s_e.wait(e, 1, c)
            v(e.tensor_scalar(t[:], ax[:], 1.0, 1.0, ALU.add, ALU.subtract))
            v(e.tensor_tensor(t[:], ax[:], t[:], ALU.subtract))
            self.s_l.wait(e, 1, c)
            v(e.tensor_tensor(t[:], t[:], ln[:], ALU.add))
            e.tensor_tensor(self.delta[:], self.delta[:], t[:], ALU.add) @ self.s_delta
            self.s_delta.wait(e, 1, c)
            e.tensor_tensor(self.dtu[:], self.delta[:], self.u[:], ALU.mult) @ self.s_dtu
            self.s_dz.wait(e, 1, c)

            def flat(x):
                return x.rearrange("p m t -> p (m t)")

            def times_c(n):
                self.s_scan.wait(e, n + 1, c)
                self.s_bcast.wait(e, n + 1, c)
                cb = ps[:, 5 + 2 * (n % 2), :].unsqueeze(1).broadcast_to([P, IB, CHUNK])
                e.tensor_tensor(self.st[n % 3][:], self.st[n % 3][:], cb, ALU.mult) @ self.s_z

            for n in range(NST):
                self.s_dA.wait(e, IB * (n + 1), c)
                self.s_m1.wait(e, n + 1, c)
                s = flat(self.st[n % 3][:])
                e.tensor_tensor_scan(s, flat(self.dA[:, n % 2, :, :]), s, 0.0, ALU.mult, ALU.add) @ self.s_scan
                times_c(n)
            self.s_y.wait(e, NST, c)
            for m in range(IB):
                v(e.scalar_tensor_tensor(self.u[:, m, :], self.u[:, m, :], self.D[:, m:m + 1],
                                         ps[:, m, :], ALU.mult, ALU.add), wait=(m == IB - 1))
            v(e.tensor_tensor(self.u[:], self.u[:], self.sg[:], ALU.mult))
            v(e.tensor_copy(self.uH[:], self.u[:]))
            e.tensor_tensor(self.uL[:], self.u[:], self.uH[:].bitcast(F32), ALU.subtract) @ self.s_yl
            assert count[0] == self.s_v.per, count[0]
            self.tails(self.tail.dve, e, c)

        self.loop(e, body)


class Attention:

    UNITS = 16

    def __init__(self, k, tag, ins, before, tail):
        self.k, self.ins, self.before, self.tail = k, ins, before, tail
        k.kind = tag
        U = self.UNITS
        self.s_in = Sem(k, "in", 8)
        self.s_q = Sem(k, "q", 4)
        self.s_k = Sem(k, "k", 4)
        self.s_vT = Sem(k, "vT", 2)
        self.s_vTs = Sem(k, "vTs", 2)
        self.s_vt = Sem(k, "vt", 1)
        self.s_v = Sem(k, "v", 2)
        self.s_S = Sem(k, "S", U)
        self.s_max = Sem(k, "max", U)
        self.s_nm = Sem(k, "nm", U)
        self.s_exp = Sem(k, "exp", U)
        self.s_T = Sem(k, "T", U)
        self.s_pt = Sem(k, "pt", U)
        self.s_pv = Sem(k, "pv", U)
        self.s_rec = Sem(k, "rec", 2)
        self.s_on = Sem(k, "on", 2)
        self.s_ot = Sem(k, "ot", 2)
        self.s_oH = Sem(k, "oH", 2)
        self.s_oL = Sem(k, "oL", 2)
        self.s_o = Sem(k, "o", 1)
        self.s_fin = Sem(k, "fin", 1)
        self.s_load, self.s_wh, self.s_wl = Sem(k, "load"), Sem(k, "wh"), Sem(k, "wl")
        tail.src_ready, tail.src = self.s_fin, lambda c: self.fin
        new = Arena(k, tag).new
        self.wcols = [KB * NGRP * P, KB * NGRP * P, KB * HID, KB * HID]
        total = sum(self.wcols)
        self.raw = new("w_raw", [P, total])
        self.wH, self.wL = new("w_hi", [P, total], F32R), new("w_lo", [P, total], F32R)
        self.q, self.kk = new("q", [P, NGRP, CHUNK]), new("k", [P, NGRP, CHUNK])
        self.vT, self.v = new("vT", [P, KB, CHUNK]), new("v", [P, 4, HID])
        self.p0, self.p1 = new("p0", [P, 2, 2, P]), new("p1", [P, 2, 2, SEQ])
        self.pt = new("pT", [P, 2, 6 * P])
        self.mx, self.nm = new("max", [P, 2, 4]), new("neg_max", [P, 2, 4])
        self.sums, self.rec = new("sums", [P, 2, 2, HEADS]), new("recip", [P, 2, 2, HEADS])
        self.on = new("o_norm", [P, 2, HID])
        self.oH, self.oL = new("o_hi", [P, KB, CHUNK], F32R), new("o_lo", [P, KB, CHUNK], F32R)
        self.fin = new("out", [P, KB, CHUNK])
        self.pat = new("slopes", [P, NGRP, SEQ])
        self.mraw, self.mask = new("mask_raw", [P, SEQ]), new("mask", [P, SEQ], F32R)
        self.one = new("ident_r", [P, P], F32R)
        self.bq, self.bk = new("bq", [P, NGRP]), new("bk", [P, NGRP])
        self.bv, self.bo = new("bv", [P, KB]), new("bo", [P, KB])
        self.bqs = new("bq_scaled", [P, NGRP])

    weight, loop, tails = Scan.weight, Scan.loop, Scan.tails

    def sync(self, e):
        self.before.ready(e, NCH - 1)
        i, at = self.ins, 0
        for w, n in zip(("Wq", "Wk", "Wv", "Wo"), self.wcols):
            e.dma_start(self.raw[:, at:at + n], i[w]).then_inc(self.s_load.sem, 16)
            at += n
        for dst, name in ((self.pat, "slopes"), (self.mraw, "mask"), (self.bq, "bq"), (self.bk, "bk"),
                          (self.bv, "bv"), (self.bo, "bo")):
            e.dma_start(dst[:], i[name]).then_inc(self.s_load.sem, 16)
        if self.tail.last:
            self.tail.sync(e)

    def pool(self, e):
        self.before.ready(e, NCH - 1)
        self.loop(e, lambda c: self.tails(self.tail.pool, e, c))

    @staticmethod
    def unit(u):
        b, i = divmod(u, 8)
        r, gg = i % HGRP, i // HGRP
        return b, HSLOT * r, [(g * HGRP + r, g) for g in (2 * gg, 2 * gg + 1)]

    def tensor(self, e):
        k, ps = self.k, self.k.psum
        self.before.ready(e, NCH - 1)
        self.s_wl.wait(e, 1)

        def scores(c, u):
            b, r, heads = self.unit(u)
            s = 2 * (u % 2)
            if u >= 2:
                self.s_exp.wait(e, u - 1, c)
            two = self.mask[:].unsqueeze(1).broadcast_to([P, 2, SEQ])
            e.matmul(ps[:, s, 0:2 * P], self.one[:], two[:, :, P:], start=True, stop=False)
            for x, (h, g) in enumerate(heads):
                e.matmul(ps[:, s, x * P:(x + 1) * P], self.q[r:r + HSLOT, g, b * SEQ:b * SEQ + P],
                         self.kk[r:r + HSLOT, g, b * SEQ:b * SEQ + P], start=False, stop=(x == 1))
            e.matmul(ps[:, s + 1, :], self.one[:], two, start=True, stop=False)
            for x, (h, g) in enumerate(heads):
                m = e.matmul(ps[:, s + 1, x * SEQ:(x + 1) * SEQ],
                             self.q[r:r + HSLOT, g, b * SEQ + P:(b + 1) * SEQ],
                             self.kk[r:r + HSLOT, g, b * SEQ:(b + 1) * SEQ], start=False, stop=(x == 1))
            m @ self.s_S

        def turn(c, u):
            self.s_exp.wait(e, u + 1, c)
            if u:
                self.s_pt.wait(e, u, c)
            for x in range(2):
                for kt in range(2):
                    e.transpose(ps[:, 4, (2 * x + kt) * P:(2 * x + kt + 1) * P],
                                self.p1[:, u % 2, x, kt * P:(kt + 1) * P], k.ident[:])
            for x in range(2):
                m = e.transpose(ps[:, 5, x * P:(x + 1) * P], self.p0[:, u % 2, x, :], k.ident[:])
            m @ self.s_T

        def values(c, u):
            b, r, heads = self.unit(u)
            self.s_pt.wait(e, u + 1, c)
            if u == 8:
                self.s_on.wait(e, 1, c)
            pt = self.pt[:, u % 2, :]
            for x, (h, g) in enumerate(heads):
                d = slice(h * HD, (h + 1) * HD)
                e.matmul(ps[:, 6, h * HD:(h + 1) * HD], pt[:, (4 + x) * P:(5 + x) * P],
                         self.v[:, 2 * b, d], start=True, stop=True)
                for kt in range(2):
                    m = e.matmul(ps[:, 6, HID + h * HD:HID + (h + 1) * HD],
                                 pt[:, (2 * x + kt) * P:(2 * x + kt + 1) * P],
                                 self.v[:, 2 * b + kt, d], start=(kt == 0), stop=(kt == 1))
            m @ self.s_pv

        def turn_out(c, b):
            self.s_on.wait(e, b + 1, c)
            if b:
                self.s_oL.wait(e, 1, c)
            for kb in range(KB):
                for j in range(2):
                    m = e.transpose(ps[:, 7, kb * SEQ + j * P:kb * SEQ + (j + 1) * P],
                                    self.on[:, j, kb * P:(kb + 1) * P], k.ident[:])
            m @ self.s_ot

        def body(c):
            cols = bass.ds(c * CHUNK, CHUNK)
            for m in range(2 * NGRP):
                which, g = divmod(m, NGRP)
                for kb in range(KB):
                    w = self.weight(which, slice(kb * NGRP * P + g * P, kb * NGRP * P + (g + 1) * P))
                    x = three(e, ps[:, m, :], *w, k.xH[:, kb, cols], k.xL[:, kb, cols], kb == 0, kb == KB - 1)
                x @ self.s_in
            self.s_q.wait(e, 2, c)
            for ob in range(KB):
                for kb in range(KB):
                    w = self.weight(2, slice(kb * HID + ob * P, kb * HID + (ob + 1) * P))
                    x = three(e, ps[:, ob, :], *w, k.xH[:, kb, cols], k.xL[:, kb, cols], kb == 0, kb == KB - 1)
                x @ self.s_vT
            self.s_vTs.wait(e, 2, c)
            for j in range(4):
                for kb in range(KB):
                    x = e.transpose(ps[:, 2 + j // 2, (j % 2) * HID + kb * P:(j % 2) * HID + (kb + 1) * P],
                                    self.vT[:, kb, j * P:(j + 1) * P], k.ident[:])
            x @ self.s_vt
            self.s_k.wait(e, 4, c)
            scores(c, 0)
            self.s_v.wait(e, 2, c)
            for u in range(self.UNITS + 1):
                if u + 1 < self.UNITS:
                    scores(c, u + 1)
                if u < self.UNITS:
                    turn(c, u)
                if u:
                    values(c, u - 1)
                if u == 9:
                    turn_out(c, 0)
            turn_out(c, 1)
            self.s_oL.wait(e, 2, c)
            for ob in range(KB):
                for kb in range(KB):
                    w = self.weight(3, slice(kb * HID + ob * P, kb * HID + (ob + 1) * P))
                    x = three(e, ps[:, 4 + ob, :], *w, self.oH[:, kb, :], self.oL[:, kb, :],
                              kb == 0, kb == KB - 1)
            x @ self.s_o
            self.tails(self.tail.pe, e, c)

        self.loop(e, body)

    def scalar(self, e):
        k, ps = self.k, self.k.psum
        self.before.ready(e, NCH - 1)
        e.wait_ge(self.s_load.sem, 16 * 10)
        e.activation(self.wH[:], self.raw[:], ACT.Copy) @ self.s_wh
        self.s_wl.wait(e, 1)

        def exps(c, u):
            b, r, heads = self.unit(u)
            s = 2 * (u % 2)
            self.s_nm.wait(e, u + 1, c)
            if u >= 2:
                self.s_T.wait(e, u - 1, c)
            for x, (h, g) in enumerate(heads):
                e.activation(self.p0[:, u % 2, x, :], ps[:, s, x * P:(x + 1) * P], ACT.Exp,
                             bias=self.nm[:, u % 2, x:x + 1], accum_out=self.sums[:, b, 0, h:h + 1])
                m = e.activation(self.p1[:, u % 2, x, :], ps[:, s + 1, x * SEQ:(x + 1) * SEQ], ACT.Exp,
                                 bias=self.nm[:, u % 2, 2 + x:3 + x], accum_out=self.sums[:, b, 1, h:h + 1])
            m @ self.s_exp

        def out_hi(c, b):
            self.s_ot.wait(e, b + 1, c)
            e.activation(self.oH[:, :, b * SEQ:(b + 1) * SEQ], ps[:, 7, :].rearrange("p (k t) -> p k t", k=KB),
                         ACT.Copy) @ self.s_oH

        def body(c):
            for g in range(NGRP):
                self.s_in.wait(e, g + 1, c)
                e.activation(self.q[:, g, :], ps[:, g, :], ACT.Identity, bias=self.bqs[:, g:g + 1],
                             scale=HD ** -0.5) @ self.s_q
            for ob in range(KB):
                self.s_vT.wait(e, ob + 1, c)
                e.activation(self.vT[:, ob, :], ps[:, ob, :], ACT.Identity, bias=self.bv[:, ob:ob + 1]) @ self.s_vTs
            self.s_vt.wait(e, 1, c)
            for j in range(2):
                e.activation(self.v[:, 2 * j:2 * j + 2, :], ps[:, 2 + j, :].rearrange("p (a b) -> p a b", a=2),
                             ACT.Copy) @ self.s_v
            for u in range(self.UNITS):
                exps(c, u)
                if u == 10:
                    out_hi(c, 0)
            out_hi(c, 1)
            self.s_o.wait(e, 1, c)
            for ob in range(KB):
                m = e.activation(self.fin[:, ob, :], ps[:, 4 + ob, :], ACT.Identity, bias=self.bo[:, ob:ob + 1])
            m @ self.s_fin
            self.tails(self.tail.act, e, c)

        self.loop(e, body)

    def vector(self, e):
        k, ps = self.k, self.k.psum
        self.before.ready(e, NCH - 1)
        e.wait_ge(self.s_load.sem, 16 * 10)
        e.tensor_copy(self.mask[:], self.mraw[:])
        e.tensor_copy(self.one[:], k.ident[:])
        e.tensor_scalar(self.bqs[:], self.bq[:], HD ** -0.5, None, ALU.mult)
        self.s_wh.wait(e, 1)
        e.tensor_tensor(self.wL[:], self.raw[:], self.wH[:].bitcast(F32), ALU.subtract) @ self.s_wl

        def maxima(c, u):
            s, m = 2 * (u % 2), self.mx[:, u % 2, :]
            self.s_S.wait(e, u + 1, c)
            if u >= 2:
                self.s_exp.wait(e, u - 1, c)
            e.tensor_reduce(m[:, 0:2], ps[:, s, 0:2 * P].rearrange("p (x t) -> p x t", x=2), AX_X, ALU.max)
            e.tensor_reduce(m[:, 2:4], ps[:, s + 1, :].rearrange("p (x t) -> p x t", x=2), AX_X,
                            ALU.max) @ self.s_max
            self.s_max.wait(e, u + 1, c)
            e.tensor_scalar(self.nm[:, u % 2, :], m, -1.0, None, ALU.mult) @ self.s_nm

        def take(c, u):
            self.s_T.wait(e, u + 1, c)
            if u >= 2:
                self.s_pv.wait(e, u - 1, c)
            e.tensor_copy(self.pt[:, u % 2, 0:4 * P], ps[:, 4, :])
            e.tensor_copy(self.pt[:, u % 2, 4 * P:], ps[:, 5, 0:2 * P]) @ self.s_pt

        def norm(c, b):
            self.s_pv.wait(e, 8 * (b + 1), c)
            self.s_exp.wait(e, 8 * (b + 1), c)
            e.reciprocal(self.rec[:, b], self.sums[:, b]) @ self.s_rec
            self.s_rec.wait(e, b + 1, c)
            if b:
                self.s_ot.wait(e, 1, c)
            e.tensor_tensor(self.on[:].rearrange("p j (h d) -> p (j h) d", d=HD),
                            ps[:, 6, :].rearrange("p (n d) -> p n d", d=HD),
                            self.rec[:, b].rearrange("p j h -> p (j h)").unsqueeze(2).broadcast_to([P, 2 * HEADS, HD]),
                            ALU.mult) @ self.s_on

        def out_lo(c, b):
            self.s_oH.wait(e, b + 1, c)
            cols = slice(b * SEQ, (b + 1) * SEQ)
            e.tensor_tensor(self.oL[:, :, cols], ps[:, 7, :].rearrange("p (k t) -> p k t", k=KB),
                            self.oH[:, :, cols].bitcast(F32), ALU.subtract) @ self.s_oL

        def body(c):
            for g in range(NGRP):
                self.s_in.wait(e, NGRP + g + 1, c)
                e.scalar_tensor_tensor(self.kk[:, g, :].rearrange("p (s t) -> p s t", s=2),
                                       ps[:, NGRP + g, :].rearrange("p (s t) -> p s t", s=2),
                                       self.bk[:, g:g + 1],
                                       self.pat[:, g, :].unsqueeze(1).broadcast_to([P, 2, SEQ]),
                                       ALU.add, ALU.add) @ self.s_k
            maxima(c, 0)
            for u in range(self.UNITS):
                if u + 1 < self.UNITS:
                    maxima(c, u + 1)
                take(c, u)
                if u == 8:
                    norm(c, 0)
                if u == 11:
                    out_lo(c, 0)
            norm(c, 1)
            out_lo(c, 1)
            self.tails(self.tail.dve, e, c)

        self.loop(e, body)


class Prep:

    NB = 2 * INTER // 512
    UP = HID ** -0.5
    DOWN = INTER ** -0.5

    def __init__(self, k, ins, pack):
        self.k, self.ins, self.pack = k, ins, pack
        k.kind = "prep_"
        self.s_load = Sem(k, "load")
        self.s_su = Sem(k, "su")
        self.s_mm = Sem(k, "mm")
        self.s_ev = Sem(k, "ev")
        self.s_bf = Sem(k, "bf")
        self.s_k = Sem(k, "k")
        self.s_out = Sem(k, "out")
        self.s_d = Sem(k, "d")
        new = Arena(k, "prep_").new
        self.ug, self.dn = new("ug", [P, KB, 2 * INTER]), new("dn", [P, FFN_TILES, HID])
        self.had = new("had", [P, P])
        self.su, self.sd = new("su", [P, KB]), new("sd", [P, FFN_TILES])
        self.cu, self.cd = new("cu", [P, 2 * INTER]), new("cd", [P, HID])
        self.t1 = new("t1", [P, 2, 512])
        self.sum = new("sum", [P, KB, 512])
        self.k2 = new("k2", [P, self.NB, KB, 512])
        self.d = [new(f"d{i}", [P, FFN_TILES, HID]) for i in range(2)]

    def sync(self, e):
        i = self.ins
        for dst, src in ((self.had[:], i["had"]), (self.ug[:], i["ffn_ug"]), (self.dn[:], i["ffn_dn"]),
                         (self.su[:], i["su_ug"]), (self.sd[:], i["su_dp"]),
                         (self.cu[:], i["c_ug"].partition_broadcast(P)),
                         (self.cd[:], i["c_dp"].partition_broadcast(P))):
            e.dma_start(dst, src).then_inc(self.s_load.sem, 16)
        for n in range(self.NB):
            self.s_k.wait(e, 2 * n + 2)
            for kb in range(KB):
                at = ((n // 2) * KB + kb) * P
                e.dma_start(self.pack[4 * (n % 2):4 * (n % 2) + 4, :, at:at + P].rearrange("t p f -> p t f"),
                            self.k2[:, n, kb, :].rearrange("p (t f) -> p t f", f=P)).then_inc(self.s_out.sem, 16)
        self.s_d.wait(e, 6 + FFN_TILES)
        e.dma_start(self.pack[:, :, 2 * KB * P:].rearrange("t p f -> p t f"), self.d[1][:]).then_inc(self.s_out.sem, 16)
        e.wait_ge(self.s_out.sem, 16 * (KB * self.NB + 1))

    def tensor(self, e):
        e.wait_ge(self.s_load.sem, 16 * 7)
        for n in range(self.NB):
            if n >= 2:
                self.s_bf.wait(e, 2 * n - 2)
            for kb in range(KB):
                m = e.matmul(self.k.psum[:, 2 * (n % 2) + kb, :], self.had[:],
                             self.ug[:, kb, n * 512:(n + 1) * 512], start=True, stop=True)
            m @ self.s_mm
        self.s_bf.wait(e, 2 * self.NB)
        for b in range(4):
            m = e.matmul(self.k.psum[:, b, :], self.had[:],
                         self.dn[:, 2 * b:2 * b + 2, :].rearrange("p a f -> p (a f)"), start=True, stop=True)
        m @ self.s_mm

    def scalar(self, e):
        for n in range(self.NB):
            self.s_mm.wait(e, n + 1)
            if n >= 2:
                self.s_bf.wait(e, 2 * n - 2)
            e.activation(self.t1[:, n % 2, :], self.k.psum[:, 2 * (n % 2) + 1, :], ACT.Copy) @ self.s_ev
        self.s_mm.wait(e, self.NB + 1)
        e.activation(self.d[0][:].rearrange("p (a b) f -> p a (b f)", a=4), self.k.psum[:, 0:4, :],
                     ACT.Copy) @ self.s_ev

    def vector(self, e):
        e.wait_ge(self.s_load.sem, 16 * 7)
        e.tensor_scalar(self.su[:], self.su[:], self.UP, None, ALU.mult) @ self.s_su
        e.tensor_scalar(self.sd[:], self.sd[:], self.DOWN, None, ALU.mult) @ self.s_su
        self.s_su.wait(e, 2)
        for n in range(self.NB):
            self.s_ev.wait(e, n + 1)
            self.s_k.wait(e, 2 * n)
            for kb, op in enumerate((ALU.add, ALU.subtract)):
                e.tensor_tensor(self.sum[:, kb, :], self.k.psum[:, 2 * (n % 2), :], self.t1[:, n % 2, :],
                                op) @ self.s_bf
            for kb in range(KB):
                self.s_bf.wait(e, 2 * n + kb + 1)
                e.scalar_tensor_tensor(self.k2[:, n, kb, :], self.sum[:, kb, :], self.su[:, kb:kb + 1],
                                       self.cu[:, n * 512:(n + 1) * 512], ALU.mult, ALU.mult) @ self.s_k
        self.s_ev.wait(e, self.NB + 1)
        for stage, h in enumerate((1, 2, 4)):
            a, b = (x[:].rearrange("p (n two h) f -> p n two (h f)", two=2, h=h)
                    for x in (self.d[stage % 2], self.d[(stage + 1) % 2]))
            self.s_d.wait(e, 2 * stage)
            e.tensor_tensor(b[:, :, 0, :], a[:, :, 0, :], a[:, :, 1, :], ALU.add) @ self.s_d
            e.tensor_tensor(b[:, :, 1, :], a[:, :, 0, :], a[:, :, 1, :], ALU.subtract) @ self.s_d
        self.s_d.wait(e, 6)
        for t in range(FFN_TILES):
            e.scalar_tensor_tensor(self.d[1][:, t, :], self.d[1][:, t, :], self.sd[:, t:t + 1], self.cd[:],
                                   ALU.mult, ALU.mult) @ self.s_d

    def pool(self, e):
        pass


def program(nc, ins, out, stages=6):
    with ExitStack() as ctx:
        k = Kern(nc, ctx)
        x = ins["x"].rearrange("b s f -> (b s) f")
        tails = [Tail(k, "t0_", entry=True, route=True)]
        pack = nc.dram_tensor("ffn_pack", [FFN_TILES, P, SwiGLU.WCOLS], F32, kind="Internal").ap()
        parts = [Prep(k, ins, pack), Entry(k, x, tails[0])]
        for n in range(1, stages + 1):
            tails.append(Tail(k, f"t{n}_", last=(n == stages), route=(n == 2 and n < stages)))
            tails[n].out = out.rearrange("b s f -> (b s) f")
            if n in (1, 3):
                parts.append(SwiGLU(k, f"moe{n}_", MOE_TILES // MOE_G, MOE_G, ins["moe_pack"],
                                    ins["gate_rows"], tails[n - 1], tails[n]))
            if n == 2:
                parts.append(Scan(k, "scan_", ins, tails[n - 1], tails[n]))
            if n in (4, 6):
                parts.append(SwiGLU(k, f"ffn{n}_", 1, FFN_TILES, pack, None, tails[n - 1], tails[n]))
            if n == 5:
                parts.append(Attention(k, "attn_", ins, tails[n - 1], tails[n]))

        block = ctx.enter_context(nc.Block())

        @block.sync
        def _(e):
            for s in k.credits:
                e.sem_inc(s.sem, s.base)
            e.dma_start(k.ident[:], ins["ident"]).then_inc(k.s_const.sem, 16)
            e.dma_start(k.gw[:], ins["gate_w"]).then_inc(k.s_const.sem, 16)
            for p in parts:
                p.sync(e)

        @block.gpsimd
        def _(e):
            e.memset(k.half[:], -0.5) @ k.s_half
            k.s_half.wait(e, 1)
            for p in parts:
                p.pool(e)

        @block.vector
        def _(e):
            e.memset(k.gate[0:32, :].bitcast(F32), 1.0) @ k.s_init
            e.memset(k.gate[32:64, :].bitcast(F32), 0.0) @ k.s_init
            e.wait_ge(k.s_const.sem, 32)
            e.tensor_copy(k.gwH[:], k.gw[:]) @ k.s_init
            k.s_init.wait(e, 3)
            e.tensor_tensor(k.gwL[:], k.gw[:], k.gwH[:].bitcast(F32), ALU.subtract) @ k.s_init
            for p in parts:
                p.vector(e)

        @block.scalar
        def _(e):
            k.s_init.wait(e, 4)
            for p in parts:
                p.scalar(e)

        @block.tensor
        def _(e):
            e.wait_ge(k.s_const.sem, 32)
            k.s_init.wait(e, 4)
            for p in parts:
                p.tensor(e)


def blocks(w, n=P):
    return w.reshape(-1, n, w.shape[-1]).transpose(1, 0, 2)


def layout(inputs):
    a = {n: np.asarray(v) for n, v in inputs.items()}
    f32 = np.float32
    out = {"x": a["L0_attn_x"], "ident": np.eye(P, dtype=f32)}
    out["gate_w"] = blocks(a["L0_ffn_gate_w"].T)
    w13, sw13 = a["L0_ffn_w13"], a["L0_ffn_sw13"]
    full = MOE_TILES * P
    parts = []
    for half in range(2):
        w = np.zeros((full, HID), f32)
        w[:NEXP * EINT] = w13[:, half * EINT:(half + 1) * EINT, :].reshape(-1, HID)
        w[NEXP * EINT:FEAT] = sw13[half * 2 * EINT:(half + 1) * 2 * EINT]
        parts.append(w.reshape(MOE_TILES, P, KB, P).transpose(0, 3, 2, 1).reshape(MOE_TILES, P, KB * P))
    d = np.zeros((full, HID), f32)
    d[:NEXP * EINT] = a["L0_ffn_w2"].transpose(0, 2, 1).reshape(-1, HID)
    d[NEXP * EINT:FEAT] = a["L0_ffn_sw2"].T
    parts.append(d.reshape(MOE_TILES, P, HID))
    out["moe_pack"] = np.concatenate(parts, axis=2)
    rows = np.zeros((full, 64), f32)
    f = np.arange(FEAT)
    expert = np.minimum(f // EINT, ONES_ROW)
    rows[f, expert] = 1.0
    routed = f[:NEXP * EINT]
    rows[routed, 32 + expert[routed]] = 1.0
    out["gate_rows"] = rows.reshape(MOE_TILES, P, 64).transpose(0, 2, 1)
    out["W_in"] = blocks(a["L0_attn_W_in"].T).reshape(P, -1)
    out["Wx"] = blocks(a["L0_attn_Wx"].T).reshape(P, -1)
    out["Wdt"] = a["L0_attn_Wdt"].T
    out["Wout"] = blocks(a["L0_attn_Wout"].T).reshape(P, -1)
    out["conv_w"] = blocks(a["L0_attn_conv_w"])
    for name in ("conv_b", "dt_bias", "D"):
        out[name] = a["L0_attn_" + name].reshape(-1, P).T
    out["A"] = blocks(a["L0_attn_A"])
    out["dt_ln"] = a["L0_attn_dt_ln_w"].reshape(P, 1)
    out["bc_ln"] = np.concatenate([a["L0_attn_b_ln_w"], a["L0_attn_c_ln_w"]]).reshape(2 * NST, 1)
    out["state_pick"] = np.tile(np.eye(2 * NST, dtype=f32), (2, 1))
    slot = (np.arange(HEADS)[:, None] * HSLOT + np.arange(HD)).ravel()
    pos = np.arange(HEADS) * HSLOT + HD
    for name in "qk":
        w = np.zeros((HID, HEADS * HSLOT), f32)
        w[:, slot] = a["L1_attn_W" + name]
        out["W" + name] = blocks(w).reshape(P, -1)
        b = np.zeros(HEADS * HSLOT, f32)
        b[slot] = a["L1_attn_b" + name]
        if name == "q":
            b[pos] = HD ** 0.5
        out["b" + name] = b.reshape(-1, P).T
    out["Wv"] = blocks(a["L1_attn_Wv"]).reshape(P, -1)
    out["Wo"] = blocks(a["L1_attn_Wo"]).reshape(P, -1)
    out["bv"] = a["L1_attn_bv"].reshape(-1, P).T
    out["bo"] = a["L1_attn_bo"].reshape(-1, P).T
    first = 2.0 ** (-2.0 ** -(np.log2(HEADS) - 3))
    slopes = np.array([first * first ** i for i in range(HEADS)], dtype=f32)
    pat = np.zeros((HEADS * HSLOT, SEQ), f32)
    pat[pos] = -slopes[:, None] * (SEQ - 1 - np.arange(SEQ, dtype=f32))[None, :]
    out["slopes"] = blocks(pat)
    mask = np.zeros((P, SEQ), f32)
    mask[:, P:] = np.where(np.arange(P)[None, :] > np.arange(P)[:, None], MASKED, 0.0)
    out["mask"] = mask
    had = np.ones((1, 1), f32)
    while had.shape[0] < P:
        had = np.block([[had, had], [had, -had]])
    out["had"] = had
    out["ffn_ug"] = blocks(np.concatenate([a["L1_ffn_W_gate"].T, a["L1_ffn_W_up"].T], axis=1))
    out["ffn_dn"] = blocks(a["L1_ffn_W_down"].T)
    out["su_ug"] = a["L1_ffn_SU_ug"].reshape(-1, P).T
    out["su_dp"] = a["L1_ffn_SU_dp"].reshape(-1, P).T
    out["c_ug"] = np.concatenate([a["L1_ffn_Wscale_ug"][INTER:], a["L1_ffn_Wscale_ug"][:INTER]])
    out["c_dp"] = a["L1_ffn_Wscale_dp"]
    return {n: np.ascontiguousarray(v, dtype=v.dtype) for n, v in out.items()}


def kernel(**inputs):
    import concourse.bacc as bacc
    from concourse.bass_utils import run_bass_kernel_spmd

    nc = bacc.Bacc("TRN2", target_bir_lowering=False, num_devices=1)
    arrays = layout(inputs)
    ins = {n: nc.dram_tensor(n, list(v.shape), mybir.dt.from_np(v.dtype), kind="ExternalInput").ap()
           for n, v in arrays.items()}
    out = nc.dram_tensor("out", [BATCH, SEQ, HID], F32, kind="ExternalOutput").ap()
    program(nc, ins, out)
    return run_bass_kernel_spmd(nc, [arrays], core_ids=[0]).results[0]["out"]
```

```python
from contextlib import ExitStack

import numpy as np

import concourse.bass as bass
from concourse import mybir

F32 = mybir.dt.float32
F32R = mybir.dt.float32r
ALU = mybir.AluOpType
ACT = mybir.ActivationFunctionType
AX_X = mybir.AxisListType.X

P = 128
BATCH, SEQ, HID = 8, 256, 256
TOK = BATCH * SEQ
TILES = TOK // P
CHUNK = 512
NCH = TOK // CHUNK
KB = HID // P
EPS = 1e-5

NEXP, TOPK, EINT = 16, 6, 176
FEAT = NEXP * EINT + 2 * EINT
MOE_TILES = -(-FEAT // P)
MOE_G = 5
ONES_ROW = NEXP
INTER = 1024
FFN_TILES = INTER // P
IN, NST, KCONV, RANK = 512, 16, 4, 128
IB = IN // P
XP = RANK + 2 * NST
HEADS, HD = 16, 16
HSLOT = 32
HGRP = P // HSLOT
NGRP = HEADS // HGRP
MASKED = -1e30


class Sem:

    def __init__(self, k, name, per=0, credit=0, passes=0, total=0):
        self.per, key = per, k.kind + name
        if key in k.used:
            self.sem, self.base = k.used[key]
        else:
            self.sem, self.base = k.ctx.enter_context(k.nc.semaphore(key)), credit
            if credit:
                k.credits.append(self)
        k.used[key] = self.sem, self.base + (total or passes * per)

    def wait(self, eng, count, it=0):
        v = it * self.per + (count + self.base)
        if isinstance(v, int) and v <= 0:
            return
        eng.wait_ge(self.sem, v)

    def __rmatmul__(self, ins):
        ins.then_inc(self.sem, 1)
        return ins


class Kern:

    def __init__(self, nc, ctx):
        self.nc, self.ctx, self.kind, self.credits, self.used = nc, ctx, "", [], {}
        self.base = 20480
        self.psum = ctx.enter_context(nc.psum_tensor("psum", [P, 8, 512], F32))
        self.X = self.keep("X", [P, TILES, HID])
        self.xH = self.keep("xnT_hi", [P, KB, TOK], F32R)
        self.xL = self.keep("xnT_lo", [P, KB, TOK], F32R)
        self.acc_at = self.base
        self.accT = self.keep("accT", [P, KB, TOK])
        self.gate = self.keep("gate_table", [64, TOK], F32R)
        self.ident = self.keep("ident", [P, P])
        self.xst = self.keep("x_stage", [P, 2, HID])
        self.st6 = self.keep("bn6", [P, 2, 6])
        self.mv = self.keep("mean_var", [P, 2, 2])
        self.rs = self.keep("rstd", [P, 2])
        self.half = self.keep("minus_half", [P, 16])
        self.gw = self.keep("gate_w_raw", [P, KB, NEXP])
        self.gwp = self.keep("gate_w_parts", [P, KB, 2 * NEXP], F32R)
        self.lgT = self.keep("logitsT_parts", [2 * NEXP, CHUNK])
        self.fold = self.keep("add_parts", [2 * NEXP, NEXP])
        self.lg = self.keep("logits", [P, 4, NEXP])
        self.ex = self.keep("exps", [P, 4, NEXP])
        self.mx = self.keep("top8", [P, 4, 8])
        self.rest = self.keep("not_chosen", [P, 4, NEXP])
        self.red = self.keep("row_stats", [P, 4])
        self.red2 = self.keep("row_stats2", [P, 4])
        self.s_const = Sem(self, "const")
        self.s_init = Sem(self, "init")
        self.s_half = Sem(self, "half")
        self.s_own = Sem(self, "own")
        self.arena = self.base

    def own(self, e):
        e.sem_inc(self.s_own.sem, 1)

    def at(self, name, shape, dt, off):
        return self.nc.alloc_sbuf_tensor_at(name, list(shape), dt, offset=off)

    def keep(self, name, shape, dt=F32):
        t = self.at(name, shape, dt, self.base)
        self.base += -(-4 * int(np.prod(shape[1:])) // 32) * 32
        return t


class Arena:

    def __init__(self, k, tag):
        self.k, self.tag, self.off = k, tag, k.arena

    def new(self, name, shape, dt=F32, over=None):
        off = self.off if over is None else over
        t = self.k.at(self.tag + name, shape, dt, off)
        end = off + -(-4 * int(np.prod(shape[1:])) // 32) * 32
        if over is None:
            self.off = end
        return t


def three(e, out, wH, wL, xH, xL, start, stop):
    e.matmul(out, wH, xH, start=start, stop=False)
    e.matmul(out, wH, xL, start=False, stop=False)
    return e.matmul(out, wL, xH, start=False, stop=stop)


class Tail:

    def __init__(self, k, tag, entry=False, last=False, route=False):
        self.k, self.entry, self.last, self.route = k, entry, last, route
        k.kind = "tail_"
        self.src_ready = None
        self.src = None
        if not entry:
            self.s_back = Sem(k, "back", 2, passes=NCH)
            self.s_add = Sem(k, "add", 2, credit=1, passes=NCH)
        if last:
            self.s_store = Sem(k, "store")
            return
        self.s_st = Sem(k, "bnst", 4, passes=NCH)
        self.s_ag = Sem(k, "bnag", 4, passes=NCH)
        self.s_ve = Sem(k, "vareps", 2, passes=NCH)
        self.s_rs = Sem(k, "rstd", 2, passes=NCH)
        self.s_xs = Sem(k, "xs", 2, passes=NCH)
        self.s_fw = Sem(k, "fw", 2, passes=NCH)
        self.s_xH = Sem(k, "xH", 2, credit=1, passes=NCH)
        self.s_xL = Sem(k, "xL", 2, credit=1, passes=NCH)
        if entry:
            self.s_in = [Sem(k, f"in{c}") for c in range(NCH)]
        if route:
            self.r_lgT = Sem(k, "r_lgT", 1, passes=NCH)
            self.r_lgTs = Sem(k, "r_lgTs", 1, passes=NCH)
            self.r_lg = Sem(k, "r_lg", 1, passes=NCH)
            self.r_v = Sem(k, "r_v", 16, passes=NCH)
            self.r_ex = Sem(k, "r_ex", 1, passes=NCH)
            self.r_cT = Sem(k, "r_cT", 1, passes=NCH)
            self.r_cH = Sem(k, "r_cH", 1, credit=1, passes=NCH)
            self.r_cL = Sem(k, "r_cL", 1, credit=1, passes=NCH)

    def bank(self):
        return self.k.psum[:, 7, :]

    def ready(self, e, c):
        self.s_xH.wait(e, 2, c)
        self.s_xL.wait(e, 2, c)
        if self.route:
            self.r_cH.wait(e, 1, c)
            self.r_cL.wait(e, 1, c)

    def idle(self, e, c):
        if self.last:
            return self.s_add.wait(e, 0, c)
        self.s_xH.wait(e, 0, c)
        self.s_xL.wait(e, 0, c)
        if self.route:
            self.r_cH.wait(e, 0, c)
            self.r_cL.wait(e, 0, c)

    def pe(self, e, c, slot):
        k, ptr, p = self.k, self.bank(), slot // 2
        if slot in (0, 2) and not self.entry:
            if slot == 0:
                self.src_ready.wait(e, 1, c)
            elif not self.last:
                self.s_xL.wait(e, 1, c)
            else:
                self.s_add.wait(e, 1, c)
            src = self.src(c)
            for j in range(2):
                for kb in range(KB):
                    m = e.transpose(ptr[:, j * 256 + kb * P:j * 256 + kb * P + P],
                                    src[:, kb, (2 * p + j) * P:(2 * p + j + 1) * P], k.ident[:])
            m @ self.s_back
        if slot in (1, 3) and not self.last:
            self.s_xs.wait(e, p + 1, c)
            for j in range(2):
                for kb in range(KB):
                    m = e.transpose(ptr[:, kb * 256 + j * P:kb * 256 + j * P + P],
                                    k.xst[:, j, kb * P:(kb + 1) * P], k.ident[:])
            m @ self.s_fw
        if slot == 4:
            self.s_xH.wait(e, 2, c)
            self.s_xL.wait(e, 2, c)
            k.own(e)
            n = 0
            for kb in range(KB):
                for x in (k.xH, k.xL):
                    n += 1
                    m = e.matmul(ptr[0:2 * NEXP, :], k.gwp[:, kb, :], x[:, kb, bass.ds(c * CHUNK, CHUNK)],
                                 start=(n == 1), stop=(n == 2 * KB))
            m @ self.r_lgT
        if slot == 5:
            self.r_lgTs.wait(e, 1, c)
            k.own(e)
            for j in range(4):
                m = e.matmul(ptr[:, j * NEXP:(j + 1) * NEXP], k.lgT[:, j * P:(j + 1) * P], k.fold[:],
                             start=True, stop=True)
            m @ self.r_lg
        if slot == 6:
            self.r_v.wait(e, 16, c)
            for j in range(4):
                m = e.transpose(ptr[0:NEXP, j * P:(j + 1) * P], k.lg[:, j, :], k.ident[:])
            m @ self.r_cT

    def act(self, e, c, slot):
        k, ptr, p = self.k, self.bank(), slot // 2
        if slot in (1, 3) and not self.last:
            self.s_fw.wait(e, p + 1, c)
            e.activation(k.xH[:, :, bass.ds(c * CHUNK + p * 256, 256)],
                         ptr.rearrange("p (k t) -> p k t", k=KB), ACT.Copy) @ self.s_xH
        if slot == 4:
            self.r_lgT.wait(e, 1, c)
            e.activation(k.lgT[:], ptr[0:2 * NEXP, :], ACT.Copy) @ self.r_lgTs
        if slot == 5:
            self.r_v.wait(e, 2, c)
            e.activation(k.ex[:], k.lg[:], ACT.Exp) @ self.r_ex
        if slot == 6:
            self.r_cT.wait(e, 1, c)
            e.activation(k.gate[0:NEXP, bass.ds(c * CHUNK, CHUNK)], ptr[0:NEXP, :], ACT.Copy) @ self.r_cH

    def sync(self, e):
        for c in range(NCH):
            self.s_add.wait(e, 2, c)
            e.dma_start(self.out[c * CHUNK:(c + 1) * CHUNK, :].rearrange("(n p) f -> p n f", p=P),
                        self.k.X[:, 4 * c:4 * c + 4, :]).then_inc(self.s_store.sem, 16)
        e.wait_ge(self.s_store.sem, 16 * NCH)

    def pool(self, e, c, slot):
        if slot in (0, 2) and not self.last:
            k, p = self.k, slot // 2
            self.s_ag.wait(e, 2 * p + 2, c)
            k.own(e)
            e.tensor_scalar(k.rs[:], k.mv[:, :, 1], EPS, None, ALU.add) @ self.s_ve
            self.s_ve.wait(e, p + 1, c)
            e.tensor_tensor(k.rs[:], k.rs[:], k.half[:, 0:2], ALU.pow) @ self.s_rs

    def add(self, e, c, p):
        rows = self.k.X[:, bass.ds(c * 4 + 2 * p, 2), :]
        if self.entry:
            self.s_in[c].wait(e, 16)
            return
        self.s_back.wait(e, p + 1, c)
        e.tensor_tensor(rows, rows, self.bank().rearrange("p (j f) -> p j f", j=2), ALU.add) @ self.s_add

    def stats(self, e, c, p):
        if self.last:
            return
        k = self.k
        if not self.entry:
            self.s_add.wait(e, p + 1, c)
        for j in range(2):
            if j == 0:
                k.own(e)
            e.bn_stats(k.st6[:, j, :], k.X[:, c * 4 + 2 * p + j, :]) @ self.s_st
        for j in range(2):
            self.s_st.wait(e, 2 * p + j + 1, c)
            k.own(e)
            e.bn_aggr(k.mv[:, j, :], k.st6[:, j, :]) @ self.s_ag

    def norm(self, e, c, p):
        if self.last:
            return
        k = self.k
        self.s_rs.wait(e, p + 1, c)
        for j in range(2):
            m = e.tensor_scalar(k.xst[:, j, :], k.X[:, c * 4 + 2 * p + j, :], k.mv[:, j, 0:1],
                                k.rs[:, j:j + 1], ALU.subtract, ALU.mult)
        m @ self.s_xs

    def low(self, e, c, p):
        if self.last:
            return
        k = self.k
        self.s_xH.wait(e, p + 1, c)
        cols = bass.ds(c * CHUNK + p * 256, 256)
        e.tensor_tensor(k.xL[:, :, cols], self.bank().rearrange("p (k t) -> p k t", k=KB),
                        k.xH[:, :, cols].bitcast(F32), ALU.subtract) @ self.s_xL

    def dve(self, e, c, slot):
        k, ptr, p = self.k, self.bank(), slot // 2
        if slot in (0, 2):
            self.add(e, c, p)
            self.stats(e, c, p)
            self.norm(e, c, p)
        if slot in (1, 3):
            self.low(e, c, p)
        if slot == 5:
            n = [0]

            def step(ins):
                ins @ self.r_v
                n[0] += 1
                self.r_v.wait(e, n[0], c)

            def over(x):
                return x[:].unsqueeze(2).broadcast_to([P, 4, NEXP])

            self.r_lg.wait(e, 1, c)
            logits = ptr[:, 0:4 * NEXP].rearrange("p (j x) -> p j x", j=4)
            step(e.tensor_reduce(k.red[:], logits, AX_X, ALU.max))
            step(e.tensor_tensor(k.lg[:], logits, over(k.red), ALU.subtract))
            self.r_ex.wait(e, 1, c)
            for j in range(4):
                k.own(e)
                step(e.max(k.mx[:, j, :], k.ex[:, j, :]))
            step(e.memset(k.mx[:, :, TOPK:8], -1.0))
            for j in range(4):
                k.own(e)
                e.match_replace(k.rest[:, j, :], k.mx[:, j, :], k.ex[:, j, :], 0.0) @ self.r_v
            n[0] = 11
            self.r_v.wait(e, 11, c)
            step(e.tensor_tensor(k.lg[:], k.ex[:], k.rest[:], ALU.subtract))
            step(e.tensor_reduce(k.red[:], k.lg[:], AX_X, ALU.add))
            step(e.tensor_scalar(k.red2[:], k.red[:], 1e-20, None, ALU.add))
            step(e.reciprocal(k.red[:], k.red2[:]))
            step(e.tensor_tensor(k.lg[:], k.lg[:], over(k.red), ALU.mult))
        if slot == 6:
            self.r_cH.wait(e, 1, c)
            cols = bass.ds(c * CHUNK, CHUNK)
            e.tensor_tensor(k.gate[32:32 + NEXP, cols], ptr[0:NEXP, :],
                            k.gate[0:NEXP, cols].bitcast(F32), ALU.subtract) @ self.r_cL


class SwiGLU:

    WCOLS = 2 * KB * P + HID

    def __init__(self, k, tag, groups, G, pack, rows, before, tail):
        self.k, self.NG, self.G, self.pack, self.rows = k, groups, G, pack, rows
        self.before, self.tail = before, tail
        k.kind = "glu_"
        S = NCH * G
        self.S = S
        self.s_raw = [Sem(k, f"raw{i}", 32 if rows is not None else 16, passes=groups) for i in range(G)]
        self.s_wH = Sem(k, "wH", G, passes=groups)
        self.s_wL = Sem(k, "wL", G, passes=groups)
        self.s_gu = Sem(k, "gu", S, passes=groups)
        self.s_cb = Sem(k, "cb", S, passes=groups)
        self.s_dn = Sem(k, "dn", S, credit=G, passes=groups)
        self.s_silu = Sem(k, "silu", S, passes=groups)
        self.s_hH = Sem(k, "hH", S, passes=groups)
        self.s_t = Sem(k, "t", S, credit=2, passes=groups)
        self.s_h = Sem(k, "h", S, passes=groups) if rows is not None else None
        self.s_hL = Sem(k, "hL", S, credit=2, passes=groups)
        self.s_acc = Sem(k, "acc", 4, credit=1, passes=groups)
        self.s_zero = Sem(k, "zero", total=1)
        tail.src_ready, tail.src = _Shifted(self.s_acc, 4 * (groups - 1)), \
            lambda c: k.accT[:, :, c * CHUNK:(c + 1) * CHUNK]
        a = Arena(k, tag)
        self.raw = a.new("w_raw", [P, G, self.WCOLS])
        self.raws = a.new("rows_raw", [64, G, P])
        self.wH = a.new("w_hi", [P, G, self.WCOLS], F32R)
        self.wL = a.new("w_lo", [P, G, self.WCOLS], F32R)
        self.rw = a.new("rows", [64, G, P], F32R)
        self.hb = a.new("hidden", [P, 2, CHUNK])
        self.hH = a.new("hidden_hi", [P, 2, CHUNK], F32R)
        self.hL = a.new("hidden_lo", [P, 2, CHUNK], F32R)

    def over_groups(self, e, step):
        if self.NG > 1:
            with e.Fori(0, self.NG - 1) as g:
                for s in range(self.S):
                    step(g, s, False)
        for s in range(self.S):
            step(self.NG - 1, s, True)

    def tails(self, fn, e, s, late=0):
        c, t = divmod(s, self.G)
        if c and late <= t < 4 + late:
            fn(e, c - 1, t - late)

    def after(self, fn, e):
        for slot in range(4):
            fn(e, NCH - 1, slot)
        if self.tail.route:
            for c in range(NCH):
                for slot in (4, 5, 6):
                    fn(e, c, slot)

    def sync(self, e):
        self.before.ready(e, NCH - 1)
        for t in range(self.G):
            e.dma_start(self.raw[:, t, :], self.pack[t]).then_inc(self.s_raw[t].sem, 16)
            if self.rows is not None:
                e.dma_start(self.raws[:, t, :], self.rows[t]).then_inc(self.s_raw[t].sem, 16)
        if self.NG > 1:
            with e.Fori(0, self.NG - 1) as g:
                for t in range(self.G):
                    self.s_wH.wait(e, t + 1, g)
                    self.s_wL.wait(e, t + 1, g)
                    nxt = g * self.G + (self.G + t)
                    e.dma_start(self.raw[:, t, :], self.pack[bass.ds(nxt, 1), :, :].rearrange("o p n -> (o p) n")).then_inc(self.s_raw[t].sem, 16)
                    if self.rows is not None:
                        e.dma_start(self.raws[:, t, :], self.rows[bass.ds(nxt, 1), :, :].rearrange("o p n -> (o p) n")).then_inc(self.s_raw[t].sem, 16)
        if self.tail.last:
            self.tail.sync(e)

    def pool(self, e):
        self.before.ready(e, NCH - 1)
        e.memset(self.k.accT[:], 0.0) @ self.s_zero
        for c in range(NCH):
            for slot in (0, 2):
                self.tail.pool(e, c, slot)

    def gu(self, e, g, s):
        c, t = divmod(s, self.G)
        k, b = self.k, 2 * (s % 2)
        if c == 0:
            self.s_wH.wait(e, t + 1, g)
            self.s_wL.wait(e, t + 1, g)
        self.s_t.wait(e, s - 1, g)
        cols = slice(c * CHUNK, (c + 1) * CHUNK)
        for half in range(2):
            for kb in range(KB):
                w = slice((half * KB + kb) * P, (half * KB + kb + 1) * P)
                m = three(e, k.psum[:, b + half, :], self.wH[:, t, w], self.wL[:, t, w],
                          k.xH[:, kb, cols], k.xL[:, kb, cols], kb == 0, kb == KB - 1)
        m @ self.s_gu

    def cb(self, e, g, s):
        if self.rows is None:
            return
        c, t = divmod(s, self.G)
        e.matmul(self.k.psum[:, 4, :], self.rw[:, t, :], self.k.gate[:, c * CHUNK:(c + 1) * CHUNK],
                 start=True, stop=True) @ self.s_cb

    def down(self, e, g, s):
        c, t = divmod(s, self.G)
        if t == 0:
            self.s_acc.wait(e, c, g)
        self.s_hH.wait(e, s + 1, g)
        self.s_hL.wait(e, s + 1, g)
        for ob in range(KB):
            w = slice(2 * KB * P + ob * P, 2 * KB * P + (ob + 1) * P)
            m = three(e, self.k.psum[:, 5 + ob, :], self.wH[:, t, w], self.wL[:, t, w],
                      self.hH[:, s % 2, :], self.hL[:, s % 2, :], t == 0, t == self.G - 1)
        m @ self.s_dn

    def tensor(self, e):
        for c in range(NCH):
            self.before.ready(e, c)
            if c == 0:
                self.gu(e, 0, 0)
                self.cb(e, 0, 0)

        def step(g, s, last):
            if s + 1 < self.S:
                self.gu(e, g, s + 1)
            elif not last:
                self.gu(e, g + 1, 0)
            self.down(e, g, s)
            if s + 1 < self.S:
                self.cb(e, g, s + 1)
            elif not last:
                self.cb(e, g + 1, 0)
            if last:
                self.tails(self.tail.pe, e, s)

        self.over_groups(e, step)
        self.after(self.tail.pe, e)

    def split_hi(self, e, g, t):
        self.s_raw[t].wait(e, self.s_raw[t].per, g)
        self.s_dn.wait(e, t + 1 - self.G, g)
        e.activation(self.wH[:, t, :], self.raw[:, t, :], ACT.Copy) @ self.s_wH

    def split_lo(self, e, g, t):
        if self.rows is not None:
            self.s_raw[t].wait(e, self.s_raw[t].per, g)
            self.s_dn.wait(e, t + 1 - self.G, g)
            e.tensor_copy(self.rw[:, t, :], self.raws[:, t, :])
        self.s_wH.wait(e, t + 1, g)
        e.tensor_tensor(self.wL[:, t, :], self.raw[:, t, :], self.wH[:, t, :].bitcast(F32),
                        ALU.subtract) @ self.s_wL

    def splits(self, fn, e, g, s, last):
        if s < self.G - 1:
            fn(e, g, s + 1)
        elif s == self.S - 1 and not last:
            fn(e, g + 1, 0)

    def scalar(self, e):
        self.before.ready(e, NCH - 1)
        self.split_hi(e, 0, 0)

        def step(g, s, last):
            b = s % 2
            self.splits(self.split_hi, e, g, s, last)
            self.s_gu.wait(e, s + 1, g)
            self.s_hL.wait(e, s - 1, g)
            e.activation(self.hb[:, b, :], self.k.psum[:, 2 * b, :], ACT.Silu) @ self.s_silu
            (self.s_h or self.s_t).wait(e, s + 1, g)
            self.s_dn.wait(e, s - 1, g)
            e.activation(self.hH[:, b, :], self.hb[:, b, :], ACT.Copy) @ self.s_hH
            if last:
                self.tails(self.tail.act, e, s, late=1)

        self.over_groups(e, step)
        self.after(self.tail.act, e)

    def vector(self, e):
        k = self.k
        self.before.ready(e, NCH - 1)
        self.split_lo(e, 0, 0)
        self.s_zero.wait(e, 1)

        def take(g, c):
            self.s_dn.wait(e, (c + 1) * self.G, g)
            cols = slice(c * CHUNK, (c + 1) * CHUNK)
            e.scalar_tensor_tensor(k.accT[:, :, cols], k.psum[:, 5:5 + KB, :], 0.5,
                                   k.accT[:, :, cols], ALU.mult, ALU.add) @ self.s_acc

        def step(g, s, last):
            b, (c, t) = s % 2, divmod(s, self.G)
            tail = self.tail if last and c and t < 5 else None
            self.splits(self.split_lo, e, g, s, last)
            self.s_silu.wait(e, s + 1, g)
            e.tensor_tensor(self.hb[:, b, :], self.hb[:, b, :], k.psum[:, 2 * b + 1, :],
                            ALU.mult) @ self.s_t
            if tail and t in (2, 4):
                tail.norm(e, c - 1, t // 2 - 1)
            if self.s_h:
                self.s_cb.wait(e, s + 1, g)
                self.s_t.wait(e, s + 1, g)
                e.tensor_tensor(self.hb[:, b, :], self.hb[:, b, :], k.psum[:, 4, :],
                                ALU.mult) @ self.s_h
            if c and t == 0:
                take(g, c - 1)
            if tail and t in (1, 3):
                tail.add(e, c - 1, t // 2)
            self.s_hH.wait(e, s + 1, g)
            self.s_dn.wait(e, s - 1, g)
            e.tensor_tensor(self.hL[:, b, :], self.hb[:, b, :], self.hH[:, b, :].bitcast(F32),
                            ALU.subtract) @ self.s_hL
            if tail and t in (1, 3):
                tail.stats(e, c - 1, t // 2)
            if tail and t in (2, 4):
                tail.low(e, c - 1, t // 2 - 1)
            if s == self.S - 1:
                take(g, NCH - 1)

        self.over_groups(e, step)
        self.after(self.tail.dve, e)


class _Shifted:

    def __init__(self, sem, shift):
        self.sem, self.shift = sem, shift

    def wait(self, eng, count, c):
        self.sem.wait(eng, self.shift + c + count)


class Entry:

    def __init__(self, k, x, tail):
        self.k, self.x, self.tail = k, x, tail

    def sync(self, e):
        for c in range(NCH):
            e.dma_start(self.k.X[:, 4 * c:4 * c + 4, :],
                        self.x[c * CHUNK:(c + 1) * CHUNK, :].rearrange("(n p) f -> p n f", p=P)
                        ).then_inc(self.tail.s_in[c].sem, 16)

    def run(self, e, fn):
        for c in range(NCH):
            for slot in range(7):
                fn(e, c, slot)

    def tensor(self, e):
        self.run(e, self.tail.pe)

    def scalar(self, e):
        self.run(e, self.tail.act)

    def vector(self, e):
        self.run(e, self.tail.dve)

    def pool(self, e):
        self.run(e, self.tail.pool)


class Scan:

    def __init__(self, k, tag, ins, before, tail):
        self.k, self.ins, self.before, self.tail = k, ins, before, tail
        k.kind = tag
        self.s_in = Sem(k, "in", 8)
        self.s_hp = Sem(k, "hp", 4)
        self.s_cv = Sem(k, "cv", 4)
        self.s_sg = Sem(k, "sg", 4)
        self.s_pad = Sem(k, "pad", 1)
        self.s_conv = Sem(k, "conv", 4)
        self.s_u = Sem(k, "u", 4)
        self.s_uh = Sem(k, "uh", 4)
        self.s_ul = Sem(k, "ul", 4)
        self.s_xp = Sem(k, "xp", 2)
        self.s_sq = Sem(k, "sq", 2)
        self.s_mm = Sem(k, "mm", 2)
        self.s_ln = Sem(k, "ln", 2)
        self.s_rt = Sem(k, "rt", 2)
        self.s_xw = Sem(k, "xw", 2)
        self.s_tsw = Sem(k, "tsw", 2)
        self.s_th = Sem(k, "th", 2)
        self.s_tsl = Sem(k, "tsl", 2)
        self.s_dt = Sem(k, "dt", 4)
        self.s_abs = Sem(k, "abs", 4)
        self.s_e = Sem(k, "e", 2)
        self.s_relu = Sem(k, "relu", 4)
        self.s_l = Sem(k, "l", 2)
        self.s_lost = Sem(k, "lost", 2)
        self.s_rc = Sem(k, "rc", 2)
        self.s_delta = Sem(k, "delta", 2)
        self.s_dtu = Sem(k, "dtu", 2)
        self.s_dz = Sem(k, "dz", 1)
        self.s_bB = Sem(k, "bB", NST)
        self.s_bC = Sem(k, "bC", NST)
        self.s_bs = Sem(k, "bs", NST)
        self.s_dA = Sem(k, "dA", NST)
        self.s_m0 = Sem(k, "m0", 1)
        self.s_m1 = Sem(k, "m1", NST - 1)
        self.s_scan = Sem(k, "scan", NST)
        self.s_z = Sem(k, "z", NST - 1)
        self.s_zb = Sem(k, "zb", IB)
        self.s_y = Sem(k, "y", NST - 1)
        self.s_yb = Sem(k, "yb", IB)
        self.s_yg = Sem(k, "yg", IB)
        self.s_yh = Sem(k, "yh", IB)
        self.s_yl = Sem(k, "yl", IB)
        self.s_o = Sem(k, "o", 1)
        self.s_fin = Sem(k, "fin", 1)
        self.s_v = Sem(k, "v", 14)
        self.s_load = Sem(k, "load")
        self.s_wh, self.s_wl = Sem(k, "wh"), Sem(k, "wl")
        self.s_one = Sem(k, "one")
        tail.src_ready, tail.src = self.s_fin, lambda c: self.fin
        a = Arena(k, tag)
        new = a.new
        self.wcols = [KB * 2 * IN, IB * XP, IN, IB * HID]
        total = sum(self.wcols)
        self.wH, self.wL = new("w_hi", [P, total], F32R), new("w_lo", [P, total], F32R)
        self.u = new("u", [P, IB, CHUNK])
        self.sg = new("silu_gate", [P, IB, CHUNK])
        at = a.off
        self.delta = new("delta", [P, IB, CHUNK])
        self.dtu = new("delta_u", [P, IB, CHUNK])
        self.hpad = new("conv_in", [P, IB, 2, SEQ + KCONV - 1], over=at)
        at = a.off
        self.dA = new("decay", [P, 2, IB, CHUNK])
        small = Arena(k, tag)
        small.off = at
        self.sq = [small.new(f"squares{i}", [n, CHUNK]) for i, n in enumerate(self.NORM)]
        self.rt = [small.new(f"rms_inv{i}", [n, CHUNK]) for i, n in enumerate(self.NORM)]
        self.wt = [small.new(f"weighted{i}", [n, CHUNK]) for i, n in enumerate(self.NORM)]
        self.tsH = small.new("ts_hi", [P, CHUNK], F32R)
        self.tsL = small.new("ts_lo", [P, CHUNK], F32R)
        assert small.off <= a.off
        at = a.off
        self.st = [new(f"state{i}", [P, IB, CHUNK]) for i in range(self.NBUF)]
        self.raw = new("w_raw", [P, total], over=at)
        self.Bs = new("B_all", [P, 2, CHUNK])
        self.bc = new("BC", [64, CHUNK], F32R)
        self.fin = new("out", [P, KB, CHUNK])
        self.cw, self.cb = new("conv_w", [P, IB, KCONV]), new("conv_b", [P, IB])
        self.lnw = [new("dt_ln", [P, 1]), new("bc_ln", [2 * NST, 1])]
        self.mean = [new("mean_ts", [P, P]), new("mean_bc", [2 * NST, 2 * NST])]
        self.eps = new("eps", [P, 1])
        self.dtb, self.A, self.D = new("dt_bias", [P, IB]), new("A", [P, IB, NST]), new("D", [P, IB])
        self.eye = new("state_pick_raw", [64, 2 * NST])
        self.pick = new("state_pick", [64, 2 * NST], F32R)
        assert a.off <= k.nc.sbuf_usable_end, a.off
        acc = Arena(k, tag)
        acc.off = k.acc_at
        self.uH, self.uL = acc.new("u_hi", [P, IB, CHUNK], F32R), acc.new("u_lo", [P, IB, CHUNK], F32R)

    NBUF = 4
    NORM = (RANK, 2 * NST)

    def weight(self, n, cols):
        at = sum(self.wcols[:n])
        s = slice(at + cols.start, at + cols.stop)
        return self.wH[:, s], self.wL[:, s]

    def run(self, e, pre, main, fn):
        slots = 7 if self.tail.route else 4

        def tail_of(c):
            return lambda a, b: [fn(e, c, slot) for slot in range(a, min(b, slots))]

        pre(0, lambda a, b: None)
        with e.Fori(0, NCH - 1) as c:
            main(c, True)
            pre(c + 1, tail_of(c))
        main(NCH - 1, False)
        tail_of(NCH - 1)(0, 7)

    def sync(self, e):
        self.before.ready(e, NCH - 1)
        i = self.ins
        at = 0
        for w, n in zip(("W_in", "Wx", "Wdt", "Wout"), self.wcols):
            e.dma_start(self.raw[:, at:at + n], i[w]).then_inc(self.s_load.sem, 16)
            at += n
        for dst, name in ((self.cw, "conv_w"), (self.cb, "conv_b"), (self.lnw[0], "dt_ln"),
                          (self.lnw[1], "bc_ln"), (self.dtb, "dt_bias"), (self.A, "A"), (self.D, "D"),
                          (self.eye, "state_pick"), (self.mean[1], "mean_bc")):
            e.dma_start(dst[:], i[name]).then_inc(self.s_load.sem, 16)
        if self.tail.last:
            self.tail.sync(e)

    def pool(self, e):
        k = self.k
        self.before.ready(e, NCH - 1)
        e.memset(self.mean[0][:], 1.0 / RANK) @ self.s_one
        e.memset(self.eps[:], EPS) @ self.s_one

        def pre(c, tail):
            self.s_scan.wait(e, 0, c)
            k.own(e)
            e.memset(self.hpad[:, :, :, 0:KCONV - 1], 0.0) @ self.s_pad
            tail(0, 4)
            tail(4, 7)
            self.s_dt.wait(e, 4, c)
            self.s_tsl.wait(e, 2, c)
            k.own(e)
            e.memset(self.dA[:].rearrange("p a b (s t) -> p (a b s) t", t=SEQ)[:, :, 0], 0.0) @ self.s_dz
            for h in range(2):
                m = slice(2 * h, 2 * h + 2)
                self.s_relu.wait(e, 2 * h + 2, c)
                self.s_lost.wait(e, h + 1, c)
                e.tensor_tensor(self.delta[:, m, :], self.delta[:, m, :], self.st[2][:, m, :],
                                ALU.add) @ self.s_rc

        def main(c, more):
            self.s_dtu.wait(e, 2, c)
            for n in range(1, NST):
                self.s_bs.wait(e, n + 1, c)
                if n >= self.NBUF:
                    self.s_y.wait(e, n - self.NBUF + 1, c)
                e.tensor_tensor(self.st[n % self.NBUF][:], self.dtu[:],
                                self.Bs[:, n % 2, :].unsqueeze(1).broadcast_to([P, IB, CHUNK]),
                                ALU.mult) @ self.s_m1

        self.run(e, pre, main, self.tail.pool)

    def tensor(self, e):
        k, ps = self.k, self.k.psum
        self.before.ready(e, NCH - 1)
        self.s_wl.wait(e, 1)
        self.s_one.wait(e, 2)

        def project(c, m, bank):
            cols = bass.ds(c * CHUNK, CHUNK)
            for kb in range(KB):
                w = self.weight(0, slice(kb * 2 * IN + m * P, kb * 2 * IN + (m + 1) * P))
                x = three(e, ps[:, bank, :], *w, k.xH[:, kb, cols], k.xL[:, kb, cols], kb == 0, kb == KB - 1)
            x @ self.s_in

        def x_proj(c, ib, rows=(0, 1)):
            self.s_ul.wait(e, ib + 1, c)
            for i in rows:
                a, n = ((0, RANK), (RANK, 2 * NST))[i]
                w = self.weight(1, slice(ib * XP + a, ib * XP + a + n))
                x = three(e, ps[0:n, i, :], *w, self.uH[:, ib, :], self.uL[:, ib, :], ib == 0, ib == IB - 1)
                if ib == IB - 1:
                    x @ self.s_xp

        def bcast(c, n, part):
            x = e.matmul(ps[:, 4 + 2 * (n % 2) + part, :],
                         self.pick[:, part * NST + n:part * NST + n + 1].broadcast_to([64, P]), self.bc[:],
                         start=True, stop=True)
            x @ (self.s_bC if part else self.s_bB)

        def pre(c, tail):
            tail(0, 1)
            for m in range(3):
                project(c, IB + m, IB + m)
            tail(1, 2)
            self.s_cv.wait(e, 2, c)
            x_proj(c, 0)
            tail(2, 3)
            self.s_sg.wait(e, 1, c)
            project(c, IB + 3, 4)
            x_proj(c, 1)
            tail(3, 4)
            x_proj(c, 2)
            tail(4, 5)
            x_proj(c, 3, (0,))
            tail(5, 6)
            x_proj(c, 3, (1,))
            self.s_cv.wait(e, 4, c)
            for i, n in enumerate(self.NORM):
                self.s_sq.wait(e, i + 1, c)
                k.own(e)
                e.matmul(ps[0:n, 2 + i, :], self.mean[i][:], self.sq[i][:], start=True, stop=True) @ self.s_mm
            tail(6, 7)
            self.s_xw.wait(e, 2, c)
            self.s_ln.wait(e, 2, c)
            self.s_tsl.wait(e, 1, c)
            for m in range(IB):
                w = self.weight(2, slice(m * P, (m + 1) * P))
                three(e, ps[:, m, :], *w, self.tsH[:], self.tsL[:], True, True) @ self.s_dt
            self.s_th.wait(e, 2, c)
            self.s_tsl.wait(e, 2, c)
            self.s_sg.wait(e, 4, c)
            bcast(c, 0, 0)
            bcast(c, 0, 1)
            bcast(c, 1, 0)
            self.s_bs.wait(e, 1, c)
            bcast(c, 2, 0)

        def main(c, more):
            self.tail.idle(e, c)
            bcast(c, 1, 1)
            self.s_e.wait(e, 2, c)
            self.s_relu.wait(e, 4, c)
            for n in range(NST):
                if n + 3 < NST:
                    self.s_bs.wait(e, n + 2, c)
                    bcast(c, n + 3, 0)
                last = n == NST - 1
                if not last:
                    self.s_z.wait(e, n + 1, c)
                for m in range(IB):
                    if last:
                        self.s_zb.wait(e, m + 1, c)
                    x = e.matmul(ps[:, m, :], k.ident[:], self.st[n % self.NBUF][:, m, :], start=(n == 0), stop=last)
                    if last:
                        x @ self.s_yb
                if not last:
                    x @ self.s_y
                if n + 2 < NST:
                    bcast(c, n + 2, 1)
            for ib in range(IB):
                self.s_yl.wait(e, ib + 1, c)
                for ob in range(KB):
                    w = self.weight(3, slice(ib * HID + ob * P, ib * HID + (ob + 1) * P))
                    x = three(e, ps[:, 4 + ob, :], *w, self.uH[:, ib, :], self.uL[:, ib, :],
                              ib == 0, ib == IB - 1)
                if ib == IB - 1:
                    x @ self.s_o
                if more:
                    project(c + 1, ib, ib)

        for m in range(IB):
            project(0, m, m)
        self.run(e, pre, main, self.tail.pe)

    def scalar(self, e):
        k, ps = self.k, self.k.psum
        self.before.ready(e, NCH - 1)
        e.wait_ge(self.s_load.sem, 16 * 13)
        e.activation(self.wH[:], self.raw[:], ACT.Copy) @ self.s_wh
        self.s_one.wait(e, 2)

        def high(c, m):
            self.s_conv.wait(e, m + 1, c)
            e.activation(self.u[:, m, :], self.u[:, m, :], ACT.Silu) @ self.s_u
            self.s_u.wait(e, m + 1, c)
            e.activation(self.uH[:, m, :], self.u[:, m, :], ACT.Copy) @ self.s_uh

        def gate(c, m, bank):
            self.s_in.wait(e, IB + m + 1, c)
            e.activation(self.sg[:, m, :], ps[:, bank, :], ACT.Silu) @ self.s_sg

        def conv_in(c, m):
            if m == 0:
                self.s_pad.wait(e, 1, c)
            self.s_in.wait(e, m + 1, c)
            e.activation(self.hpad[:, m, :, KCONV - 1:], ps[:, m, :].rearrange("p (s t) -> p s t", s=2),
                         ACT.Copy) @ self.s_hp
            e.activation(self.u[:, m, :], ps[:, m, :], ACT.Identity, bias=self.cb[:, m:m + 1],
                         scale=self.cw[:, m, KCONV - 1:KCONV]) @ self.s_cv

        def pre(c, tail):
            gate(c, 0, 4)
            high(c, 0)
            tail(0, 2)
            gate(c, 1, 5)
            high(c, 1)
            gate(c, 2, 6)
            high(c, 2)
            tail(2, 4)
            gate(c, 3, 4)
            high(c, 3)
            tail(4, 6)
            for i, n in enumerate(self.NORM):
                self.s_xp.wait(e, i + 1, c)
                e.activation(self.sq[i][:], ps[0:n, i, :], ACT.Square) @ self.s_sq
            for i, n in enumerate(self.NORM):
                self.s_mm.wait(e, i + 1, c)
                e.activation(self.rt[i][:], ps[0:n, 2 + i, :], ACT.Ln, bias=self.eps[0:n, :]) @ self.s_ln
            for i in range(2):
                self.s_ln.wait(e, i + 1, c)
                e.activation(self.rt[i][:], self.rt[i][:], ACT.Exp, scale=-0.5) @ self.s_rt
            for i, n in enumerate(self.NORM):
                e.activation(self.wt[i][:], ps[0:n, i, :], ACT.Copy, scale=self.lnw[i][:]) @ self.s_xw
            for i, dst in enumerate((self.tsH[:], self.bc[0:2 * NST, :])):
                self.s_tsw.wait(e, i + 1, c)
                e.activation(dst, self.wt[i][:], ACT.Copy) @ self.s_th
            tail(6, 7)
            ax, ln = self.st[0], self.st[1]
            for m in range(IB):
                self.s_dt.wait(e, m + 1, c)
                e.activation(ax[:, m, :], ps[:, m, :], ACT.Abs, bias=self.dtb[:, m:m + 1]) @ self.s_abs
            for h in range(2):
                m = slice(2 * h, 2 * h + 2)
                self.s_abs.wait(e, 2 * h + 2, c)
                e.activation(ax[:, m, :], ax[:, m, :], ACT.Exp, scale=-1.0) @ self.s_e
            for h in range(2):
                m = slice(2 * h, 2 * h + 2)
                self.s_e.wait(e, h + 1, c)
                e.activation(ln[:, m, :], ax[:, m, :], ACT.Ln, bias=1.0) @ self.s_l
            for n in range(2):
                keep_b(c, n)

        def keep_b(c, n):
            self.s_bB.wait(e, n + 1, c)
            if n == 2:
                self.s_m0.wait(e, 1, c)
            if n >= 3:
                self.s_m1.wait(e, n - 2, c)
            e.activation(self.Bs[:, n % 2, :], ps[:, 4 + 2 * (n % 2), :], ACT.Copy) @ self.s_bs

        def main(c, more):
            self.s_dz.wait(e, 1, c)
            for n in range(NST):
                if n >= 2:
                    keep_b(c, n)
                if n >= 2:
                    self.s_scan.wait(e, n - 1, c)
                for m in range(IB):
                    if n == 0 and m % 2 == 0:
                        self.s_delta.wait(e, m // 2 + 1, c)
                    x = e.activation(
                        self.dA[:, n % 2, m, :].rearrange("p (s t) -> p s t", s=2)[:, :, 1:],
                        self.delta[:, m, :].rearrange("p (s t) -> p s t", s=2)[:, :, 1:],
                        ACT.Exp, scale=self.A[:, m, n:n + 1])
                x @ self.s_dA
            for m in range(IB):
                self.s_yg.wait(e, m + 1, c)
                e.activation(self.uH[:, m, :], self.u[:, m, :], ACT.Copy) @ self.s_yh
                if more and m:
                    conv_in(c + 1, m - 1)
            self.s_o.wait(e, 1, c)
            e.activation(self.fin[:], ps[:, 4:6, :], ACT.Copy) @ self.s_fin
            if more:
                conv_in(c + 1, IB - 1)

        for m in range(IB):
            conv_in(0, m)
        self.run(e, pre, main, self.tail.act)

    def vector(self, e):
        k, ps = self.k, self.k.psum
        self.before.ready(e, NCH - 1)
        e.wait_ge(self.s_load.sem, 16 * 13)
        e.tensor_copy(self.pick[:], self.eye[:])
        self.s_wh.wait(e, 1)
        e.tensor_tensor(self.wL[:], self.raw[:], self.wH[:].bitcast(F32), ALU.subtract) @ self.s_wl
        self.s_wl.wait(e, 1)

        def low(c, m, high, sem):
            high.wait(e, m + 1, c)
            e.tensor_tensor(self.uL[:, m, :], self.u[:, m, :], self.uH[:, m, :].bitcast(F32),
                            ALU.subtract) @ sem

        def conv(c, m):
            self.s_cv.wait(e, m + 1, c)
            self.s_hp.wait(e, m + 1, c)
            um = self.u[:, m, :].rearrange("p (s t) -> p s t", s=2)
            for tap in range(KCONV - 1):
                last = tap == KCONV - 2
                e.scalar_tensor_tensor(um, self.hpad[:, m, :, tap:tap + SEQ], self.cw[:, m, tap:tap + 1],
                                       um, ALU.mult, ALU.add) @ (self.s_conv if last else self.s_v)
                if not last:
                    self.s_v.wait(e, 2 * m + tap + 1, c)

        def pre(c, tail):
            conv(c, 0)
            conv(c, 1)
            tail(0, 1)
            low(c, 0, self.s_uh, self.s_ul)
            tail(1, 2)
            conv(c, 2)
            low(c, 1, self.s_uh, self.s_ul)
            tail(2, 3)
            conv(c, 3)
            low(c, 2, self.s_uh, self.s_ul)
            tail(3, 4)
            low(c, 3, self.s_uh, self.s_ul)
            tail(4, 6)
            for i in range(2):
                self.s_rt.wait(e, i + 1, c)
                self.s_xw.wait(e, i + 1, c)
                e.tensor_tensor(self.wt[i][:], self.wt[i][:], self.rt[i][:], ALU.mult) @ self.s_tsw
            for i, (lo, hi) in enumerate(((self.tsL[:], self.tsH[:]),
                                          (self.bc[32:32 + 2 * NST, :], self.bc[0:2 * NST, :]))):
                self.s_th.wait(e, i + 1, c)
                e.tensor_tensor(lo, self.wt[i][:], hi.bitcast(F32), ALU.subtract) @ self.s_tsl
            tail(6, 7)
            for m in range(IB):
                self.s_abs.wait(e, m + 1, c)
                e.tensor_scalar(self.delta[:, m, :], ps[:, m, :], self.dtb[:, m:m + 1], 0.0, ALU.add,
                                ALU.max) @ self.s_relu
            ax, ln, t = self.st[:3]
            for h in range(2):
                m = slice(2 * h, 2 * h + 2)
                self.s_e.wait(e, h + 1, c)
                e.tensor_scalar(t[:, m, :], ax[:, m, :], 1.0, 1.0, ALU.add, ALU.subtract) @ self.s_v
                self.s_v.wait(e, 8 + h + 1, c)
                e.tensor_tensor(t[:, m, :], ax[:, m, :], t[:, m, :], ALU.subtract) @ self.s_lost
            for h in range(2):
                m = slice(2 * h, 2 * h + 2)
                self.s_l.wait(e, h + 1, c)
                self.s_rc.wait(e, h + 1, c)
                e.tensor_tensor(self.delta[:, m, :], self.delta[:, m, :], ln[:, m, :], ALU.add) @ self.s_delta
                self.s_delta.wait(e, h + 1, c)
                e.tensor_tensor(self.dtu[:, m, :], self.delta[:, m, :], self.u[:, m, :], ALU.mult) @ self.s_dtu

        def flat(x):
            return x.rearrange("p m t -> p (m t)")

        def main(c, more):
            self.s_dtu.wait(e, 2, c)
            self.s_bs.wait(e, 1, c)
            e.tensor_tensor(self.st[0][:], self.dtu[:],
                            self.Bs[:, 0, :].unsqueeze(1).broadcast_to([P, IB, CHUNK]), ALU.mult) @ self.s_m0
            self.s_m0.wait(e, 1, c)
            for n in range(NST):
                st, cb = self.st[n % self.NBUF], ps[:, 5 + 2 * (n % 2), :]
                self.s_dA.wait(e, n + 1, c)
                if n:
                    self.s_m1.wait(e, n, c)
                s = flat(st[:])
                e.tensor_tensor_scan(s, flat(self.dA[:, n % 2, :, :]), s, 0.0, ALU.mult, ALU.add) @ self.s_scan
                self.s_scan.wait(e, n + 1, c)
                self.s_bC.wait(e, n + 1, c)
                if n < NST - 1:
                    e.tensor_tensor(st[:], st[:], cb.unsqueeze(1).broadcast_to([P, IB, CHUNK]),
                                    ALU.mult) @ self.s_z
                else:
                    for m in range(IB):
                        e.tensor_tensor(st[:, m, :], st[:, m, :], cb, ALU.mult) @ self.s_zb
            for m in range(IB):
                self.s_yb.wait(e, m + 1, c)
                e.scalar_tensor_tensor(self.u[:, m, :], self.u[:, m, :], self.D[:, m:m + 1],
                                       ps[:, m, :], ALU.mult, ALU.add) @ self.s_v
                self.s_v.wait(e, 10 + m + 1, c)
                e.tensor_tensor(self.u[:, m, :], self.u[:, m, :], self.sg[:, m, :], ALU.mult) @ self.s_yg
                if m:
                    low(c, m - 1, self.s_yh, self.s_yl)
            low(c, IB - 1, self.s_yh, self.s_yl)

        self.run(e, pre, main, self.tail.dve)


class Attention:

    UNITS = 16

    def __init__(self, k, tag, ins, before, tail):
        self.k, self.ins, self.before, self.tail = k, ins, before, tail
        k.kind = tag
        U = self.UNITS
        self.s_in = Sem(k, "in", 8)
        self.s_q = Sem(k, "q", 4)
        self.s_k = Sem(k, "k", 4)
        self.s_vT = Sem(k, "vT", 2)
        self.s_vTs = Sem(k, "vTs", 2)
        self.s_vt = Sem(k, "vt", 1)
        self.s_v = Sem(k, "v", 2)
        self.s_S = Sem(k, "S", U)
        self.s_max = Sem(k, "max", U)
        self.s_nm = Sem(k, "nm", U)
        self.s_exp = Sem(k, "exp", U)
        self.s_T = Sem(k, "T", U)
        self.s_pt = Sem(k, "pt", U)
        self.s_pv = Sem(k, "pv", U)
        self.s_rec = Sem(k, "rec", U)
        self.s_pn = Sem(k, "pn", U)
        self.s_oH = Sem(k, "oH", 4)
        self.s_oL = Sem(k, "oL", 4)
        self.s_o = Sem(k, "o", 1)
        self.s_fin = Sem(k, "fin", 1)
        self.s_vz = Sem(k, "vz")
        self.s_load, self.s_wh, self.s_wl = Sem(k, "load"), Sem(k, "wh"), Sem(k, "wl")
        tail.src_ready, tail.src = self.s_fin, lambda c: self.fin
        new = Arena(k, tag).new
        self.wcols = [KB * NGRP * P, KB * NGRP * P, KB * HID, NGRP * HID]
        total = sum(self.wcols)
        self.raw = new("w_raw", [P, total])
        self.wH, self.wL = new("w_hi", [P, total], F32R), new("w_lo", [P, total], F32R)
        self.q, self.kk = new("q", [P, NGRP, CHUNK]), new("k", [P, NGRP, CHUNK])
        self.vT, self.v = new("vT", [P, KB, CHUNK]), new("v", [P, 4, HEADS, HSLOT])
        self.p0, self.p1 = new("p0", [P, 3, 2, P]), new("p1", [P, 3, 2, SEQ])
        self.pt = new("pT", [P, 2, 2, 3 * P])
        self.mx, self.nm = new("max", [P, 3, 4]), new("neg_max", [P, 3, 4])
        self.sums, self.rec = new("sums", [P, 3, 4]), new("recip", [P, 3, 4])
        self.oH, self.oL = new("o_hi", [P, NGRP, CHUNK], F32R), new("o_lo", [P, NGRP, CHUNK], F32R)
        self.fin = new("out", [P, KB, CHUNK])
        self.pat = new("slopes", [P, NGRP, SEQ])
        self.mraw, self.mask = new("mask_raw", [P, P]), new("mask", [P, P], F32R)
        self.one = new("ident_r", [P, P], F32R)
        self.bq, self.bk = new("bq", [P, NGRP]), new("bk", [P, NGRP])
        self.bv, self.bo = new("bv", [P, KB]), new("bo", [P, KB])
        self.bqs = new("bq_scaled", [P, NGRP])

    weight, run = Scan.weight, Scan.run

    def sync(self, e):
        self.before.ready(e, NCH - 1)
        i, at = self.ins, 0
        for w, n in zip(("Wq", "Wk", "Wv", "Wo"), self.wcols):
            e.dma_start(self.raw[:, at:at + n], i[w]).then_inc(self.s_load.sem, 16)
            at += n
        for dst, name in ((self.pat, "slopes"), (self.mraw, "mask"), (self.bq, "bq"), (self.bk, "bk"),
                          (self.bv, "bv"), (self.bo, "bo")):
            e.dma_start(dst[:], i[name]).then_inc(self.s_load.sem, 16)
        if self.tail.last:
            self.tail.sync(e)

    def pool(self, e):
        self.before.ready(e, NCH - 1)
        e.memset(self.v[:], 0.0) @ self.s_vz

        self.run(e, lambda c, tail: tail(0, 4), lambda c, more: None, self.tail.pool)

    @staticmethod
    def unit(u):
        b, i = divmod(u, 8)
        r, gg = i % HGRP, i // HGRP
        return b, HSLOT * r, [(g * HGRP + r, g) for g in (2 * gg, 2 * gg + 1)]

    def tensor(self, e):
        k, ps = self.k, self.k.psum
        self.before.ready(e, NCH - 1)
        self.s_wl.wait(e, 1)

        def scores(c, u):
            b, r, heads = self.unit(u)
            s = 2 * (u % 2)
            if u >= 2:
                self.s_exp.wait(e, u - 1, c)
            for j in range(2):
                n = (j + 1) * P
                for x, (h, g) in enumerate(heads):
                    e.matmul(ps[:, s + j, x * n:(x + 1) * n],
                             self.q[r:r + HSLOT, g, b * SEQ + j * P:b * SEQ + (j + 1) * P],
                             self.kk[r:r + HSLOT, g, b * SEQ:b * SEQ + n], start=True, stop=False)
                    m = e.matmul(ps[:, s + j, (x + 1) * n - P:(x + 1) * n], self.one[:], self.mask[:],
                                 start=False, stop=True)
            m @ self.s_S

        def turn(c, u):
            self.s_pn.wait(e, u + 1, c)
            if u:
                self.s_pt.wait(e, u, c)
            for x in range(2):
                for n, block in enumerate((self.p0[:, u % 3, x, :], self.p1[:, u % 3, x, 0:P],
                                           self.p1[:, u % 3, x, P:])):
                    m = e.transpose(ps[:, 4 + x, n * P:(n + 1) * P], block, k.ident[:])
            m @ self.s_T

        def values(c, u):
            b, r, heads = self.unit(u)
            bank = 6 + (u % 8) // 4
            self.s_pt.wait(e, u + 1, c)
            if u >= 8 and u % 4 == 0:
                self.s_oL.wait(e, u // 4 - 1, c)
            for x, (h, g) in enumerate(heads):
                pt = self.pt[:, u % 2, x, :]
                e.matmul(ps[r:r + HSLOT, bank, x * SEQ:(x + 1) * SEQ], self.v[:, 2 * b, h, :],
                         pt[:, 0:SEQ], start=True, stop=False)
                m = e.matmul(ps[r:r + HSLOT, bank, x * SEQ + P:(x + 1) * SEQ], self.v[:, 2 * b + 1, h, :],
                             pt[:, SEQ:], start=False, stop=True)
            m @ self.s_pv

        def project(c, which, block, bank, sem):
            cols = bass.ds(c * CHUNK, CHUNK)
            for kb in range(KB):
                n = self.wcols[which] // KB
                w = self.weight(which, slice(kb * n + block * P, kb * n + (block + 1) * P))
                x = three(e, ps[:, bank, :], *w, k.xH[:, kb, cols], k.xL[:, kb, cols], kb == 0, kb == KB - 1)
            x @ sem

        def queries(c, blocks):
            for g in blocks:
                project(c, 0, g, g, self.s_in)

        def keys(c, g):
            if g:
                self.s_q.wait(e, g, c)
            project(c, 1, g, (6, 0, 1, 2)[g], self.s_in)

        def pre(c, tail):
            tail(0, 1)
            keys(c, 0)
            keys(c, 1)
            tail(1, 2)
            keys(c, 2)
            tail(2, 3)
            keys(c, 3)
            self.s_q.wait(e, 4, c)
            project(c, 2, 0, 3, self.s_vT)
            tail(3, 4)
            project(c, 2, 1, 4, self.s_vT)
            self.s_k.wait(e, 1, c)
            self.s_vTs.wait(e, 2, c)
            for j in range(4):
                for kb in range(KB):
                    x = e.transpose(ps[:, 5 + j // 2, (j % 2) * HID + kb * P:(j % 2) * HID + (kb + 1) * P],
                                    self.vT[:, kb, j * P:(j + 1) * P], k.ident[:])
            x @ self.s_vt

        def main(c, more):
            self.tail.idle(e, c)
            self.s_k.wait(e, 4, c)
            scores(c, 0)
            scores(c, 1)
            self.s_v.wait(e, 2, c)
            for u in range(self.UNITS + 1):
                if u + 2 < self.UNITS:
                    scores(c, u + 2)
                if u:
                    values(c, u - 1)
                if u < self.UNITS:
                    turn(c, u)
            if more:
                self.s_exp.wait(e, self.UNITS, c)
                queries(c + 1, (0, 1))
            self.s_oL.wait(e, 4, c)
            for ob in range(KB):
                for g in range(NGRP):
                    w = self.weight(3, slice(g * HID + ob * P, g * HID + (ob + 1) * P))
                    x = three(e, ps[:, 4 + ob, :], *w, self.oH[:, g, :], self.oL[:, g, :],
                              g == 0, g == NGRP - 1)
            x @ self.s_o
            if more:
                queries(c + 1, (2, 3))

        queries(0, range(NGRP))
        self.run(e, pre, main, self.tail.pe)

    def scalar(self, e):
        k, ps = self.k, self.k.psum
        self.before.ready(e, NCH - 1)
        e.wait_ge(self.s_load.sem, 16 * 10)
        e.activation(self.wH[:], self.raw[:], ACT.Copy) @ self.s_wh
        self.s_wl.wait(e, 1)
        self.s_vz.wait(e, 1)

        def exps(c, u):
            b, r, heads = self.unit(u)
            s = 2 * (u % 2)
            self.s_nm.wait(e, u + 1, c)
            if u >= 3:
                self.s_T.wait(e, u - 2, c)
            for x in range(2):
                e.activation(self.p0[:, u % 3, x, :], ps[:, s, x * P:(x + 1) * P], ACT.Exp,
                             bias=self.nm[:, u % 3, x:x + 1], accum_out=self.sums[:, u % 3, x:x + 1])
                m = e.activation(self.p1[:, u % 3, x, :], ps[:, s + 1, x * SEQ:(x + 1) * SEQ], ACT.Exp,
                                 bias=self.nm[:, u % 3, 2 + x:3 + x],
                                 accum_out=self.sums[:, u % 3, 2 + x:3 + x])
            m @ self.s_exp

        def out_hi(c, n):
            b, gg = divmod(n, 2)
            self.s_pv.wait(e, 4 * n + 4, c)
            e.activation(self.oH[:, 2 * gg:2 * gg + 2, b * SEQ:(b + 1) * SEQ],
                         ps[:, 6 + gg, :].rearrange("p (x t) -> p x t", x=2), ACT.Copy) @ self.s_oH

        def queries(c, blocks):
            for g in blocks:
                self.s_in.wait(e, g + 1, c)
                e.activation(self.q[:, g, :], ps[:, g, :], ACT.Identity, bias=self.bqs[:, g:g + 1],
                             scale=HD ** -0.5) @ self.s_q

        def pre(c, tail):
            tail(0, 2)
            for ob in range(KB):
                self.s_vT.wait(e, ob + 1, c)
                e.activation(self.vT[:, ob, :], ps[:, 3 + ob, :], ACT.Identity, bias=self.bv[:, ob:ob + 1]) @ self.s_vTs
                if ob == 0:
                    tail(2, 4)
            self.s_vt.wait(e, 1, c)
            for j in range(2):
                e.activation(self.v[:, 2 * j:2 * j + 2, :, 0:HD],
                             ps[:, 5 + j, :].rearrange("p (a h d) -> p a h d", a=2, d=HD), ACT.Copy) @ self.s_v

        def main(c, more):
            for u in range(self.UNITS):
                exps(c, u)
                if u >= 5 and u % 4 == 1:
                    out_hi(c, u // 4 - 1)
            out_hi(c, 3)
            if more:
                queries(c + 1, (0, 1))
            self.s_o.wait(e, 1, c)
            for ob in range(KB):
                m = e.activation(self.fin[:, ob, :], ps[:, 4 + ob, :], ACT.Identity, bias=self.bo[:, ob:ob + 1])
            m @ self.s_fin
            if more:
                queries(c + 1, (2, 3))

        queries(0, range(NGRP))
        self.run(e, pre, main, self.tail.act)

    def vector(self, e):
        k, ps = self.k, self.k.psum
        self.before.ready(e, NCH - 1)
        e.wait_ge(self.s_load.sem, 16 * 10)
        e.tensor_copy(self.mask[:], self.mraw[:])
        e.tensor_copy(self.one[:], k.ident[:])
        e.tensor_scalar(self.bqs[:], self.bq[:], HD ** -0.5, None, ALU.mult)
        self.s_wh.wait(e, 1)
        e.tensor_tensor(self.wL[:], self.raw[:], self.wH[:].bitcast(F32), ALU.subtract) @ self.s_wl

        def maxima(c, u):
            s, m = 2 * (u % 2), self.mx[:, u % 3, :]
            self.s_S.wait(e, u + 1, c)
            if u >= 3:
                self.s_exp.wait(e, u - 2, c)
            e.tensor_reduce(m[:, 0:2], ps[:, s, 0:2 * P].rearrange("p (x t) -> p x t", x=2), AX_X, ALU.max)
            e.tensor_reduce(m[:, 2:4], ps[:, s + 1, :].rearrange("p (x t) -> p x t", x=2), AX_X,
                            ALU.max) @ self.s_max
            self.s_max.wait(e, u + 1, c)
            e.tensor_scalar(self.nm[:, u % 3, :], m, -1.0, None, ALU.mult) @ self.s_nm

        def divide(c, u):
            self.s_exp.wait(e, u + 1, c)
            e.reciprocal(self.rec[:, u % 3, :], self.sums[:, u % 3, :]) @ self.s_rec
            self.s_rec.wait(e, u + 1, c)
            for x in range(2):
                for p, at in ((self.p0, x), (self.p1, 2 + x)):
                    m = e.tensor_scalar(p[:, u % 3, x, :], p[:, u % 3, x, :],
                                        self.rec[:, u % 3, at:at + 1], None, ALU.mult)
            m @ self.s_pn

        def take(c, u):
            self.s_T.wait(e, u + 1, c)
            if u >= 2:
                self.s_pv.wait(e, u - 1, c)
            for x in range(2):
                m = e.tensor_copy(self.pt[:, u % 2, x, :], ps[:, 4 + x, 0:3 * P])
            m @ self.s_pt

        def out_lo(c, n):
            b, gg = divmod(n, 2)
            self.s_oH.wait(e, n + 1, c)
            at = (slice(None), slice(2 * gg, 2 * gg + 2), slice(b * SEQ, (b + 1) * SEQ))
            e.tensor_tensor(self.oL[at], ps[:, 6 + gg, :].rearrange("p (x t) -> p x t", x=2),
                            self.oH[at].bitcast(F32), ALU.subtract) @ self.s_oL

        def pre(c, tail):
            tail(0, 1)
            for g in range(NGRP):
                self.s_in.wait(e, NGRP + g + 1, c)
                bank = (6, 0, 1, 2)[g]
                e.scalar_tensor_tensor(self.kk[:, g, :].rearrange("p (s t) -> p s t", s=2),
                                       ps[:, bank, :].rearrange("p (s t) -> p s t", s=2),
                                       self.bk[:, g:g + 1],
                                       self.pat[:, g, :].unsqueeze(1).broadcast_to([P, 2, SEQ]),
                                       ALU.add, ALU.add) @ self.s_k
                if g in (1, 2):
                    tail(g, g + 1)
            tail(3, 4)

        def main(c, more):
            maxima(c, 0)
            maxima(c, 1)
            divide(c, 0)
            for u in range(self.UNITS):
                if u + 2 < self.UNITS:
                    maxima(c, u + 2)
                if u + 1 < self.UNITS:
                    divide(c, u + 1)
                take(c, u)
                if u >= 5 and u % 4 == 1:
                    out_lo(c, u // 4 - 1)
            out_lo(c, 3)

        self.run(e, pre, main, self.tail.dve)


class Prep:

    NB = 2 * INTER // 512
    UP = HID ** -0.5
    DOWN = INTER ** -0.5

    def __init__(self, k, ins, pack):
        self.k, self.ins, self.pack = k, ins, pack
        k.kind = "prep_"
        self.s_load = Sem(k, "load")
        self.s_su = Sem(k, "su")
        self.s_mm = Sem(k, "mm")
        self.s_ev = Sem(k, "ev")
        self.s_bf = Sem(k, "bf")
        self.s_k = Sem(k, "k")
        self.s_out = Sem(k, "out")
        self.s_d = Sem(k, "d")
        new = Arena(k, "prep_").new
        self.ug, self.dn = new("ug", [P, KB, 2 * INTER]), new("dn", [P, FFN_TILES, HID])
        self.had = new("had", [P, P])
        self.su, self.sd = new("su", [P, KB]), new("sd", [P, FFN_TILES])
        self.cu, self.cd = new("cu", [P, 2 * INTER]), new("cd", [P, HID])
        self.t1 = new("t1", [P, 2, 512])
        self.sum = new("sum", [P, KB, 512])
        self.k2 = new("k2", [P, self.NB, KB, 512])
        self.d = [new(f"d{i}", [P, FFN_TILES, HID]) for i in range(2)]

    def sync(self, e):
        i = self.ins
        for dst, src in ((self.had[:], i["had"]), (self.ug[:], i["ffn_ug"]), (self.dn[:], i["ffn_dn"]),
                         (self.su[:], i["su_ug"]), (self.sd[:], i["su_dp"]),
                         (self.cu[:], i["c_ug"].partition_broadcast(P)),
                         (self.cd[:], i["c_dp"].partition_broadcast(P))):
            e.dma_start(dst, src).then_inc(self.s_load.sem, 16)
        for n in range(self.NB):
            self.s_k.wait(e, 2 * n + 2)
            for kb in range(KB):
                at = ((n // 2) * KB + kb) * P
                e.dma_start(self.pack[4 * (n % 2):4 * (n % 2) + 4, :, at:at + P].rearrange("t p f -> p t f"),
                            self.k2[:, n, kb, :].rearrange("p (t f) -> p t f", f=P)).then_inc(self.s_out.sem, 16)
        self.s_d.wait(e, 6 + FFN_TILES)
        e.dma_start(self.pack[:, :, 2 * KB * P:].rearrange("t p f -> p t f"), self.d[1][:]).then_inc(self.s_out.sem, 16)
        e.wait_ge(self.s_out.sem, 16 * (KB * self.NB + 1))

    def tensor(self, e):
        e.wait_ge(self.s_load.sem, 16 * 7)
        for n in range(self.NB):
            if n >= 2:
                self.s_bf.wait(e, 2 * n - 2)
            for kb in range(KB):
                m = e.matmul(self.k.psum[:, 2 * (n % 2) + kb, :], self.had[:],
                             self.ug[:, kb, n * 512:(n + 1) * 512], start=True, stop=True)
            m @ self.s_mm
        self.s_bf.wait(e, 2 * self.NB)
        for b in range(4):
            m = e.matmul(self.k.psum[:, b, :], self.had[:],
                         self.dn[:, 2 * b:2 * b + 2, :].rearrange("p a f -> p (a f)"), start=True, stop=True)
        m @ self.s_mm

    def scalar(self, e):
        for n in range(self.NB):
            self.s_mm.wait(e, n + 1)
            if n >= 2:
                self.s_bf.wait(e, 2 * n - 2)
            e.activation(self.t1[:, n % 2, :], self.k.psum[:, 2 * (n % 2) + 1, :], ACT.Copy) @ self.s_ev
        self.s_mm.wait(e, self.NB + 1)
        e.activation(self.d[0][:].rearrange("p (a b) f -> p a (b f)", a=4), self.k.psum[:, 0:4, :],
                     ACT.Copy) @ self.s_ev

    def vector(self, e):
        e.wait_ge(self.s_load.sem, 16 * 7)
        e.tensor_scalar(self.su[:], self.su[:], self.UP, None, ALU.mult) @ self.s_su
        e.tensor_scalar(self.sd[:], self.sd[:], self.DOWN, None, ALU.mult) @ self.s_su
        self.s_su.wait(e, 2)
        for n in range(self.NB):
            self.s_ev.wait(e, n + 1)
            self.s_k.wait(e, 2 * n)
            for kb, op in enumerate((ALU.add, ALU.subtract)):
                e.tensor_tensor(self.sum[:, kb, :], self.k.psum[:, 2 * (n % 2), :], self.t1[:, n % 2, :],
                                op) @ self.s_bf
            for kb in range(KB):
                self.s_bf.wait(e, 2 * n + kb + 1)
                e.scalar_tensor_tensor(self.k2[:, n, kb, :], self.sum[:, kb, :], self.su[:, kb:kb + 1],
                                       self.cu[:, n * 512:(n + 1) * 512], ALU.mult, ALU.mult) @ self.s_k
        self.s_ev.wait(e, self.NB + 1)
        for stage, h in enumerate((1, 2, 4)):
            a, b = (x[:].rearrange("p (n two h) f -> p n two (h f)", two=2, h=h)
                    for x in (self.d[stage % 2], self.d[(stage + 1) % 2]))
            self.s_d.wait(e, 2 * stage)
            e.tensor_tensor(b[:, :, 0, :], a[:, :, 0, :], a[:, :, 1, :], ALU.add) @ self.s_d
            e.tensor_tensor(b[:, :, 1, :], a[:, :, 0, :], a[:, :, 1, :], ALU.subtract) @ self.s_d
        self.s_d.wait(e, 6)
        for t in range(FFN_TILES):
            e.scalar_tensor_tensor(self.d[1][:, t, :], self.d[1][:, t, :], self.sd[:, t:t + 1], self.cd[:],
                                   ALU.mult, ALU.mult) @ self.s_d

    def pool(self, e):
        pass


def program(nc, ins, out, stages=6):
    with ExitStack() as ctx:
        k = Kern(nc, ctx)
        x = ins["x"].rearrange("b s f -> (b s) f")
        tails = [Tail(k, "t0_", entry=True, route=True)]
        pack = nc.dram_tensor("ffn_pack", [FFN_TILES, P, SwiGLU.WCOLS], F32, kind="Internal").ap()
        parts = [Prep(k, ins, pack), Entry(k, x, tails[0])]
        for n in range(1, stages + 1):
            tails.append(Tail(k, f"t{n}_", last=(n == stages), route=(n == 2 and n < stages)))
            tails[n].out = out.rearrange("b s f -> (b s) f")
            if n in (1, 3):
                parts.append(SwiGLU(k, f"moe{n}_", MOE_TILES // MOE_G, MOE_G, ins["moe_pack"],
                                    ins["gate_rows"], tails[n - 1], tails[n]))
            if n == 2:
                parts.append(Scan(k, "scan_", ins, tails[n - 1], tails[n]))
            if n in (4, 6):
                parts.append(SwiGLU(k, f"ffn{n}_", 1, FFN_TILES, pack, None, tails[n - 1], tails[n]))
            if n == 5:
                parts.append(Attention(k, "attn_", ins, tails[n - 1], tails[n]))

        block = ctx.enter_context(nc.Block())

        @block.sync
        def _(e):
            for s in k.credits:
                e.sem_inc(s.sem, s.base)
            e.dma_start(k.ident[:], ins["ident"]).then_inc(k.s_const.sem, 16)
            e.dma_start(k.gw[:], ins["gate_w"]).then_inc(k.s_const.sem, 16)
            e.dma_start(k.fold[:], ins["add_parts"]).then_inc(k.s_const.sem, 16)
            for p in parts:
                p.sync(e)

        @block.gpsimd
        def _(e):
            e.memset(k.half[:], -0.5) @ k.s_half
            k.s_half.wait(e, 1)
            for p in parts:
                p.pool(e)

        @block.vector
        def _(e):
            e.memset(k.gate[0:32, :].bitcast(F32), 1.0) @ k.s_init
            e.memset(k.gate[32:64, :].bitcast(F32), 0.0) @ k.s_init
            e.wait_ge(k.s_const.sem, 48)
            e.tensor_copy(k.gwp[:, :, 0:NEXP], k.gw[:]) @ k.s_init
            k.s_init.wait(e, 3)
            e.tensor_tensor(k.gwp[:, :, NEXP:], k.gw[:], k.gwp[:, :, 0:NEXP].bitcast(F32),
                            ALU.subtract) @ k.s_init
            for p in parts:
                p.vector(e)

        @block.scalar
        def _(e):
            k.s_init.wait(e, 4)
            for p in parts:
                p.scalar(e)

        @block.tensor
        def _(e):
            e.wait_ge(k.s_const.sem, 48)
            k.s_init.wait(e, 4)
            for p in parts:
                p.tensor(e)


def blocks(w, n=P):
    return w.reshape(-1, n, w.shape[-1]).transpose(1, 0, 2)


def layout(inputs):
    a = {n: np.asarray(v) for n, v in inputs.items()}
    f32 = np.float32
    out = {"x": a["L0_attn_x"], "ident": np.eye(P, dtype=f32)}
    out["add_parts"] = np.tile(np.eye(NEXP, dtype=f32), (2, 1))
    out["gate_w"] = blocks(a["L0_ffn_gate_w"].T)
    w13, sw13 = a["L0_ffn_w13"], a["L0_ffn_sw13"]
    full = MOE_TILES * P
    parts = []
    for half in range(2):
        w = np.zeros((full, HID), f32)
        w[:NEXP * EINT] = w13[:, half * EINT:(half + 1) * EINT, :].reshape(-1, HID)
        w[NEXP * EINT:FEAT] = sw13[half * 2 * EINT:(half + 1) * 2 * EINT]
        parts.append(w.reshape(MOE_TILES, P, KB, P).transpose(0, 3, 2, 1).reshape(MOE_TILES, P, KB * P))
    d = np.zeros((full, HID), f32)
    d[:NEXP * EINT] = a["L0_ffn_w2"].transpose(0, 2, 1).reshape(-1, HID)
    d[NEXP * EINT:FEAT] = a["L0_ffn_sw2"].T
    parts.append(d.reshape(MOE_TILES, P, HID))
    out["moe_pack"] = np.concatenate(parts, axis=2)
    rows = np.zeros((full, 64), f32)
    f = np.arange(FEAT)
    expert = np.minimum(f // EINT, ONES_ROW)
    rows[f, expert] = 1.0
    routed = f[:NEXP * EINT]
    rows[routed, 32 + expert[routed]] = 1.0
    out["gate_rows"] = rows.reshape(MOE_TILES, P, 64).transpose(0, 2, 1)
    out["W_in"] = blocks(a["L0_attn_W_in"].T).reshape(P, -1)
    out["Wx"] = blocks(a["L0_attn_Wx"].T).reshape(P, -1)
    out["Wdt"] = a["L0_attn_Wdt"].T
    out["Wout"] = blocks(a["L0_attn_Wout"].T).reshape(P, -1)
    out["conv_w"] = blocks(a["L0_attn_conv_w"])
    for name in ("conv_b", "dt_bias", "D"):
        out[name] = a["L0_attn_" + name].reshape(-1, P).T
    out["A"] = blocks(a["L0_attn_A"])
    out["dt_ln"] = a["L0_attn_dt_ln_w"].reshape(P, 1)
    out["bc_ln"] = np.concatenate([a["L0_attn_b_ln_w"], a["L0_attn_c_ln_w"]]).reshape(2 * NST, 1)
    out["mean_bc"] = np.kron(np.eye(2, dtype=f32), np.full((NST, NST), 1.0 / NST, f32))
    out["state_pick"] = np.tile(np.eye(2 * NST, dtype=f32), (2, 1))
    slot = (np.arange(HEADS)[:, None] * HSLOT + np.arange(HD)).ravel()
    pos = np.arange(HEADS) * HSLOT + HD
    for name in "qk":
        w = np.zeros((HID, HEADS * HSLOT), f32)
        w[:, slot] = a["L1_attn_W" + name]
        out["W" + name] = blocks(w).reshape(P, -1)
        b = np.zeros(HEADS * HSLOT, f32)
        b[slot] = a["L1_attn_b" + name]
        if name == "q":
            b[pos] = HD ** 0.5
        out["b" + name] = b.reshape(-1, P).T
    out["Wv"] = blocks(a["L1_attn_Wv"]).reshape(P, -1)
    w = np.zeros((HEADS * HSLOT, HID), f32)
    w[slot] = a["L1_attn_Wo"]
    out["Wo"] = blocks(w).reshape(P, -1)
    out["bv"] = a["L1_attn_bv"].reshape(-1, P).T
    out["bo"] = a["L1_attn_bo"].reshape(-1, P).T
    first = 2.0 ** (-2.0 ** -(np.log2(HEADS) - 3))
    slopes = np.array([first * first ** i for i in range(HEADS)], dtype=f32)
    pat = np.zeros((HEADS * HSLOT, SEQ), f32)
    pat[pos] = -slopes[:, None] * (SEQ - 1 - np.arange(SEQ, dtype=f32))[None, :]
    out["slopes"] = blocks(pat)
    out["mask"] = np.where(np.arange(P)[None, :] > np.arange(P)[:, None], MASKED, 0.0).astype(f32)
    had = np.ones((1, 1), f32)
    while had.shape[0] < P:
        had = np.block([[had, had], [had, -had]])
    out["had"] = had
    out["ffn_ug"] = blocks(np.concatenate([a["L1_ffn_W_gate"].T, a["L1_ffn_W_up"].T], axis=1))
    out["ffn_dn"] = blocks(a["L1_ffn_W_down"].T)
    out["su_ug"] = a["L1_ffn_SU_ug"].reshape(-1, P).T
    out["su_dp"] = a["L1_ffn_SU_dp"].reshape(-1, P).T
    out["c_ug"] = np.concatenate([a["L1_ffn_Wscale_ug"][INTER:], a["L1_ffn_Wscale_ug"][:INTER]])
    out["c_dp"] = a["L1_ffn_Wscale_dp"]
    return {n: np.ascontiguousarray(v, dtype=v.dtype) for n, v in out.items()}


def kernel(**inputs):
    import concourse.bacc as bacc
    from concourse.bass_utils import run_bass_kernel_spmd

    nc = bacc.Bacc("TRN2", target_bir_lowering=False, num_devices=1)
    arrays = layout(inputs)
    ins = {n: nc.dram_tensor(n, list(v.shape), mybir.dt.from_np(v.dtype), kind="ExternalInput").ap()
           for n, v in arrays.items()}
    out = nc.dram_tensor("out", [BATCH, SEQ, HID], F32, kind="ExternalOutput").ap()
    program(nc, ins, out)
    return run_bass_kernel_spmd(nc, [arrays], core_ids=[0]).results[0]["out"]
```

```python
from contextlib import ExitStack

import numpy as np

import concourse.bass as bass
from concourse import mybir

F32 = mybir.dt.float32
F32R = mybir.dt.float32r
ALU = mybir.AluOpType
ACT = mybir.ActivationFunctionType
AX_X = mybir.AxisListType.X

P = 128
BATCH, SEQ, HID = 8, 256, 256
TOK = BATCH * SEQ
TILES = TOK // P
CHUNK = 512
NCH = TOK // CHUNK
KB = HID // P
EPS = 1e-5

NEXP, TOPK, EINT = 16, 6, 176
FEAT = NEXP * EINT + 2 * EINT
MOE_TILES = -(-FEAT // P)
MOE_G = 5
ONES_ROW = NEXP
INTER = 1024
FFN_TILES = INTER // P
IN, NST, KCONV, RANK = 512, 16, 4, 128
IB = IN // P
XP = RANK + 2 * NST
HEADS, HD = 16, 16
HSLOT = 32
HGRP = P // HSLOT
NGRP = HEADS // HGRP
MASKED = -1e30


class Sem:

    def __init__(self, k, name, per=0, credit=0, passes=0, total=0):
        self.per, key = per, k.kind + name
        if key in k.used:
            self.sem, self.base = k.used[key]
        else:
            self.sem, self.base = k.ctx.enter_context(k.nc.semaphore(key)), credit
            if credit:
                k.credits.append(self)
        k.used[key] = self.sem, self.base + (total or passes * per)

    def wait(self, eng, count, it=0):
        v = it * self.per + (count + self.base)
        if isinstance(v, int) and v <= 0:
            return
        eng.wait_ge(self.sem, v)

    def __rmatmul__(self, ins):
        ins.then_inc(self.sem, 1)
        return ins


class Kern:

    def __init__(self, nc, ctx):
        self.nc, self.ctx, self.kind, self.credits, self.used = nc, ctx, "", [], {}
        self.base = 20480
        self.psum = ctx.enter_context(nc.psum_tensor("psum", [P, 8, 512], F32))
        self.X = self.keep("X", [P, TILES, HID])
        self.xH = self.keep("xnT_hi", [P, KB, TOK], F32R)
        self.xL = self.keep("xnT_lo", [P, KB, TOK], F32R)
        self.acc_at = self.base
        self.accT = self.keep("accT", [P, KB, TOK])
        self.gate = self.keep("gate_table", [64, TOK], F32R)
        self.ident = self.keep("ident", [P, P])
        self.xst = self.keep("x_stage", [P, 2, 2, HID])
        self.st6 = self.keep("bn6", [P, 2, 2, 6])
        self.mv = self.keep("mean_var", [P, 2, 2, 2])
        self.rs = self.keep("rstd", [P, 2, 2])
        self.half = self.keep("minus_half", [P, 16])
        self.gw = self.keep("gate_w_raw", [P, KB, NEXP])
        self.gwp = self.keep("gate_w_parts", [P, KB, 2 * NEXP], F32R)
        self.lgT = self.keep("logitsT_parts", [2 * NEXP, CHUNK])
        self.fold = self.keep("add_parts", [2 * NEXP, NEXP])
        self.lg = self.keep("logits", [P, TILES, NEXP])
        self.ex = self.keep("exps", [P, TILES, NEXP])
        self.mx = self.keep("top8", [P, TILES, 8])
        self.rest = self.keep("not_chosen", [P, TILES, NEXP])
        self.red = self.keep("row_stats", [P, TILES])
        self.red2 = self.keep("row_stats2", [P, TILES])
        self.s_const = Sem(self, "const")
        self.s_init = Sem(self, "init")
        self.s_half = Sem(self, "half")
        self.s_own = Sem(self, "own")
        self.arena = self.base

    def own(self, e):
        e.sem_inc(self.s_own.sem, 1)

    def at(self, name, shape, dt, off):
        return self.nc.alloc_sbuf_tensor_at(name, list(shape), dt, offset=off)

    def keep(self, name, shape, dt=F32):
        t = self.at(name, shape, dt, self.base)
        self.base += -(-4 * int(np.prod(shape[1:])) // 32) * 32
        return t


class Arena:

    def __init__(self, k, tag):
        self.k, self.tag, self.off = k, tag, k.arena

    def new(self, name, shape, dt=F32, over=None):
        off = self.off if over is None else over
        t = self.k.at(self.tag + name, shape, dt, off)
        end = off + -(-4 * int(np.prod(shape[1:])) // 32) * 32
        if over is None:
            self.off = end
        return t


def three(e, out, wH, wL, xH, xL, start, stop):
    e.matmul(out, wH, xH, start=start, stop=False)
    e.matmul(out, wH, xL, start=False, stop=False)
    return e.matmul(out, wL, xH, start=False, stop=stop)


class Tail:

    def __init__(self, k, tag, entry=False, last=False, route=False):
        self.k, self.entry, self.last, self.route = k, entry, last, route
        k.kind = "tail_"
        self.two = False
        self.src_ready = None
        self.src = None
        if not entry:
            self.s_back = Sem(k, "back", 2, passes=NCH)
            self.s_add = Sem(k, "add", 2, credit=1, passes=NCH)
        if last:
            self.s_store = Sem(k, "store")
            return
        self.s_st = Sem(k, "bnst", 4, passes=NCH)
        self.s_ag = Sem(k, "bnag", 4, passes=NCH)
        self.s_ve = Sem(k, "vareps", 2, passes=NCH)
        self.s_rs = Sem(k, "rstd", 2, passes=NCH)
        self.s_xs = Sem(k, "xs", 2, passes=NCH)
        self.s_fw = Sem(k, "fw", 2, passes=NCH)
        self.s_xH = Sem(k, "xH", 2, credit=1, passes=NCH)
        self.s_xL = Sem(k, "xL", 2, credit=1, passes=NCH)
        if entry:
            self.s_in = [Sem(k, f"in{c}") for c in range(NCH)]
        if route:
            self.n = NCH if entry else 1
            self.r_lgT = Sem(k, "r_lgT", 1, passes=NCH)
            self.r_lgTs = Sem(k, "r_lgTs", 1, passes=NCH)
            self.r_lg = Sem(k, "r_lg", 1, passes=NCH)
            self.r_v = Sem(k, "r_v", 8 + 8 * self.n, passes=NCH // self.n)
            self.r_ex = Sem(k, "r_ex", 1, passes=NCH // self.n)
            self.r_cT = Sem(k, "r_cT", 1, passes=NCH)
            self.r_cH = Sem(k, "r_cH", 1, credit=1, passes=NCH)
            self.r_cL = Sem(k, "r_cL", 1, credit=1, passes=NCH)

    def final(self, fn, e, lead=None):
        c, self.two = NCH - 1, True
        if fn == self.dve:
            for p in range(2):
                self.add(e, c, p)
                self.stats(e, c, p)
            for p in range(2):
                self.norm(e, c, p)
            self.low(e, c, 0)
            if lead:
                lead(e)
            self.low(e, c, 1)
        else:
            for slot in (0, 2, 1, 3):
                fn(e, c, slot)
                if slot == 1 and lead:
                    lead(e)
        for slot in (4, 5, 6) if self.route else ():
            fn(e, c, slot)
        self.two = False

    def bank(self, p=1):
        return self.k.psum[:, 6 + p if self.entry or self.two else 7, :]

    def ready(self, e, c):
        self.s_xH.wait(e, 2, c)
        self.s_xL.wait(e, 2, c)
        if self.route:
            self.r_cH.wait(e, 1, c)
            self.r_cL.wait(e, 1, c)

    def idle(self, e, c):
        if self.last:
            return self.s_add.wait(e, 0, c)
        self.s_xH.wait(e, 0, c)
        self.s_xL.wait(e, 0, c)
        if self.route:
            self.r_cH.wait(e, 0, c)
            self.r_cL.wait(e, 0, c)

    def pe(self, e, c, slot):
        k, p = self.k, slot // 2
        if slot in (0, 2) and not self.entry:
            if slot == 0:
                self.src_ready.wait(e, 1, c)
            elif not self.two:
                (self.s_add if self.last else self.s_xL).wait(e, 1, c)
            src = self.src(c)
            for j in range(2):
                for kb in range(KB):
                    m = e.transpose(self.bank(p)[:, j * 256 + kb * P:j * 256 + kb * P + P],
                                    src[:, kb, (2 * p + j) * P:(2 * p + j + 1) * P], k.ident[:])
            m @ self.s_back
        if slot in (1, 3) and not self.last:
            self.s_xs.wait(e, p + 1, c)
            if self.entry and c:
                self.s_xL.wait(e, p + 1, c - 1)
            for j in range(2):
                for kb in range(KB):
                    m = e.transpose(self.bank(p)[:, kb * 256 + j * P:kb * 256 + j * P + P],
                                    k.xst[:, p, j, kb * P:(kb + 1) * P], k.ident[:])
            m @ self.s_fw
        if slot == 4:
            self.logits(e, c, self.bank())
        if slot == 5:
            self.turn_logits(e, c, self.bank(), 0)
        if slot == 6:
            self.turn_gates(e, c, self.bank(), 0)

    def act(self, e, c, slot):
        k, p = self.k, slot // 2
        if slot in (1, 3) and not self.last:
            self.s_fw.wait(e, p + 1, c)
            e.activation(k.xH[:, :, bass.ds(c * CHUNK + p * 256, 256)],
                         self.bank(p).rearrange("p (k t) -> p k t", k=KB), ACT.Copy) @ self.s_xH
        if slot == 4:
            self.keep_logits(e, c, self.bank())
        if slot == 5:
            self.exps(e, c)
        if slot == 6:
            self.gates_hi(e, c, self.bank())

    def logits(self, e, c, bank):
        k = self.k
        self.s_xH.wait(e, 2, c)
        self.s_xL.wait(e, 2, c)
        k.own(e)
        for kb in range(KB):
            for x in (k.xH, k.xL):
                m = e.matmul(bank[0:2 * NEXP, :], k.gwp[:, kb, :], x[:, kb, bass.ds(c * CHUNK, CHUNK)],
                             start=(kb == 0 and x is k.xH), stop=(kb == KB - 1 and x is k.xL))
        m @ self.r_lgT

    def turn_logits(self, e, c, bank, tile):
        k = self.k
        self.r_lgTs.wait(e, 1, c)
        k.own(e)
        for j in range(4):
            m = e.matmul(bank[:, (tile + j) * NEXP:(tile + j + 1) * NEXP], k.lgT[:, j * P:(j + 1) * P],
                         k.fold[:], start=True, stop=True)
        m @ self.r_lg

    def turn_gates(self, e, c, bank, tile):
        k = self.k
        self.r_v.wait(e, self.r_v.per, c if self.n == 1 else 0)
        for j in range(4):
            m = e.transpose(bank[0:NEXP, j * P:(j + 1) * P], k.lg[:, tile + j, :], k.ident[:])
        m @ self.r_cT

    def keep_logits(self, e, c, bank):
        self.r_lgT.wait(e, 1, c)
        e.activation(self.k.lgT[:], bank[0:2 * NEXP, :], ACT.Copy) @ self.r_lgTs

    def exps(self, e, c):
        k, t = self.k, 4 * self.n
        self.r_v.wait(e, 2, c)
        e.activation(k.ex[:, 0:t, :], k.lg[:, 0:t, :], ACT.Exp) @ self.r_ex

    def gates_hi(self, e, c, bank):
        self.r_cT.wait(e, 1, c)
        e.activation(self.k.gate[0:NEXP, bass.ds(c * CHUNK, CHUNK)], bank[0:NEXP, :], ACT.Copy) @ self.r_cH

    def choose(self, e, c, bank):
        k, n, t = self.k, [0], 4 * self.n
        lg, ex, rest, mx = (x[:, 0:t, :] for x in (k.lg, k.ex, k.rest, k.mx))
        red, red2 = k.red[:, 0:t], k.red2[:, 0:t]

        def step(ins, wait=True):
            ins @ self.r_v
            n[0] += 1
            if wait:
                self.r_v.wait(e, n[0], c)

        over = red.unsqueeze(2).broadcast_to([P, t, NEXP])
        if self.n == 1:
            self.r_lg.wait(e, 1, c)
        else:
            self.r_lg.wait(e, 1, NCH - 1)
        logits = bank[:, 0:t * NEXP].rearrange("p (j x) -> p j x", j=t)
        step(e.tensor_reduce(red, logits, AX_X, ALU.max))
        step(e.tensor_tensor(lg, logits, over, ALU.subtract))
        self.r_ex.wait(e, 1, c)
        for j in range(t):
            if j == 0:
                k.own(e)
            step(e.max(mx[:, j, :], ex[:, j, :]), wait=(j == t - 1))
        step(e.memset(mx[:, :, TOPK:8], -1.0))
        for j in range(t):
            if j == 0:
                k.own(e)
            step(e.match_replace(rest[:, j, :], mx[:, j, :], ex[:, j, :], 0.0), wait=(j == t - 1))
        step(e.tensor_tensor(lg, ex, rest, ALU.subtract))
        step(e.tensor_reduce(red, lg, AX_X, ALU.add))
        step(e.tensor_scalar(red2, red, 1e-20, None, ALU.add))
        step(e.reciprocal(red, red2))
        step(e.tensor_tensor(lg, lg, over, ALU.mult))
        assert n[0] == self.r_v.per, n[0]

    def gates_lo(self, e, c, bank):
        k, cols = self.k, bass.ds(c * CHUNK, CHUNK)
        self.r_cH.wait(e, 1, c)
        e.tensor_tensor(k.gate[32:32 + NEXP, cols], bank[0:NEXP, :], k.gate[0:NEXP, cols].bitcast(F32),
                        ALU.subtract) @ self.r_cL

    def sync(self, e):
        for c in range(NCH):
            self.s_add.wait(e, 2, c)
            e.dma_start(self.out[c * CHUNK:(c + 1) * CHUNK, :].rearrange("(n p) f -> p n f", p=P),
                        self.k.X[:, 4 * c:4 * c + 4, :]).then_inc(self.s_store.sem, 16)
        e.wait_ge(self.s_store.sem, 16 * NCH)

    def pool(self, e, c, slot):
        if slot in (0, 2) and not self.last:
            k, p = self.k, slot // 2
            self.s_ag.wait(e, 2 * p + 2, c)
            k.own(e)
            e.tensor_scalar(k.rs[:, p, :], k.mv[:, p, :, 1], EPS, None, ALU.add) @ self.s_ve
            self.s_ve.wait(e, p + 1, c)
            e.tensor_tensor(k.rs[:, p, :], k.rs[:, p, :], k.half[:, 0:2], ALU.pow) @ self.s_rs

    def add(self, e, c, p):
        rows = self.k.X[:, bass.ds(c * 4 + 2 * p, 2), :]
        if self.entry:
            self.s_in[c].wait(e, 16)
            return
        self.s_back.wait(e, p + 1, c)
        e.tensor_tensor(rows, rows, self.bank(p).rearrange("p (j f) -> p j f", j=2), ALU.add) @ self.s_add

    def stats(self, e, c, p):
        if self.last:
            return
        k = self.k
        if not self.entry:
            self.s_add.wait(e, p + 1, c)
        for j in range(2):
            if j == 0:
                k.own(e)
            e.bn_stats(k.st6[:, p, j, :], k.X[:, c * 4 + 2 * p + j, :]) @ self.s_st
        for j in range(2):
            self.s_st.wait(e, 2 * p + j + 1, c)
            k.own(e)
            e.bn_aggr(k.mv[:, p, j, :], k.st6[:, p, j, :]) @ self.s_ag

    def norm(self, e, c, p):
        if self.last:
            return
        k = self.k
        self.s_rs.wait(e, p + 1, c)
        for j in range(2):
            m = e.tensor_scalar(k.xst[:, p, j, :], k.X[:, c * 4 + 2 * p + j, :], k.mv[:, p, j, 0:1],
                                k.rs[:, p, j:j + 1], ALU.subtract, ALU.mult)
        m @ self.s_xs

    def low(self, e, c, p):
        if self.last:
            return
        k = self.k
        self.s_xH.wait(e, p + 1, c)
        cols = bass.ds(c * CHUNK + p * 256, 256)
        e.tensor_tensor(k.xL[:, :, cols], self.bank(p).rearrange("p (k t) -> p k t", k=KB),
                        k.xH[:, :, cols].bitcast(F32), ALU.subtract) @ self.s_xL

    def dve(self, e, c, slot):
        p = slot // 2
        if slot in (0, 2):
            self.add(e, c, p)
            self.stats(e, c, p)
            self.norm(e, c, p)
        if slot in (1, 3):
            self.low(e, c, p)
        if slot == 5:
            self.choose(e, c, self.bank())
        if slot == 6:
            self.gates_lo(e, c, self.bank())


class SwiGLU:

    WCOLS = 2 * KB * P + HID
    MOE_END = 4 * MOE_G * (3 * WCOLS + 2 * P) + 4 * 6 * CHUNK
    FFN_END = 4 * FFN_TILES * 2 * WCOLS + 4 * 6 * CHUNK

    @staticmethod
    def ffn_raw_at(k):
        return (k.nc.sbuf_usable_end - 4 * FFN_TILES * SwiGLU.WCOLS) // 32 * 32

    def __init__(self, k, tag, groups, G, pack, rows, before, tail):
        self.prev = self.next = None
        self.k, self.NG, self.G, self.pack, self.rows = k, groups, G, pack, rows
        self.before, self.tail = before, tail
        k.kind = "glu_"
        S = NCH * G
        self.S = S
        self.s_raw = [Sem(k, f"raw{i}" if rows is not None else f"ffn_raw{i}",
                          32 if rows is not None else 16, passes=groups) for i in range(G)]
        self.s_wH = Sem(k, "wH", G, passes=groups)
        self.s_wL = Sem(k, "wL", G, passes=groups)
        self.s_gu = Sem(k, "gu", S, passes=groups)
        self.s_cb = Sem(k, "cb", S, passes=groups)
        self.s_dn = Sem(k, "dn", S, credit=G, passes=groups)
        self.s_silu = Sem(k, "silu", S, passes=groups)
        self.s_hH = Sem(k, "hH", S, passes=groups)
        self.s_t = Sem(k, "t", S, credit=2, passes=groups)
        self.s_h = Sem(k, "h", S, passes=groups) if rows is not None else None
        self.s_hL = Sem(k, "hL", S, credit=2, passes=groups)
        self.s_acc = Sem(k, "acc", 4, credit=1, passes=groups)
        self.s_zero = Sem(k, "zero", total=1)
        tail.src_ready, tail.src = _Shifted(self.s_acc, 4 * (groups - 1)), \
            lambda c: k.accT[:, :, c * CHUNK:(c + 1) * CHUNK]
        a = Arena(k, tag)
        if rows is not None:
            self.raw = a.new("w_raw", [P, G, self.WCOLS])
            self.raws = a.new("rows_raw", [64, G, P])
            self.rw = a.new("rows", [64, G, P], F32R)
        else:
            self.raw = a.new("w_raw", [P, G, self.WCOLS], over=self.ffn_raw_at(k))
        self.wH = a.new("w_hi", [P, G, self.WCOLS], F32R)
        self.wL = a.new("w_lo", [P, G, self.WCOLS], F32R)
        self.end = a.off
        self.hb = a.new("hidden", [P, 2, CHUNK])
        self.hH = a.new("hidden_hi", [P, 2, CHUNK], F32R)
        self.hL = a.new("hidden_lo", [P, 2, CHUNK], F32R)
        assert a.off - k.arena == (self.FFN_END if rows is None else self.MOE_END)

    def over_groups(self, e, step):
        last = self.NG == 1
        step(0, 0, last)
        if not last:
            with e.Fori(0, self.NG - 1) as g:
                for s in range(1, self.S):
                    step(g, s, False)
                step(g + 1, 0, False)
        for s in range(1, self.S):
            step(self.NG - 1, s, True)

    def tails(self, fn, e, s, late=0):
        c, t = divmod(s, self.G)
        if c and late <= t < 4 + late:
            fn(e, c - 1, t - late)

    def after(self, fn, e, lead=None):
        self.tail.final(fn, e, lead)

    def freed(self, e):
        self.s_dn.wait(e, self.S, self.NG - 1)

    def clear(self, e):
        if self.rows is None:
            self.prev.before.ready(e, NCH - 1)
        else:
            self.prev.freed(e)

    def first(self, e):
        for t in range(self.G):
            e.dma_start(self.raw[:, t, :], self.pack[t]).then_inc(self.s_raw[t].sem, 16)
            if self.rows is not None:
                e.dma_start(self.raws[:, t, :], self.rows[t]).then_inc(self.s_raw[t].sem, 16)

    def sync(self, e):
        if self.prev:
            self.clear(e)
            self.first(e)
        if self.NG > 1:
            with e.Fori(0, self.NG - 1) as g:
                for t in range(self.G):
                    self.s_wH.wait(e, t + 1, g)
                    self.s_wL.wait(e, t + 1, g)
                    nxt = g * self.G + (self.G + t)
                    e.dma_start(self.raw[:, t, :], self.pack[bass.ds(nxt, 1), :, :].rearrange("o p n -> (o p) n")).then_inc(self.s_raw[t].sem, 16)
                    if self.rows is not None:
                        e.dma_start(self.raws[:, t, :], self.rows[bass.ds(nxt, 1), :, :].rearrange("o p n -> (o p) n")).then_inc(self.s_raw[t].sem, 16)
        if self.tail.last:
            self.tail.sync(e)

    def zero(self, e):
        e.memset(self.k.accT[:], 0.0) @ self.s_zero

    def pool(self, e):
        if self.prev:
            self.before.ready(e, NCH - 1)
            self.zero(e)
        for c in range(NCH):
            for slot in (0, 2):
                self.tail.pool(e, c, slot)

    def gu(self, e, g, s):
        c, t = divmod(s, self.G)
        k, b = self.k, 2 * (s % 2)
        if t == 0:
            self.before.ready(e, c)
        if c == 0:
            self.s_wH.wait(e, t + 1, g)
            self.s_wL.wait(e, t + 1, g)
        self.s_t.wait(e, s - 1, g)
        cols = slice(c * CHUNK, (c + 1) * CHUNK)
        for half in range(2):
            for kb in range(KB):
                w = slice((half * KB + kb) * P, (half * KB + kb + 1) * P)
                m = three(e, k.psum[:, b + half, :], self.wH[:, t, w], self.wL[:, t, w],
                          k.xH[:, kb, cols], k.xL[:, kb, cols], kb == 0, kb == KB - 1)
        m @ self.s_gu

    def cb(self, e, g, s):
        if self.rows is None:
            return
        c, t = divmod(s, self.G)
        e.matmul(self.k.psum[:, 4, :], self.rw[:, t, :], self.k.gate[:, c * CHUNK:(c + 1) * CHUNK],
                 start=True, stop=True) @ self.s_cb

    def down(self, e, g, s):
        c, t = divmod(s, self.G)
        if t == 0:
            self.s_acc.wait(e, c, g)
        self.s_hH.wait(e, s + 1, g)
        self.s_hL.wait(e, s + 1, g)
        for ob in range(KB):
            w = slice(2 * KB * P + ob * P, 2 * KB * P + (ob + 1) * P)
            m = three(e, self.k.psum[:, 5 + ob, :], self.wH[:, t, w], self.wL[:, t, w],
                      self.hH[:, s % 2, :], self.hL[:, s % 2, :], t == 0, t == self.G - 1)
        m @ self.s_dn

    def tensor(self, e):
        self.gu(e, 0, 0)
        self.cb(e, 0, 0)

        def step(g, s, last):
            if s + 1 < self.S:
                self.gu(e, g, s + 1)
            elif not last:
                self.gu(e, g + 1, 0)
            self.down(e, g, s)
            if s + 1 < self.S:
                self.cb(e, g, s + 1)
            elif not last:
                self.cb(e, g + 1, 0)
            if last:
                self.tails(self.tail.pe, e, s)

        self.over_groups(e, step)
        self.after(self.tail.pe, e)

    def lead_act(self, e):
        self.prev.freed(e)
        self.split_hi(e, 0, 0)

    def lead_dve(self, e):
        self.prev.freed(e)
        self.split_lo(e, 0, 0)

    def split_hi(self, e, g, t):
        self.s_raw[t].wait(e, self.s_raw[t].per, g)
        self.s_dn.wait(e, t + 1 - self.G, g)
        e.activation(self.wH[:, t, :], self.raw[:, t, :], ACT.Copy) @ self.s_wH

    def split_lo(self, e, g, t):
        if self.rows is not None:
            self.s_raw[t].wait(e, self.s_raw[t].per, g)
            self.s_dn.wait(e, t + 1 - self.G, g)
            e.tensor_copy(self.rw[:, t, :], self.raws[:, t, :])
        self.s_wH.wait(e, t + 1, g)
        e.tensor_tensor(self.wL[:, t, :], self.raw[:, t, :], self.wH[:, t, :].bitcast(F32),
                        ALU.subtract) @ self.s_wL

    def splits(self, fn, e, g, s, last):
        if s < self.G - 1:
            fn(e, g, s + 1)
        elif s == self.S - 1 and not last:
            fn(e, g + 1, 0)

    def scalar(self, e):
        self.before.ready(e, NCH - 1)
        if not self.prev:
            self.split_hi(e, 0, 0)

        def step(g, s, last):
            b = s % 2
            self.splits(self.split_hi, e, g, s, last)
            self.s_gu.wait(e, s + 1, g)
            self.s_hL.wait(e, s - 1, g)
            e.activation(self.hb[:, b, :], self.k.psum[:, 2 * b, :], ACT.Silu) @ self.s_silu
            (self.s_h or self.s_t).wait(e, s + 1, g)
            self.s_dn.wait(e, s - 1, g)
            e.activation(self.hH[:, b, :], self.hb[:, b, :], ACT.Copy) @ self.s_hH
            if last:
                self.tails(self.tail.act, e, s, late=1)

        self.over_groups(e, step)
        self.after(self.tail.act, e, self.next and self.next.lead_act)

    def vector(self, e):
        k = self.k
        self.before.ready(e, NCH - 1)
        if not self.prev:
            self.split_lo(e, 0, 0)
        self.s_zero.wait(e, 1)

        def take(g, c):
            self.s_dn.wait(e, (c + 1) * self.G, g)
            cols = slice(c * CHUNK, (c + 1) * CHUNK)
            e.scalar_tensor_tensor(k.accT[:, :, cols], k.psum[:, 5:5 + KB, :], 0.5,
                                   k.accT[:, :, cols], ALU.mult, ALU.add) @ self.s_acc

        def step(g, s, last):
            b, (c, t) = s % 2, divmod(s, self.G)
            tail = self.tail if last and c and t < 5 else None
            self.splits(self.split_lo, e, g, s, last)
            self.s_silu.wait(e, s + 1, g)
            e.tensor_tensor(self.hb[:, b, :], self.hb[:, b, :], k.psum[:, 2 * b + 1, :],
                            ALU.mult) @ self.s_t
            if tail and t in (2, 4):
                tail.norm(e, c - 1, t // 2 - 1)
            if self.s_h:
                self.s_cb.wait(e, s + 1, g)
                self.s_t.wait(e, s + 1, g)
                e.tensor_tensor(self.hb[:, b, :], self.hb[:, b, :], k.psum[:, 4, :],
                                ALU.mult) @ self.s_h
            if c and t == 0:
                take(g, c - 1)
            elif s == 0 and not isinstance(g, int):
                take(g - 1, NCH - 1)
            if tail and t in (1, 3):
                tail.add(e, c - 1, t // 2)
            self.s_hH.wait(e, s + 1, g)
            self.s_dn.wait(e, s - 1, g)
            e.tensor_tensor(self.hL[:, b, :], self.hb[:, b, :], self.hH[:, b, :].bitcast(F32),
                            ALU.subtract) @ self.s_hL
            if tail and t in (1, 3):
                tail.stats(e, c - 1, t // 2)
            if tail and t in (2, 4):
                tail.low(e, c - 1, t // 2 - 1)
            if s == self.S - 1 and last:
                take(g, NCH - 1)

        self.over_groups(e, step)
        self.after(self.tail.dve, e, self.next and self.next.lead_dve)


class _Shifted:

    def __init__(self, sem, shift):
        self.sem, self.shift = sem, shift

    def wait(self, eng, count, c):
        self.sem.wait(eng, self.shift + c + count)


class Entry:

    PAIRS = 2 * NCH
    ROUTES = {3: (0,), 5: (1,), 7: (2,)}
    BLOCKS = {5: (0,), 6: (1,), 7: (2, 3)}

    def __init__(self, k, x, tail, prep):
        self.k, self.x, self.tail, self.prep = k, x, tail, prep

    def sync(self, e):
        for c in range(NCH):
            e.dma_start(self.k.X[:, 4 * c:4 * c + 4, :],
                        self.x[c * CHUNK:(c + 1) * CHUNK, :].rearrange("(n p) f -> p n f", p=P)
                        ).then_inc(self.tail.s_in[c].sem, 16)

    def tensor(self, e):
        t, ps = self.tail, self.k.psum

        def route(c):
            t.logits(e, c, ps[:, 4, :])
            t.turn_logits(e, c, ps[:, 5, :], 4 * c)

        for q in range(self.PAIRS):
            t.pe(e, q // 2, 2 * (q % 2) + 1)
            for c in self.ROUTES.get(q, ()):
                route(c)
            for n in self.BLOCKS.get(q, ()):
                self.prep.tensor(e, n)
        route(NCH - 1)
        self.prep.tensor(e, Prep.NB)
        for c in range(NCH):
            t.turn_gates(e, c, ps[:, 4 + c, :], 4 * c)

    def scalar(self, e):
        t, ps = self.tail, self.k.psum
        for q in range(self.PAIRS):
            t.act(e, q // 2, 2 * (q % 2) + 1)
            for c in self.ROUTES.get(q, ()):
                t.keep_logits(e, c, ps[:, 4, :])
            for n in self.BLOCKS.get(q, ()):
                self.prep.scalar(e, n)
        t.keep_logits(e, NCH - 1, ps[:, 4, :])
        t.exps(e, 0)
        self.prep.scalar(e, Prep.NB)
        for c in range(NCH):
            t.gates_hi(e, c, ps[:, 4 + c, :])

    def vector(self, e):
        t, ps = self.tail, self.k.psum
        for q in range(self.PAIRS + 2):
            if q < self.PAIRS:
                t.add(e, q // 2, q % 2)
                t.stats(e, q // 2, q % 2)
            if 1 <= q <= self.PAIRS:
                t.norm(e, (q - 1) // 2, (q - 1) % 2)
            if q >= 2:
                t.low(e, (q - 2) // 2, q % 2)
            for n in self.BLOCKS.get(q - 1, ()):
                self.prep.vector(e, n)
        t.choose(e, 0, ps[:, 5, :])
        for c in range(NCH):
            t.gates_lo(e, c, ps[:, 4 + c, :])

    def pool(self, e):
        for q in range(self.PAIRS):
            self.tail.pool(e, q // 2, 2 * (q % 2))


class Scan:

    def __init__(self, k, tag, ins, before, tail):
        self.k, self.ins, self.before, self.tail = k, ins, before, tail
        k.kind = tag
        self.s_in = Sem(k, "in", 8)
        self.s_hp = Sem(k, "hp", 4)
        self.s_cv = Sem(k, "cv", 4)
        self.s_sg = Sem(k, "sg", 4)
        self.s_pad = Sem(k, "pad", 1)
        self.s_conv = Sem(k, "conv", 3)
        self.s_tap = Sem(k, "tap", 3)
        self.s_sum = Sem(k, "sum", 3)
        self.s_u = Sem(k, "u", 4)
        self.s_uh = Sem(k, "uh", 4)
        self.s_ul = Sem(k, "ul", 4)
        self.s_xp = Sem(k, "xp", 2)
        self.s_sq = Sem(k, "sq", 2)
        self.s_mm = Sem(k, "mm", 2)
        self.s_ln = Sem(k, "ln", 2)
        self.s_rt = Sem(k, "rt", 2)
        self.s_xw = Sem(k, "xw", 2)
        self.s_tsw = Sem(k, "tsw", 2)
        self.s_th = Sem(k, "th", 2)
        self.s_tsl = Sem(k, "tsl", 2)
        self.s_dt = Sem(k, "dt", 4)
        self.s_abs = Sem(k, "abs", 4)
        self.s_e = Sem(k, "e", 2)
        self.s_relu = Sem(k, "relu", 4)
        self.s_l = Sem(k, "l", 2)
        self.s_lost = Sem(k, "lost", 2)
        self.s_rc = Sem(k, "rc", 2)
        self.s_delta = Sem(k, "delta", 2)
        self.s_dtu = Sem(k, "dtu", 2)
        self.s_dz = Sem(k, "dz", 1)
        self.s_bB = Sem(k, "bB", NST)
        self.s_bC = Sem(k, "bC", NST)
        self.s_bs = Sem(k, "bs", NST)
        self.s_dA = Sem(k, "dA", NST)
        self.s_m0 = Sem(k, "m0", 1)
        self.s_m1 = Sem(k, "m1", NST - 1)
        self.s_scan = Sem(k, "scan", NST)
        self.s_z = Sem(k, "z", NST - 1)
        self.s_zb = Sem(k, "zb", IB)
        self.s_y = Sem(k, "y", NST - 1)
        self.s_yb = Sem(k, "yb", IB)
        self.s_yg = Sem(k, "yg", IB)
        self.s_yh = Sem(k, "yh", IB)
        self.s_yl = Sem(k, "yl", IB)
        self.s_o = Sem(k, "o", 1)
        self.s_fin = Sem(k, "fin", 1)
        self.s_v = Sem(k, "v", 12)
        self.s_load = Sem(k, "load")
        self.s_wh, self.s_wl = Sem(k, "wh"), Sem(k, "wl")
        self.s_one = Sem(k, "one")
        tail.src_ready, tail.src = self.s_fin, lambda c: self.fin
        a = Arena(k, tag)
        new = a.new
        self.wcols = [KB * 2 * IN, IB * XP, IN, IB * HID]
        total = sum(self.wcols)
        self.wH, self.wL = new("w_hi", [P, total], F32R), new("w_lo", [P, total], F32R)
        self.u = new("u", [P, IB, CHUNK])
        self.sg = new("silu_gate", [P, IB, CHUNK])
        at = a.off
        self.delta = new("delta", [P, IB, CHUNK])
        self.dtu = new("delta_u", [P, IB, CHUNK])
        self.hpad = new("conv_in", [P, IB, 2, SEQ + KCONV - 1], over=at)
        at = a.off
        self.dA = new("decay", [P, 2, IB, CHUNK])
        small = Arena(k, tag)
        small.off = at
        self.sq = [small.new(f"squares{i}", [n, CHUNK]) for i, n in enumerate(self.NORM)]
        self.rt = [small.new(f"rms_inv{i}", [n, CHUNK]) for i, n in enumerate(self.NORM)]
        self.wt = [small.new(f"weighted{i}", [n, CHUNK]) for i, n in enumerate(self.NORM)]
        self.tsH = small.new("ts_hi", [P, CHUNK], F32R)
        self.tsL = small.new("ts_lo", [P, CHUNK], F32R)
        assert small.off <= a.off
        at = a.off
        self.st = [new(f"state{i}", [P, IB, CHUNK]) for i in range(self.NBUF)]
        self.raw = new("w_raw", [P, total], over=at)
        self.Bs = new("B_all", [P, 2, CHUNK])
        self.bc = new("BC", [64, CHUNK], F32R)
        self.fin = new("out", [P, KB, CHUNK], over=at + 3 * 4 * IB * CHUNK)
        self.cw, self.cb = new("conv_w", [P, IB, KCONV]), new("conv_b", [P, IB])
        self.lnw = [new("dt_ln", [P, 1]), new("bc_ln", [2 * NST, 1])]
        self.mean = [new("mean_ts", [P, P]), new("mean_bc", [2 * NST, 2 * NST])]
        self.eps = new("eps", [P, 1])
        self.dtb, self.A, self.D = new("dt_bias", [P, IB]), new("A", [P, IB, NST]), new("D", [P, IB])
        self.eye = new("state_pick_raw", [64, 2 * NST])
        self.pick = new("state_pick", [64, 2 * NST], F32R)
        assert a.off <= k.nc.sbuf_usable_end, a.off
        assert at >= SwiGLU.MOE_END + k.arena
        acc = Arena(k, tag)
        acc.off = k.acc_at
        self.uH, self.uL = acc.new("u_hi", [P, IB, CHUNK], F32R), acc.new("u_lo", [P, IB, CHUNK], F32R)

    NBUF = 4
    NORM = (RANK, 2 * NST)

    def weight(self, n, cols):
        at = sum(self.wcols[:n])
        s = slice(at + cols.start, at + cols.stop)
        return self.wH[:, s], self.wL[:, s]

    def run(self, e, pre, main, fn, lead=None):
        slots = 7 if self.tail.route else 4

        def tail_of(c):
            return lambda a, b: [fn(e, c, slot) for slot in range(a, min(b, slots))]

        pre(0, lambda a, b: None)
        with e.Fori(0, NCH - 1) as c:
            main(c, True)
            pre(c + 1, tail_of(c))
        main(NCH - 1, False)
        self.tail.final(fn, e, lead)

    def freed(self, e):
        self.s_o.wait(e, 1, NCH - 1)

    def lead_act(self, e):
        self.prev.freed(e)
        e.wait_ge(self.s_load.sem, 16 * self.LOADS)
        n = self.wcols[0]
        e.activation(self.wH[:, 0:n], self.raw[:, 0:n], ACT.Copy) @ self.s_wh

    def lead_dve(self, e):
        self.s_wh.wait(e, 1)
        n = self.wcols[0]
        e.tensor_tensor(self.wL[:, 0:n], self.raw[:, 0:n], self.wH[:, 0:n].bitcast(F32),
                        ALU.subtract) @ self.s_wl

    def rest_act(self, e):
        n = self.wcols[0]
        e.activation(self.wH[:, n:], self.raw[:, n:], ACT.Copy) @ self.s_wh

    def rest_dve(self, e):
        n = self.wcols[0]
        self.s_wh.wait(e, 2)
        e.tensor_tensor(self.wL[:, n:], self.raw[:, n:], self.wH[:, n:].bitcast(F32),
                        ALU.subtract) @ self.s_wl
        self.s_wl.wait(e, 2)

    LOADS = 13

    def load(self, e):
        i = self.ins
        at = 0
        for w, n in zip(("W_in", "Wx", "Wdt", "Wout"), self.wcols):
            e.dma_start(self.raw[:, at:at + n], i[w]).then_inc(self.s_load.sem, 16)
            at += n
        for dst, name in ((self.cw, "conv_w"), (self.cb, "conv_b"), (self.lnw[0], "dt_ln"),
                          (self.lnw[1], "bc_ln"), (self.dtb, "dt_bias"), (self.A, "A"), (self.D, "D"),
                          (self.eye, "state_pick"), (self.mean[1], "mean_bc")):
            e.dma_start(dst[:], i[name]).then_inc(self.s_load.sem, 16)

    def sync(self, e):
        if self.tail.last:
            self.tail.sync(e)

    def pool(self, e):
        k = self.k
        self.before.ready(e, NCH - 1)
        e.memset(self.mean[0][:], 1.0 / RANK) @ self.s_one
        e.memset(self.eps[:], EPS) @ self.s_one

        def pre(c, tail):
            self.s_scan.wait(e, 0, c)
            k.own(e)
            e.memset(self.hpad[:, :, :, 0:KCONV - 1], 0.0) @ self.s_pad
            tail(0, 1)
            conv(c)
            tail(2, 4)
            tail(4, 7)
            self.s_dt.wait(e, 4, c)
            self.s_tsl.wait(e, 2, c)
            k.own(e)
            e.memset(self.dA[:].rearrange("p a b (s t) -> p (a b s) t", t=SEQ)[:, :, 0], 0.0) @ self.s_dz
            for h in range(2):
                m = slice(2 * h, 2 * h + 2)
                self.s_relu.wait(e, 2 * h + 2, c)
                self.s_lost.wait(e, h + 1, c)
                e.tensor_tensor(self.delta[:, m, :], self.delta[:, m, :], self.st[2][:, m, :],
                                ALU.add) @ self.s_rc

        def conv(c):
            m, parts = IB - 1, (self.sq[0], self.rt[0], self.wt[0])
            self.s_cv.wait(e, m + 1, c)
            self.s_hp.wait(e, m + 1, c)
            for tap in range(KCONV - 1):
                k.own(e)
                e.tensor_scalar(parts[tap][:].rearrange("p (s t) -> p s t", s=2),
                                self.hpad[:, m, :, tap:tap + SEQ], self.cw[:, m, tap:tap + 1], None,
                                ALU.mult) @ self.s_tap
            for tap in range(KCONV - 1):
                self.s_tap.wait(e, tap + 1, c)
                if tap:
                    self.s_sum.wait(e, tap, c)
                e.tensor_tensor(self.u[:, m, :], self.u[:, m, :], parts[tap][:], ALU.add) @ self.s_sum

        def main(c, more):
            self.s_dtu.wait(e, 2, c)
            for n in range(1, NST):
                self.s_bs.wait(e, n + 1, c)
                if n >= self.NBUF:
                    self.s_y.wait(e, n - self.NBUF + 1, c)
                e.tensor_tensor(self.st[n % self.NBUF][:], self.dtu[:],
                                self.Bs[:, n % 2, :].unsqueeze(1).broadcast_to([P, IB, CHUNK]),
                                ALU.mult) @ self.s_m1

        self.run(e, pre, main, self.tail.pool)

    def tensor(self, e):
        k, ps = self.k, self.k.psum
        self.s_wl.wait(e, 1)

        def project(c, m, bank):
            cols = bass.ds(c * CHUNK, CHUNK)
            for kb in range(KB):
                w = self.weight(0, slice(kb * 2 * IN + m * P, kb * 2 * IN + (m + 1) * P))
                x = three(e, ps[:, bank, :], *w, k.xH[:, kb, cols], k.xL[:, kb, cols], kb == 0, kb == KB - 1)
            x @ self.s_in

        def x_proj(c, ib, rows=(0, 1)):
            self.s_ul.wait(e, ib + 1, c)
            for i in rows:
                a, n = ((0, RANK), (RANK, 2 * NST))[i]
                w = self.weight(1, slice(ib * XP + a, ib * XP + a + n))
                x = three(e, ps[0:n, i, :], *w, self.uH[:, ib, :], self.uL[:, ib, :], ib == 0, ib == IB - 1)
                if ib == IB - 1:
                    x @ self.s_xp

        def bcast(c, n, part):
            x = e.matmul(ps[:, 4 + 2 * (n % 2) + part, :],
                         self.pick[:, part * NST + n:part * NST + n + 1].broadcast_to([64, P]), self.bc[:],
                         start=True, stop=True)
            x @ (self.s_bC if part else self.s_bB)

        def pre(c, tail):
            tail(0, 1)
            for m in range(3):
                project(c, IB + m, IB + m)
            tail(1, 2)
            self.s_cv.wait(e, 2, c)
            x_proj(c, 0)
            tail(2, 3)
            self.s_sg.wait(e, 1, c)
            project(c, IB + 3, 4)
            x_proj(c, 1)
            tail(3, 4)
            x_proj(c, 2)
            tail(4, 5)
            x_proj(c, 3, (0,))
            tail(5, 6)
            x_proj(c, 3, (1,))
            self.s_cv.wait(e, 4, c)
            for i, n in enumerate(self.NORM):
                self.s_sq.wait(e, i + 1, c)
                k.own(e)
                e.matmul(ps[0:n, 2 + i, :], self.mean[i][:], self.sq[i][:], start=True, stop=True) @ self.s_mm
            tail(6, 7)
            self.s_xw.wait(e, 2, c)
            self.s_ln.wait(e, 2, c)
            self.s_tsl.wait(e, 1, c)
            for m in range(IB):
                w = self.weight(2, slice(m * P, (m + 1) * P))
                three(e, ps[:, m, :], *w, self.tsH[:], self.tsL[:], True, True) @ self.s_dt
            self.s_th.wait(e, 2, c)
            self.s_tsl.wait(e, 2, c)
            self.s_sg.wait(e, 4, c)
            bcast(c, 0, 0)
            bcast(c, 0, 1)
            bcast(c, 1, 0)
            self.s_bs.wait(e, 1, c)
            bcast(c, 2, 0)

        def main(c, more):
            self.tail.idle(e, c)
            bcast(c, 1, 1)
            self.s_e.wait(e, 2, c)
            self.s_relu.wait(e, 4, c)
            for n in range(NST):
                if n + 3 < NST:
                    self.s_bs.wait(e, n + 2, c)
                    bcast(c, n + 3, 0)
                last = n == NST - 1
                if not last:
                    self.s_z.wait(e, n + 1, c)
                for m in range(IB):
                    if last:
                        self.s_zb.wait(e, m + 1, c)
                    x = e.matmul(ps[:, m, :], k.ident[:], self.st[n % self.NBUF][:, m, :], start=(n == 0), stop=last)
                    if last:
                        x @ self.s_yb
                if not last:
                    x @ self.s_y
                if n + 2 < NST:
                    bcast(c, n + 2, 1)
            for ib in range(IB):
                self.s_yl.wait(e, ib + 1, c)
                for ob in range(KB):
                    w = self.weight(3, slice(ib * HID + ob * P, ib * HID + (ob + 1) * P))
                    x = three(e, ps[:, 4 + ob, :], *w, self.uH[:, ib, :], self.uL[:, ib, :],
                              ib == 0, ib == IB - 1)
                if ib == IB - 1:
                    x @ self.s_o
                if more:
                    project(c + 1, ib, ib)

        self.before.ready(e, NCH - 1)
        for m in range(IB):
            project(0, m, m)
        self.s_wl.wait(e, 2)
        self.s_one.wait(e, 2)
        self.run(e, pre, main, self.tail.pe)

    def scalar(self, e):
        k, ps = self.k, self.k.psum
        self.before.ready(e, NCH - 1)
        self.rest_act(e)
        self.s_one.wait(e, 2)

        def high(c, m):
            if m == IB - 1:
                self.s_sum.wait(e, KCONV - 1, c)
            else:
                self.s_conv.wait(e, m + 1, c)
            e.activation(self.u[:, m, :], self.u[:, m, :], ACT.Silu) @ self.s_u
            self.s_u.wait(e, m + 1, c)
            e.activation(self.uH[:, m, :], self.u[:, m, :], ACT.Copy) @ self.s_uh

        def gate(c, m, bank):
            self.s_in.wait(e, IB + m + 1, c)
            e.activation(self.sg[:, m, :], ps[:, bank, :], ACT.Silu) @ self.s_sg

        def conv_in(c, m):
            if m == 0:
                self.s_pad.wait(e, 1, c)
            self.s_in.wait(e, m + 1, c)
            e.activation(self.hpad[:, m, :, KCONV - 1:], ps[:, m, :].rearrange("p (s t) -> p s t", s=2),
                         ACT.Copy) @ self.s_hp
            e.activation(self.u[:, m, :], ps[:, m, :], ACT.Identity, bias=self.cb[:, m:m + 1],
                         scale=self.cw[:, m, KCONV - 1:KCONV]) @ self.s_cv

        def pre(c, tail):
            gate(c, 0, 4)
            high(c, 0)
            high(c, 1)
            tail(0, 2)
            gate(c, 1, 5)
            high(c, 2)
            gate(c, 2, 6)
            high(c, 3)
            tail(2, 4)
            gate(c, 3, 4)
            tail(4, 6)
            for i, n in enumerate(self.NORM):
                self.s_xp.wait(e, i + 1, c)
                e.activation(self.sq[i][:], ps[0:n, i, :], ACT.Square) @ self.s_sq
            for i, n in enumerate(self.NORM):
                self.s_mm.wait(e, i + 1, c)
                e.activation(self.rt[i][:], ps[0:n, 2 + i, :], ACT.Ln, bias=self.eps[0:n, :]) @ self.s_ln
            for i in range(2):
                self.s_ln.wait(e, i + 1, c)
                e.activation(self.rt[i][:], self.rt[i][:], ACT.Exp, scale=-0.5) @ self.s_rt
            for i, n in enumerate(self.NORM):
                e.activation(self.wt[i][:], ps[0:n, i, :], ACT.Copy, scale=self.lnw[i][:]) @ self.s_xw
            for i, dst in enumerate((self.tsH[:], self.bc[0:2 * NST, :])):
                self.s_tsw.wait(e, i + 1, c)
                e.activation(dst, self.wt[i][:], ACT.Copy) @ self.s_th
            tail(6, 7)
            ax, ln = self.st[0], self.st[1]
            for m in range(IB):
                self.s_dt.wait(e, m + 1, c)
                e.activation(ax[:, m, :], ps[:, m, :], ACT.Abs, bias=self.dtb[:, m:m + 1]) @ self.s_abs
            for h in range(2):
                m = slice(2 * h, 2 * h + 2)
                self.s_abs.wait(e, 2 * h + 2, c)
                e.activation(ax[:, m, :], ax[:, m, :], ACT.Exp, scale=-1.0) @ self.s_e
            for h in range(2):
                m = slice(2 * h, 2 * h + 2)
                self.s_e.wait(e, h + 1, c)
                e.activation(ln[:, m, :], ax[:, m, :], ACT.Ln, bias=1.0) @ self.s_l
            for n in range(2):
                keep_b(c, n)

        def keep_b(c, n):
            self.s_bB.wait(e, n + 1, c)
            if n == 2:
                self.s_m0.wait(e, 1, c)
            if n >= 3:
                self.s_m1.wait(e, n - 2, c)
            e.activation(self.Bs[:, n % 2, :], ps[:, 4 + 2 * (n % 2), :], ACT.Copy) @ self.s_bs

        def main(c, more):
            self.s_dz.wait(e, 1, c)
            for n in range(NST):
                if n >= 2:
                    keep_b(c, n)
                if n >= 2:
                    self.s_scan.wait(e, n - 1, c)
                for m in range(IB):
                    if n == 0 and m % 2 == 0:
                        self.s_delta.wait(e, m // 2 + 1, c)
                    x = e.activation(
                        self.dA[:, n % 2, m, :].rearrange("p (s t) -> p s t", s=2)[:, :, 1:],
                        self.delta[:, m, :].rearrange("p (s t) -> p s t", s=2)[:, :, 1:],
                        ACT.Exp, scale=self.A[:, m, n:n + 1])
                x @ self.s_dA
            for m in range(IB):
                self.s_yg.wait(e, m + 1, c)
                e.activation(self.uH[:, m, :], self.u[:, m, :], ACT.Copy) @ self.s_yh
                if more and m:
                    conv_in(c + 1, m - 1)
            self.s_o.wait(e, 1, c)
            e.activation(self.fin[:], ps[:, 4:6, :], ACT.Copy) @ self.s_fin
            if more:
                conv_in(c + 1, IB - 1)

        for m in range(IB):
            conv_in(0, m)
        self.run(e, pre, main, self.tail.act, self.next and self.next.lead_act)

    def vector(self, e):
        k, ps = self.k, self.k.psum
        self.before.ready(e, NCH - 1)
        e.wait_ge(self.s_load.sem, 16 * self.LOADS)
        e.tensor_copy(self.pick[:], self.eye[:])
        self.rest_dve(e)

        def low(c, m, high, sem):
            high.wait(e, m + 1, c)
            e.tensor_tensor(self.uL[:, m, :], self.u[:, m, :], self.uH[:, m, :].bitcast(F32),
                            ALU.subtract) @ sem

        def conv(c, m):
            self.s_cv.wait(e, m + 1, c)
            self.s_hp.wait(e, m + 1, c)
            um = self.u[:, m, :].rearrange("p (s t) -> p s t", s=2)
            for tap in range(KCONV - 1):
                last = tap == KCONV - 2
                e.scalar_tensor_tensor(um, self.hpad[:, m, :, tap:tap + SEQ], self.cw[:, m, tap:tap + 1],
                                       um, ALU.mult, ALU.add) @ (self.s_conv if last else self.s_v)
                if not last:
                    self.s_v.wait(e, 2 * m + tap + 1, c)

        def pre(c, tail):
            conv(c, 0)
            conv(c, 1)
            tail(0, 1)
            conv(c, 2)
            low(c, 0, self.s_uh, self.s_ul)
            tail(1, 2)
            low(c, 1, self.s_uh, self.s_ul)
            low(c, 2, self.s_uh, self.s_ul)
            tail(2, 3)
            low(c, 3, self.s_uh, self.s_ul)
            tail(3, 4)
            tail(4, 6)
            for i in range(2):
                self.s_rt.wait(e, i + 1, c)
                self.s_xw.wait(e, i + 1, c)
                e.tensor_tensor(self.wt[i][:], self.wt[i][:], self.rt[i][:], ALU.mult) @ self.s_tsw
            for i, (lo, hi) in enumerate(((self.tsL[:], self.tsH[:]),
                                          (self.bc[32:32 + 2 * NST, :], self.bc[0:2 * NST, :]))):
                self.s_th.wait(e, i + 1, c)
                e.tensor_tensor(lo, self.wt[i][:], hi.bitcast(F32), ALU.subtract) @ self.s_tsl
            tail(6, 7)
            for m in range(IB):
                self.s_abs.wait(e, m + 1, c)
                e.tensor_scalar(self.delta[:, m, :], ps[:, m, :], self.dtb[:, m:m + 1], 0.0, ALU.add,
                                ALU.max) @ self.s_relu
            ax, ln, t = self.st[:3]
            for h in range(2):
                m = slice(2 * h, 2 * h + 2)
                self.s_e.wait(e, h + 1, c)
                e.tensor_scalar(t[:, m, :], ax[:, m, :], 1.0, 1.0, ALU.add, ALU.subtract) @ self.s_v
                self.s_v.wait(e, 6 + h + 1, c)
                e.tensor_tensor(t[:, m, :], ax[:, m, :], t[:, m, :], ALU.subtract) @ self.s_lost
            for h in range(2):
                m = slice(2 * h, 2 * h + 2)
                self.s_l.wait(e, h + 1, c)
                self.s_rc.wait(e, h + 1, c)
                e.tensor_tensor(self.delta[:, m, :], self.delta[:, m, :], ln[:, m, :], ALU.add) @ self.s_delta
                self.s_delta.wait(e, h + 1, c)
                e.tensor_tensor(self.dtu[:, m, :], self.delta[:, m, :], self.u[:, m, :], ALU.mult) @ self.s_dtu

        def flat(x):
            return x.rearrange("p m t -> p (m t)")

        def main(c, more):
            self.s_dtu.wait(e, 2, c)
            self.s_bs.wait(e, 1, c)
            e.tensor_tensor(self.st[0][:], self.dtu[:],
                            self.Bs[:, 0, :].unsqueeze(1).broadcast_to([P, IB, CHUNK]), ALU.mult) @ self.s_m0
            self.s_m0.wait(e, 1, c)
            for n in range(NST):
                st, cb = self.st[n % self.NBUF], ps[:, 5 + 2 * (n % 2), :]
                self.s_dA.wait(e, n + 1, c)
                if n:
                    self.s_m1.wait(e, n, c)
                s = flat(st[:])
                e.tensor_tensor_scan(s, flat(self.dA[:, n % 2, :, :]), s, 0.0, ALU.mult, ALU.add) @ self.s_scan
                self.s_scan.wait(e, n + 1, c)
                self.s_bC.wait(e, n + 1, c)
                if n < NST - 1:
                    e.tensor_tensor(st[:], st[:], cb.unsqueeze(1).broadcast_to([P, IB, CHUNK]),
                                    ALU.mult) @ self.s_z
                else:
                    for m in range(IB):
                        e.tensor_tensor(st[:, m, :], st[:, m, :], cb, ALU.mult) @ self.s_zb
            for m in range(IB):
                self.s_yb.wait(e, m + 1, c)
                e.scalar_tensor_tensor(self.u[:, m, :], self.u[:, m, :], self.D[:, m:m + 1],
                                       ps[:, m, :], ALU.mult, ALU.add) @ self.s_v
                self.s_v.wait(e, 8 + m + 1, c)
                e.tensor_tensor(self.u[:, m, :], self.u[:, m, :], self.sg[:, m, :], ALU.mult) @ self.s_yg
                if m:
                    low(c, m - 1, self.s_yh, self.s_yl)
            low(c, IB - 1, self.s_yh, self.s_yl)

        self.run(e, pre, main, self.tail.dve, self.next and self.next.lead_dve)


class Attention:

    UNITS = 16

    def __init__(self, k, tag, ins, before, tail):
        self.k, self.ins, self.before, self.tail = k, ins, before, tail
        k.kind = tag
        U = self.UNITS
        self.s_in = Sem(k, "in", 8)
        self.s_q = Sem(k, "q", 4)
        self.s_k = Sem(k, "k", 4)
        self.s_vT = Sem(k, "vT", 2)
        self.s_vTs = Sem(k, "vTs", 2)
        self.s_vt = Sem(k, "vt", 1)
        self.s_v = Sem(k, "v", 2)
        self.s_S = Sem(k, "S", U)
        self.s_max = Sem(k, "max", U)
        self.s_nm = Sem(k, "nm", U)
        self.s_exp = Sem(k, "exp", U)
        self.s_T = Sem(k, "T", U)
        self.s_pt = Sem(k, "pt", U)
        self.s_pv = Sem(k, "pv", U)
        self.s_rec = Sem(k, "rec", U)
        self.s_pn = Sem(k, "pn", U)
        self.s_oH = Sem(k, "oH", 4)
        self.s_oL = Sem(k, "oL", 4)
        self.s_o = Sem(k, "o", 1)
        self.s_fin = Sem(k, "fin", 1)
        self.s_vz = Sem(k, "vz")
        self.s_load, self.s_wh, self.s_wl = Sem(k, "load"), Sem(k, "wh"), Sem(k, "wl")
        tail.src_ready, tail.src = self.s_fin, lambda c: self.fin
        a = Arena(k, tag)
        new = a.new
        self.wcols = [KB * NGRP * P, KB * NGRP * P, KB * HID, NGRP * HID]
        total = sum(self.wcols)
        self.wH, self.wL = new("w_hi", [P, total], F32R), new("w_lo", [P, total], F32R)
        self.q, self.kk = new("q", [P, NGRP, CHUNK]), new("k", [P, NGRP, CHUNK])
        self.vT, self.v = new("vT", [P, KB, CHUNK]), new("v", [P, 4, HEADS, HSLOT])
        self.one = new("ident_r", [P, P], F32R)
        self.mask = new("mask", [P, P], F32R)
        self.bqs = new("bq_scaled", [P, NGRP])
        a.off = max(a.off, SwiGLU.FFN_END + k.arena)
        at = a.off
        self.raw = new("w_raw", [P, total])
        end, a.off = a.off, at
        self.p0, self.p1 = new("p0", [P, 3, 2, P]), new("p1", [P, 3, 2, SEQ])
        self.pt = new("pT", [P, 2, 2, 3 * P])
        a.off = max(a.off, end)
        self.pat, self.mraw = new("slopes", [P, NGRP, SEQ]), new("mask_raw", [P, P])
        self.bq, self.bk = new("bq", [P, NGRP]), new("bk", [P, NGRP])
        self.bv, self.bo = new("bv", [P, KB]), new("bo", [P, KB])
        self.mx, self.nm = new("max", [P, 3, 4]), new("neg_max", [P, 3, 4])
        self.sums, self.rec = new("sums", [P, 3, 4]), new("recip", [P, 3, 4])
        self.fin = new("out", [P, KB, CHUNK])
        acc = Arena(k, tag)
        acc.off = k.acc_at
        self.oH, self.oL = acc.new("o_hi", [P, NGRP, CHUNK], F32R), acc.new("o_lo", [P, NGRP, CHUNK], F32R)
        assert a.off <= SwiGLU.ffn_raw_at(k), a.off

    LOADS = 10

    weight, run, freed = Scan.weight, Scan.run, Scan.freed
    lead_act, lead_dve, rest_act, rest_dve = Scan.lead_act, Scan.lead_dve, Scan.rest_act, Scan.rest_dve

    def load(self, e):
        i, at = self.ins, 0
        for w, n in zip(("Wq", "Wk", "Wv", "Wo"), self.wcols):
            e.dma_start(self.raw[:, at:at + n], i[w]).then_inc(self.s_load.sem, 16)
            at += n
        for dst, name in ((self.pat, "slopes"), (self.mraw, "mask"), (self.bq, "bq"), (self.bk, "bk"),
                          (self.bv, "bv"), (self.bo, "bo")):
            e.dma_start(dst[:], i[name]).then_inc(self.s_load.sem, 16)

    def sync(self, e):
        self.prev.before.ready(e, NCH - 1)
        self.load(e)
        if self.tail.last:
            self.tail.sync(e)

    def pool(self, e):
        self.before.ready(e, NCH - 1)
        e.memset(self.v[:], 0.0) @ self.s_vz

        self.run(e, lambda c, tail: tail(0, 4), lambda c, more: None, self.tail.pool)

    @staticmethod
    def unit(u):
        b, i = divmod(u, 8)
        r, gg = i % HGRP, i // HGRP
        return b, HSLOT * r, [(g * HGRP + r, g) for g in (2 * gg, 2 * gg + 1)]

    def tensor(self, e):
        k, ps = self.k, self.k.psum
        self.s_wl.wait(e, 1)

        def scores(c, u):
            b, r, heads = self.unit(u)
            s = 2 * (u % 2)
            if u >= 2:
                self.s_exp.wait(e, u - 1, c)
            for j in range(2):
                n = (j + 1) * P
                for x, (h, g) in enumerate(heads):
                    e.matmul(ps[:, s + j, x * n:(x + 1) * n],
                             self.q[r:r + HSLOT, g, b * SEQ + j * P:b * SEQ + (j + 1) * P],
                             self.kk[r:r + HSLOT, g, b * SEQ:b * SEQ + n], start=True, stop=False)
                    m = e.matmul(ps[:, s + j, (x + 1) * n - P:(x + 1) * n], self.one[:], self.mask[:],
                                 start=False, stop=True)
            m @ self.s_S

        def turn(c, u):
            self.s_pn.wait(e, u + 1, c)
            if u:
                self.s_pt.wait(e, u, c)
            for x in range(2):
                for n, block in enumerate((self.p0[:, u % 3, x, :], self.p1[:, u % 3, x, 0:P],
                                           self.p1[:, u % 3, x, P:])):
                    m = e.transpose(ps[:, 4 + x, n * P:(n + 1) * P], block, k.ident[:])
            m @ self.s_T

        def values(c, u):
            b, r, heads = self.unit(u)
            bank = 6 + (u % 8) // 4
            self.s_pt.wait(e, u + 1, c)
            if u >= 8 and u % 4 == 0:
                self.s_oL.wait(e, u // 4 - 1, c)
            for x, (h, g) in enumerate(heads):
                pt = self.pt[:, u % 2, x, :]
                e.matmul(ps[r:r + HSLOT, bank, x * SEQ:(x + 1) * SEQ], self.v[:, 2 * b, h, :],
                         pt[:, 0:SEQ], start=True, stop=False)
                m = e.matmul(ps[r:r + HSLOT, bank, x * SEQ + P:(x + 1) * SEQ], self.v[:, 2 * b + 1, h, :],
                             pt[:, SEQ:], start=False, stop=True)
            m @ self.s_pv

        def project(c, which, block, bank, sem):
            cols = bass.ds(c * CHUNK, CHUNK)
            for kb in range(KB):
                n = self.wcols[which] // KB
                w = self.weight(which, slice(kb * n + block * P, kb * n + (block + 1) * P))
                x = three(e, ps[:, bank, :], *w, k.xH[:, kb, cols], k.xL[:, kb, cols], kb == 0, kb == KB - 1)
            x @ sem

        def queries(c, blocks):
            for g in blocks:
                project(c, 0, g, g, self.s_in)

        def keys(c, g):
            if g:
                self.s_q.wait(e, g, c)
            project(c, 1, g, (6, 0, 1, 2)[g], self.s_in)

        def pre(c, tail):
            tail(0, 1)
            keys(c, 0)
            keys(c, 1)
            tail(1, 2)
            keys(c, 2)
            tail(2, 3)
            keys(c, 3)
            self.s_q.wait(e, 4, c)
            project(c, 2, 0, 3, self.s_vT)
            tail(3, 4)
            project(c, 2, 1, 4, self.s_vT)
            self.s_k.wait(e, 1, c)
            self.s_vTs.wait(e, 2, c)
            for j in range(4):
                for kb in range(KB):
                    x = e.transpose(ps[:, 5 + j // 2, (j % 2) * HID + kb * P:(j % 2) * HID + (kb + 1) * P],
                                    self.vT[:, kb, j * P:(j + 1) * P], k.ident[:])
            x @ self.s_vt

        def main(c, more):
            self.tail.idle(e, c)
            self.s_k.wait(e, 4, c)
            scores(c, 0)
            scores(c, 1)
            self.s_v.wait(e, 2, c)
            for u in range(self.UNITS + 1):
                if u + 2 < self.UNITS:
                    scores(c, u + 2)
                if u:
                    values(c, u - 1)
                if u < self.UNITS:
                    turn(c, u)
            if more:
                self.s_exp.wait(e, self.UNITS, c)
                queries(c + 1, (0, 1))
            self.s_oL.wait(e, 4, c)
            for ob in range(KB):
                for g in range(NGRP):
                    w = self.weight(3, slice(g * HID + ob * P, g * HID + (ob + 1) * P))
                    x = three(e, ps[:, 4 + ob, :], *w, self.oH[:, g, :], self.oL[:, g, :],
                              g == 0, g == NGRP - 1)
            x @ self.s_o
            if more:
                queries(c + 1, (2, 3))

        self.before.ready(e, NCH - 1)
        queries(0, range(NGRP))
        self.s_wl.wait(e, 2)
        self.run(e, pre, main, self.tail.pe)

    def scalar(self, e):
        k, ps = self.k, self.k.psum
        self.before.ready(e, NCH - 1)
        self.rest_act(e)
        self.s_wl.wait(e, 2)
        self.s_vz.wait(e, 1)

        def exps(c, u):
            b, r, heads = self.unit(u)
            s = 2 * (u % 2)
            self.s_nm.wait(e, u + 1, c)
            if u >= 3:
                self.s_T.wait(e, u - 2, c)
            for x in range(2):
                e.activation(self.p0[:, u % 3, x, :], ps[:, s, x * P:(x + 1) * P], ACT.Exp,
                             bias=self.nm[:, u % 3, x:x + 1], accum_out=self.sums[:, u % 3, x:x + 1])
                m = e.activation(self.p1[:, u % 3, x, :], ps[:, s + 1, x * SEQ:(x + 1) * SEQ], ACT.Exp,
                                 bias=self.nm[:, u % 3, 2 + x:3 + x],
                                 accum_out=self.sums[:, u % 3, 2 + x:3 + x])
            m @ self.s_exp

        def out_hi(c, n):
            b, gg = divmod(n, 2)
            self.s_pv.wait(e, 4 * n + 4, c)
            e.activation(self.oH[:, 2 * gg:2 * gg + 2, b * SEQ:(b + 1) * SEQ],
                         ps[:, 6 + gg, :].rearrange("p (x t) -> p x t", x=2), ACT.Copy) @ self.s_oH

        def queries(c, blocks):
            for g in blocks:
                self.s_in.wait(e, g + 1, c)
                e.activation(self.q[:, g, :], ps[:, g, :], ACT.Identity, bias=self.bqs[:, g:g + 1],
                             scale=HD ** -0.5) @ self.s_q

        def pre(c, tail):
            tail(0, 2)
            for ob in range(KB):
                self.s_vT.wait(e, ob + 1, c)
                e.activation(self.vT[:, ob, :], ps[:, 3 + ob, :], ACT.Identity, bias=self.bv[:, ob:ob + 1]) @ self.s_vTs
                if ob == 0:
                    tail(2, 4)
            self.s_vt.wait(e, 1, c)
            for j in range(2):
                e.activation(self.v[:, 2 * j:2 * j + 2, :, 0:HD],
                             ps[:, 5 + j, :].rearrange("p (a h d) -> p a h d", a=2, d=HD), ACT.Copy) @ self.s_v

        def main(c, more):
            for u in range(self.UNITS):
                exps(c, u)
                if u >= 5 and u % 4 == 1:
                    out_hi(c, u // 4 - 1)
            out_hi(c, 3)
            if more:
                queries(c + 1, (0, 1))
            self.s_o.wait(e, 1, c)
            for ob in range(KB):
                m = e.activation(self.fin[:, ob, :], ps[:, 4 + ob, :], ACT.Identity, bias=self.bo[:, ob:ob + 1])
            m @ self.s_fin
            if more:
                queries(c + 1, (2, 3))

        queries(0, range(NGRP))
        self.run(e, pre, main, self.tail.act, self.next and self.next.lead_act)

    def vector(self, e):
        k, ps = self.k, self.k.psum
        self.before.ready(e, NCH - 1)
        e.wait_ge(self.s_load.sem, 16 * self.LOADS)
        e.tensor_copy(self.mask[:], self.mraw[:])
        e.tensor_copy(self.one[:], k.ident[:])
        e.tensor_scalar(self.bqs[:], self.bq[:], HD ** -0.5, None, ALU.mult)
        self.rest_dve(e)

        def maxima(c, u):
            s, m = 2 * (u % 2), self.mx[:, u % 3, :]
            self.s_S.wait(e, u + 1, c)
            if u >= 3:
                self.s_exp.wait(e, u - 2, c)
            e.tensor_reduce(m[:, 0:2], ps[:, s, 0:2 * P].rearrange("p (x t) -> p x t", x=2), AX_X, ALU.max)
            e.tensor_reduce(m[:, 2:4], ps[:, s + 1, :].rearrange("p (x t) -> p x t", x=2), AX_X,
                            ALU.max) @ self.s_max
            self.s_max.wait(e, u + 1, c)
            e.tensor_scalar(self.nm[:, u % 3, :], m, -1.0, None, ALU.mult) @ self.s_nm

        def divide(c, u):
            self.s_exp.wait(e, u + 1, c)
            e.reciprocal(self.rec[:, u % 3, :], self.sums[:, u % 3, :]) @ self.s_rec
            self.s_rec.wait(e, u + 1, c)
            for x in range(2):
                for p, at in ((self.p0, x), (self.p1, 2 + x)):
                    m = e.tensor_scalar(p[:, u % 3, x, :], p[:, u % 3, x, :],
                                        self.rec[:, u % 3, at:at + 1], None, ALU.mult)
            m @ self.s_pn

        def take(c, u):
            self.s_T.wait(e, u + 1, c)
            if u >= 2:
                self.s_pv.wait(e, u - 1, c)
            for x in range(2):
                m = e.tensor_copy(self.pt[:, u % 2, x, :], ps[:, 4 + x, 0:3 * P])
            m @ self.s_pt

        def out_lo(c, n):
            b, gg = divmod(n, 2)
            self.s_oH.wait(e, n + 1, c)
            at = (slice(None), slice(2 * gg, 2 * gg + 2), slice(b * SEQ, (b + 1) * SEQ))
            e.tensor_tensor(self.oL[at], ps[:, 6 + gg, :].rearrange("p (x t) -> p x t", x=2),
                            self.oH[at].bitcast(F32), ALU.subtract) @ self.s_oL

        def pre(c, tail):
            tail(0, 1)
            for g in range(NGRP):
                self.s_in.wait(e, NGRP + g + 1, c)
                bank = (6, 0, 1, 2)[g]
                e.scalar_tensor_tensor(self.kk[:, g, :].rearrange("p (s t) -> p s t", s=2),
                                       ps[:, bank, :].rearrange("p (s t) -> p s t", s=2),
                                       self.bk[:, g:g + 1],
                                       self.pat[:, g, :].unsqueeze(1).broadcast_to([P, 2, SEQ]),
                                       ALU.add, ALU.add) @ self.s_k
                if g in (1, 2):
                    tail(g, g + 1)
            tail(3, 4)

        def main(c, more):
            maxima(c, 0)
            maxima(c, 1)
            divide(c, 0)
            for u in range(self.UNITS):
                if u + 2 < self.UNITS:
                    maxima(c, u + 2)
                if u >= 5 and u % 4 == 1:
                    out_lo(c, u // 4 - 1)
                if u + 1 < self.UNITS:
                    divide(c, u + 1)
                take(c, u)
            out_lo(c, 3)

        self.run(e, pre, main, self.tail.dve, self.next and self.next.lead_dve)


class Prep:

    NB = 2 * INTER // 512
    UP = HID ** -0.5
    DOWN = INTER ** -0.5

    def __init__(self, k, ins, pack, behind):
        self.k, self.ins, self.pack = k, ins, pack
        k.kind = "prep_"
        self.s_load = Sem(k, "load")
        self.s_su = Sem(k, "su")
        self.s_mm = Sem(k, "mm")
        self.s_ev = Sem(k, "ev")
        self.s_bf = Sem(k, "bf")
        self.s_k = Sem(k, "k")
        self.s_out = Sem(k, "out")
        self.s_d = Sem(k, "d")
        arena = Arena(k, "prep_")
        arena.off = behind
        new = arena.new
        self.ug, self.dn = new("ug", [P, KB, 2 * INTER]), new("dn", [P, FFN_TILES, HID])
        self.had = new("had", [P, P])
        self.su, self.sd = new("su", [P, KB]), new("sd", [P, FFN_TILES])
        self.cu, self.cd = new("cu", [P, 2 * INTER]), new("cd", [P, HID])
        self.t1 = new("t1", [P, 2, 512])
        self.sum = new("sum", [P, KB, 512])
        self.k2 = new("k2", [P, self.NB, KB, 512])
        self.d = [new("d", [P, FFN_TILES, HID]), self.dn]
        assert arena.off <= k.nc.sbuf_usable_end, arena.off

    def load(self, e):
        i = self.ins
        for dst, src in ((self.had[:], i["had"]), (self.ug[:], i["ffn_ug"]), (self.dn[:], i["ffn_dn"]),
                         (self.su[:], i["su_ug"]), (self.sd[:], i["su_dp"]),
                         (self.cu[:], i["c_ug"].partition_broadcast(P)),
                         (self.cd[:], i["c_dp"].partition_broadcast(P))):
            e.dma_start(dst, src).then_inc(self.s_load.sem, 16)

    def store(self, e):
        for n in range(self.NB):
            self.s_k.wait(e, 2 * n + 2)
            for kb in range(KB):
                at = ((n // 2) * KB + kb) * P
                e.dma_start(self.pack[4 * (n % 2):4 * (n % 2) + 4, :, at:at + P].rearrange("t p f -> p t f"),
                            self.k2[:, n, kb, :].rearrange("p (t f) -> p t f", f=P)).then_inc(self.s_out.sem, 16)
        self.s_d.wait(e, 7 + FFN_TILES)
        e.dma_start(self.pack[:, :, 2 * KB * P:].rearrange("t p f -> p t f"), self.d[1][:]).then_inc(self.s_out.sem, 16)
        e.wait_ge(self.s_out.sem, 16 * (KB * self.NB + 1))

    def tensor(self, e, n):
        if n == 0:
            e.wait_ge(self.s_load.sem, 16 * 7)
        if n < self.NB:
            if n >= 2:
                self.s_bf.wait(e, 2 * n - 2)
            for kb in range(KB):
                m = e.matmul(self.k.psum[:, 2 * (n % 2) + kb, :], self.had[:],
                             self.ug[:, kb, n * 512:(n + 1) * 512], start=True, stop=True)
            m @ self.s_mm
            return
        self.s_bf.wait(e, 2 * self.NB)
        for b in range(4):
            m = e.matmul(self.k.psum[:, b, :], self.had[:],
                         self.dn[:, 2 * b:2 * b + 2, :].rearrange("p a f -> p (a f)"), start=True, stop=True)
        m @ self.s_mm

    def scalar(self, e, n):
        self.s_mm.wait(e, n + 1)
        if n < self.NB:
            if n >= 2:
                self.s_bf.wait(e, 2 * n - 2)
            e.activation(self.t1[:, n % 2, :], self.k.psum[:, 2 * (n % 2) + 1, :], ACT.Copy) @ self.s_ev
            return
        e.activation(self.d[0][:].rearrange("p (a b) f -> p a (b f)", a=4), self.k.psum[:, 0:4, :],
                     ACT.Copy) @ self.s_ev

    def vector(self, e, n):
        if n == 0:
            e.wait_ge(self.s_load.sem, 16 * 7)
            e.tensor_scalar(self.su[:], self.su[:], self.UP, None, ALU.mult) @ self.s_su
            e.tensor_scalar(self.sd[:], self.sd[:], self.DOWN, None, ALU.mult) @ self.s_su
            self.s_su.wait(e, 2)
        self.s_ev.wait(e, n + 1)
        self.s_k.wait(e, 2 * n)
        for kb, op in enumerate((ALU.add, ALU.subtract)):
            e.tensor_tensor(self.sum[:, kb, :], self.k.psum[:, 2 * (n % 2), :], self.t1[:, n % 2, :],
                            op) @ self.s_bf
        for kb in range(KB):
            self.s_bf.wait(e, 2 * n + kb + 1)
            e.scalar_tensor_tensor(self.k2[:, n, kb, :], self.sum[:, kb, :], self.su[:, kb:kb + 1],
                                   self.cu[:, n * 512:(n + 1) * 512], ALU.mult, ALU.mult) @ self.s_k

    def pool(self, e):
        self.s_ev.wait(e, self.NB + 1)
        for stage, h in enumerate((1, 2, 4)):
            a, b = (x[:].rearrange("p (n two h) f -> p n two (h f)", two=2, h=h)
                    for x in (self.d[stage % 2], self.d[(stage + 1) % 2]))
            self.s_d.wait(e, 2 * stage)
            e.tensor_tensor(b[:, :, 0, :], a[:, :, 0, :], a[:, :, 1, :], ALU.add) @ self.s_d
            e.tensor_tensor(b[:, :, 1, :], a[:, :, 0, :], a[:, :, 1, :], ALU.subtract) @ self.s_d
        self.s_d.wait(e, 6)
        for t in range(FFN_TILES):
            e.tensor_scalar(self.d[1][:, t, :], self.d[1][:, t, :], self.sd[:, t:t + 1], None,
                            ALU.mult) @ self.s_d
        self.s_d.wait(e, 6 + FFN_TILES)
        e.tensor_tensor(self.d[1][:], self.d[1][:], self.cd[:].unsqueeze(1).broadcast_to([P, FFN_TILES, HID]),
                        ALU.mult) @ self.s_d


def program(nc, ins, out, stages=6):
    with ExitStack() as ctx:
        k = Kern(nc, ctx)
        x = ins["x"].rearrange("b s f -> (b s) f")
        tails = [Tail(k, "t0_", entry=True, route=True)]
        pack = nc.dram_tensor("ffn_pack", [FFN_TILES, P, SwiGLU.WCOLS], F32, kind="Internal").ap()
        parts = []
        for n in range(1, stages + 1):
            tails.append(Tail(k, f"t{n}_", last=(n == stages), route=(n == 2 and n < stages)))
            tails[n].out = out.rearrange("b s f -> (b s) f")
            if n in (1, 3):
                parts.append(SwiGLU(k, f"moe{n}_", MOE_TILES // MOE_G, MOE_G, ins["moe_pack"],
                                    ins["gate_rows"], tails[n - 1], tails[n]))
                if n == 1:
                    moe = parts[0]
                    prep = Prep(k, ins, pack, moe.end)
                    entry = Entry(k, x, tails[0], prep)
            if n == 2:
                parts.append(Scan(k, "scan_", ins, tails[n - 1], tails[n]))
            if n in (4, 6):
                parts.append(SwiGLU(k, f"ffn{n}_", 1, FFN_TILES, pack, None, tails[n - 1], tails[n]))
            if n == 5:
                parts.append(Attention(k, "attn_", ins, tails[n - 1], tails[n]))

            if n > 1:
                parts[-1].prev, parts[-2].next = parts[-2], parts[-1]
                parts[-1].next = None

        block = ctx.enter_context(nc.Block())

        @block.sync
        def _(e):
            for s in k.credits:
                e.sem_inc(s.sem, s.base)
            e.dma_start(k.ident[:], ins["ident"]).then_inc(k.s_const.sem, 16)
            e.dma_start(k.gw[:], ins["gate_w"]).then_inc(k.s_const.sem, 16)
            e.dma_start(k.fold[:], ins["add_parts"]).then_inc(k.s_const.sem, 16)
            entry.sync(e)
            prep.load(e)
            moe.first(e)
            prep.store(e)
            for p in parts[1:2]:
                p.load(e)
            for p in parts:
                p.sync(e)

        @block.gpsimd
        def _(e):
            e.memset(k.half[:], -0.5) @ k.s_half
            k.s_half.wait(e, 1)
            moe.zero(e)
            for p in [entry, prep] + parts:
                p.pool(e)

        @block.vector
        def _(e):
            e.memset(k.gate[0:32, :].bitcast(F32), 1.0) @ k.s_init
            e.memset(k.gate[32:64, :].bitcast(F32), 0.0) @ k.s_init
            e.wait_ge(k.s_const.sem, 48)
            e.tensor_copy(k.gwp[:, :, 0:NEXP], k.gw[:]) @ k.s_init
            k.s_init.wait(e, 3)
            e.tensor_tensor(k.gwp[:, :, NEXP:], k.gw[:], k.gwp[:, :, 0:NEXP].bitcast(F32),
                            ALU.subtract) @ k.s_init
            for p in [entry] + parts:
                p.vector(e)

        @block.scalar
        def _(e):
            k.s_init.wait(e, 4)
            for p in [entry] + parts:
                p.scalar(e)

        @block.tensor
        def _(e):
            e.wait_ge(k.s_const.sem, 48)
            k.s_init.wait(e, 4)
            for p in [entry] + parts:
                p.tensor(e)


def blocks(w, n=P):
    return w.reshape(-1, n, w.shape[-1]).transpose(1, 0, 2)


def layout(inputs):
    a = {n: np.asarray(v) for n, v in inputs.items()}
    f32 = np.float32
    out = {"x": a["L0_attn_x"], "ident": np.eye(P, dtype=f32)}
    out["add_parts"] = np.tile(np.eye(NEXP, dtype=f32), (2, 1))
    out["gate_w"] = blocks(a["L0_ffn_gate_w"].T)
    w13, sw13 = a["L0_ffn_w13"], a["L0_ffn_sw13"]
    full = MOE_TILES * P
    parts = []
    for half in range(2):
        w = np.zeros((full, HID), f32)
        w[:NEXP * EINT] = w13[:, half * EINT:(half + 1) * EINT, :].reshape(-1, HID)
        w[NEXP * EINT:FEAT] = sw13[half * 2 * EINT:(half + 1) * 2 * EINT]
        parts.append(w.reshape(MOE_TILES, P, KB, P).transpose(0, 3, 2, 1).reshape(MOE_TILES, P, KB * P))
    d = np.zeros((full, HID), f32)
    d[:NEXP * EINT] = a["L0_ffn_w2"].transpose(0, 2, 1).reshape(-1, HID)
    d[NEXP * EINT:FEAT] = a["L0_ffn_sw2"].T
    parts.append(d.reshape(MOE_TILES, P, HID))
    out["moe_pack"] = np.concatenate(parts, axis=2)
    rows = np.zeros((full, 64), f32)
    f = np.arange(FEAT)
    expert = np.minimum(f // EINT, ONES_ROW)
    rows[f, expert] = 1.0
    routed = f[:NEXP * EINT]
    rows[routed, 32 + expert[routed]] = 1.0
    out["gate_rows"] = rows.reshape(MOE_TILES, P, 64).transpose(0, 2, 1)
    out["W_in"] = blocks(a["L0_attn_W_in"].T).reshape(P, -1)
    out["Wx"] = blocks(a["L0_attn_Wx"].T).reshape(P, -1)
    out["Wdt"] = a["L0_attn_Wdt"].T
    out["Wout"] = blocks(a["L0_attn_Wout"].T).reshape(P, -1)
    out["conv_w"] = blocks(a["L0_attn_conv_w"])
    for name in ("conv_b", "dt_bias", "D"):
        out[name] = a["L0_attn_" + name].reshape(-1, P).T
    out["A"] = blocks(a["L0_attn_A"])
    out["dt_ln"] = a["L0_attn_dt_ln_w"].reshape(P, 1)
    out["bc_ln"] = np.concatenate([a["L0_attn_b_ln_w"], a["L0_attn_c_ln_w"]]).reshape(2 * NST, 1)
    out["mean_bc"] = np.kron(np.eye(2, dtype=f32), np.full((NST, NST), 1.0 / NST, f32))
    out["state_pick"] = np.tile(np.eye(2 * NST, dtype=f32), (2, 1))
    slot = (np.arange(HEADS)[:, None] * HSLOT + np.arange(HD)).ravel()
    pos = np.arange(HEADS) * HSLOT + HD
    for name in "qk":
        w = np.zeros((HID, HEADS * HSLOT), f32)
        w[:, slot] = a["L1_attn_W" + name]
        out["W" + name] = blocks(w).reshape(P, -1)
        b = np.zeros(HEADS * HSLOT, f32)
        b[slot] = a["L1_attn_b" + name]
        if name == "q":
            b[pos] = HD ** 0.5
        out["b" + name] = b.reshape(-1, P).T
    out["Wv"] = blocks(a["L1_attn_Wv"]).reshape(P, -1)
    w = np.zeros((HEADS * HSLOT, HID), f32)
    w[slot] = a["L1_attn_Wo"]
    out["Wo"] = blocks(w).reshape(P, -1)
    out["bv"] = a["L1_attn_bv"].reshape(-1, P).T
    out["bo"] = a["L1_attn_bo"].reshape(-1, P).T
    first = 2.0 ** (-2.0 ** -(np.log2(HEADS) - 3))
    slopes = np.array([first * first ** i for i in range(HEADS)], dtype=f32)
    pat = np.zeros((HEADS * HSLOT, SEQ), f32)
    pat[pos] = -slopes[:, None] * (SEQ - 1 - np.arange(SEQ, dtype=f32))[None, :]
    out["slopes"] = blocks(pat)
    out["mask"] = np.where(np.arange(P)[None, :] > np.arange(P)[:, None], MASKED, 0.0).astype(f32)
    had = np.ones((1, 1), f32)
    while had.shape[0] < P:
        had = np.block([[had, had], [had, -had]])
    out["had"] = had
    out["ffn_ug"] = blocks(np.concatenate([a["L1_ffn_W_gate"].T, a["L1_ffn_W_up"].T], axis=1))
    out["ffn_dn"] = blocks(a["L1_ffn_W_down"].T)
    out["su_ug"] = a["L1_ffn_SU_ug"].reshape(-1, P).T
    out["su_dp"] = a["L1_ffn_SU_dp"].reshape(-1, P).T
    out["c_ug"] = np.concatenate([a["L1_ffn_Wscale_ug"][INTER:], a["L1_ffn_Wscale_ug"][:INTER]])
    out["c_dp"] = a["L1_ffn_Wscale_dp"]
    return {n: np.ascontiguousarray(v, dtype=v.dtype) for n, v in out.items()}


def kernel(**inputs):
    import concourse.bacc as bacc
    from concourse.bass_utils import run_bass_kernel_spmd

    nc = bacc.Bacc("TRN2", target_bir_lowering=False, num_devices=1)
    arrays = layout(inputs)
    ins = {n: nc.dram_tensor(n, list(v.shape), mybir.dt.from_np(v.dtype), kind="ExternalInput").ap()
           for n, v in arrays.items()}
    out = nc.dram_tensor("out", [BATCH, SEQ, HID], F32, kind="ExternalOutput").ap()
    program(nc, ins, out)
    return run_bass_kernel_spmd(nc, [arrays], core_ids=[0]).results[0]["out"]
```
